# Optimizing a Trainium2 kernel written in Bass

```python
import numpy as np
import jax
import jax.numpy as jnp

def _softmax(x, axis=-1):
    return jax.nn.softmax(x, axis=axis)

def _gelu(x):
    return jax.nn.gelu(x, approximate=True)

def _silu(x):
    return jax.nn.silu(x)

def _sigmoid(x):
    return jax.nn.sigmoid(x)

def _layernorm(x, axis=-1, eps=1e-05):
    m = jnp.mean(x, axis=axis, keepdims=True)
    v = jnp.var(x, axis=axis, keepdims=True)
    return (x - m) / jnp.sqrt(v + eps)

def _scatter_add(tgt, idx, src, axis=0):
    return tgt.at[idx].add(src)

def _segment_sum(src, seg, n):
    return jax.ops.segment_sum(src, seg, n)
kernel_name = 'mk_gps_d1_gnn_r8_652204'

def setup_inputs(seed: int=0):
    np.random.seed(seed)
    _w = jnp.asarray

    def _rec_inputs():
        import jax
        import jax.numpy as jnp
        _gk = jax.random.key(seed)
        x = -0.0002117 + 1 * jax.random.normal(jax.random.fold_in(_gk, 1), (12500, 256), jnp.float32)
        src = jax.random.randint(jax.random.fold_in(_gk, 2), (200000,), 0, 12500, jnp.int32)
        dst = jnp.minimum((12500 * jax.random.uniform(jax.random.fold_in(_gk, 3), (200000,)) ** 2.0).astype(jnp.int32), 99999)
        _o = jnp.argsort(dst, stable=True)
        src = src[_o]
        dst = dst[_o]
        edge_weight = jax.random.uniform(jax.random.fold_in(_gk, 12), (200000,), jnp.float32, 0.0, 0.999999)
        return (x, src, dst, edge_weight)
    x, src, dst, edge_weight = _rec_inputs()

    def _L0_gnn_setup():
        import jax, jax.numpy as jnp
        import numpy as np
        N_NODES = 12500
        N_EDGES = 200000
        D = 256
        key = jax.random.key(seed)
        ks = jax.random.split(key, 8)
        h6_all = jax.random.normal(ks[0], (N_NODES, D), dtype=jnp.float32)
        edge_index = jax.random.randint(ks[1], (2, N_EDGES), 0, N_NODES, dtype=jnp.int64)
        edge_weight = jax.random.uniform(ks[2], (N_EDGES,), dtype=jnp.float32)
        s = 1.0 / np.sqrt(D)
        W = jax.random.normal(ks[3], (D, D), dtype=jnp.float32) * s
        b = jnp.zeros((D,), dtype=jnp.float32)
        W1 = jax.random.normal(ks[4], (D, D), dtype=jnp.float32) * s
        b1 = jnp.zeros((D,), dtype=jnp.float32)
        W2 = jax.random.normal(ks[5], (D, D), dtype=jnp.float32) * s
        b2 = jnp.zeros((D,), dtype=jnp.float32)
        return {'h6_all': h6_all, 'edge_index': edge_index, 'edge_weight': edge_weight, 'W': W, 'b': b, 'W1': W1, 'b1': b1, 'W2': W2, 'b2': b2}
    _L0_gnn_all = _L0_gnn_setup()
    _L0_gnn_in = {k: v for k, v in _L0_gnn_all.items() if k in ('W', 'b', 'W1', 'b1', 'W2', 'b2')}
    del _L0_gnn_all

    def _L0_mix_setup():
        import jax, jax.numpy as jnp
        import numpy as np
        MIDC = 256
        HEADS = 8
        HEADC = MIDC // HEADS
        EPS = 1e-05

        def _ln(x, gamma, beta):
            mu = jnp.mean(x, axis=-1, keepdims=True)
            var = jnp.var(x, axis=-1, keepdims=True)
            return (x - mu) * jax.lax.rsqrt(var + EPS) * gamma + beta
        key = jax.random.key(seed)
        ks = jax.random.split(key, 8)
        B, HW, C = (8, 512, MIDC)
        s = 1.0 / np.sqrt(C)
        return {'x': jax.random.normal(ks[0], (B, HW, C), jnp.float32), 'w_qkv': jax.random.normal(ks[1], (C, 3 * C), jnp.float32) * s, 'b_qkv': jnp.zeros((3 * C,), jnp.float32), 'kln_g': jnp.ones((HEADC,), jnp.float32), 'kln_b': jnp.zeros((HEADC,), jnp.float32), 'vln_g': jnp.ones((HEADC,), jnp.float32), 'vln_b': jnp.zeros((HEADC,), jnp.float32), 'w1': jax.random.normal(ks[2], (C, C), jnp.float32) * s, 'b1': jnp.zeros((C,), jnp.float32), 'w2': jax.random.normal(ks[3], (C, C), jnp.float32) * s, 'b2': jnp.zeros((C,), jnp.float32)}
    _L0_mix_all = _L0_mix_setup()
    _L0_mix_in = {k: v for k, v in _L0_mix_all.items() if k in ('w_qkv', 'b_qkv', 'kln_g', 'kln_b', 'vln_g', 'vln_b', 'w1', 'b1', 'w2', 'b2')}
    del _L0_mix_all

    def _L0_ffn_setup():
        import jax, jax.numpy as jnp
        import numpy as np
        E = 8
        K = 2
        D = 256
        H = 512
        DOUT = 256
        EPS = 1e-05
        key = jax.random.key(seed)
        ks = jax.random.split(key, 9)
        s = 0.02
        return {'x': jax.random.normal(ks[0], (4, 1024, D), jnp.float32), 'gamma': 1.0 + 0.05 * jax.random.normal(ks[1], (D,), jnp.float32), 'beta': 0.05 * jax.random.normal(ks[2], (D,), jnp.float32), 'Wr': 0.01 * jax.random.normal(ks[3], (D, E), jnp.float32), 'br': jnp.zeros((E,), jnp.float32), 'W1': s * jax.random.normal(ks[4], (E, D, H), jnp.float32), 'b1': s * jax.random.normal(ks[5], (E, H), jnp.float32), 'W2': s * jax.random.normal(ks[6], (E, H, DOUT), jnp.float32), 'b2': s * jax.random.normal(ks[7], (E, DOUT), jnp.float32)}
    _L0_ffn_all = _L0_ffn_setup()
    _L0_ffn_in = {k: v for k, v in _L0_ffn_all.items() if k in ('gamma', 'beta', 'Wr', 'br', 'W1', 'b1', 'W2', 'b2')}
    del _L0_ffn_all
    return {'x': x, 'src': src, 'dst': dst, 'edge_weight': edge_weight, 'L0_gnn_W': _L0_gnn_in['W'], 'L0_gnn_b': _L0_gnn_in['b'], 'L0_gnn_W1': _L0_gnn_in['W1'], 'L0_gnn_b1': _L0_gnn_in['b1'], 'L0_gnn_W2': _L0_gnn_in['W2'], 'L0_gnn_b2': _L0_gnn_in['b2'], 'L0_mix_w_qkv': _L0_mix_in['w_qkv'], 'L0_mix_b_qkv': _L0_mix_in['b_qkv'], 'L0_mix_kln_g': _L0_mix_in['kln_g'], 'L0_mix_kln_b': _L0_mix_in['kln_b'], 'L0_mix_vln_g': _L0_mix_in['vln_g'], 'L0_mix_vln_b': _L0_mix_in['vln_b'], 'L0_mix_w1': _L0_mix_in['w1'], 'L0_mix_b1': _L0_mix_in['b1'], 'L0_mix_w2': _L0_mix_in['w2'], 'L0_mix_b2': _L0_mix_in['b2'], 'L0_ffn_gamma': _L0_ffn_in['gamma'], 'L0_ffn_beta': _L0_ffn_in['beta'], 'L0_ffn_Wr': _L0_ffn_in['Wr'], 'L0_ffn_br': _L0_ffn_in['br'], 'L0_ffn_W1': _L0_ffn_in['W1'], 'L0_ffn_b1': _L0_ffn_in['b1'], 'L0_ffn_W2': _L0_ffn_in['W2'], 'L0_ffn_b2': _L0_ffn_in['b2']}

def reference(x, src, dst, edge_weight, L0_gnn_W, L0_gnn_b, L0_gnn_W1, L0_gnn_b1, L0_gnn_W2, L0_gnn_b2, L0_mix_w_qkv, L0_mix_b_qkv, L0_mix_kln_g, L0_mix_kln_b, L0_mix_vln_g, L0_mix_vln_b, L0_mix_w1, L0_mix_b1, L0_mix_w2, L0_mix_b2, L0_ffn_gamma, L0_ffn_beta, L0_ffn_Wr, L0_ffn_br, L0_ffn_W1, L0_ffn_b1, L0_ffn_W2, L0_ffn_b2):
    import jax
    import jax.numpy as jnp

    def _L0_gnn_ref(h6_all, edge_index, edge_weight, W, b, W1, b1, W2, b2):
        import jax, jax.numpy as jnp
        import numpy as np
        N_NODES = 12500
        N_EDGES = 200000
        D = 256
        'GCNConv(256->256, weighted, self-loops, symmetric norm) + 2-layer MLP head.'
        N = h6_all.shape[0]
        row, col = (edge_index[0], edge_index[1])
        sl = jnp.arange(N, dtype=edge_index.dtype)
        row_sl = jnp.concatenate([row, sl])
        col_sl = jnp.concatenate([col, sl])
        ew_sl = jnp.concatenate([edge_weight, jnp.ones((N,), dtype=edge_weight.dtype)])
        deg = jax.ops.segment_sum(ew_sl, row_sl, num_segments=N)
        dinv = jnp.where(deg > 0, jax.lax.rsqrt(deg), 0.0)
        norm = dinv[row_sl] * ew_sl * dinv[col_sl]
        xw = h6_all @ W
        msgs = xw[col_sl] * norm[:, None]
        h7 = jax.ops.segment_sum(msgs, row_sl, num_segments=N) + b
        h = jax.nn.relu(h7 @ W1 + b1)
        out = h @ W2 + b2
        return out

    def _L0_mix_ref(x, w_qkv, b_qkv, kln_g, kln_b, vln_g, vln_b, w1, b1, w2, b2):
        import jax, jax.numpy as jnp
        import numpy as np
        MIDC = 256
        HEADS = 8
        HEADC = MIDC // HEADS
        EPS = 1e-05

        def _ln(x, gamma, beta):
            mu = jnp.mean(x, axis=-1, keepdims=True)
            var = jnp.var(x, axis=-1, keepdims=True)
            return (x - mu) * jax.lax.rsqrt(var + EPS) * gamma + beta
        B, HW, C = x.shape
        bias = x
        qkv = (x @ w_qkv + b_qkv).reshape(B, HW, HEADS, 3 * HEADC)
        qkv = qkv.transpose(0, 2, 1, 3)
        q, k, v = jnp.split(qkv, 3, axis=-1)
        k = _ln(k, kln_g, kln_b)
        v = _ln(v, vln_g, vln_b)
        kv = jnp.einsum('bhnd,bhne->bhde', k, v) / HW
        out = jnp.einsum('bhnd,bhde->bhne', q, kv)
        out = out.transpose(0, 2, 1, 3).reshape(B, HW, C)
        ret = out + bias
        h = jax.nn.gelu(ret @ w1 + b1, approximate=False)
        return h @ w2 + b2 + bias

    def _L0_ffn_ref(x, gamma, beta, Wr, br, W1, b1, W2, b2):
        import jax, jax.numpy as jnp
        import numpy as np
        E = 8
        K = 2
        D = 256
        H = 512
        DOUT = 256
        EPS = 1e-05
        mu = jnp.mean(x, axis=-1, keepdims=True)
        var = jnp.mean(jnp.square(x - mu), axis=-1, keepdims=True)
        xn = (x - mu) * jax.lax.rsqrt(var + EPS) * gamma + beta
        logits = jnp.einsum('bsd,de->bse', xn, Wr) + br
        top_vals, top_idx = jax.lax.top_k(logits, K)
        w = jax.nn.softmax(top_vals, axis=-1)
        w_full = jnp.einsum('bsk,bske->bse', w, jax.nn.one_hot(top_idx, E, dtype=w.dtype))
        y = jnp.zeros(x.shape[:-1] + (DOUT,), x.dtype)
        for e in range(E):
            h = jax.nn.gelu(jnp.einsum('bsd,dh->bsh', xn, W1[e]) + b1[e], approximate=False)
            y_e = jnp.einsum('bsh,hd->bsd', h, W2[e]) + b2[e]
            y = y + y_e * w_full[..., e, None]
        return y
    edge_index = jnp.stack([src, dst])
    xn = _layernorm(x, axis=-1)
    x = x + _L0_gnn_ref(xn, edge_index, edge_weight, L0_gnn_W, L0_gnn_b, L0_gnn_W1, L0_gnn_b1, L0_gnn_W2, L0_gnn_b2) + _L0_mix_ref(xn[None], L0_mix_w_qkv, L0_mix_b_qkv, L0_mix_kln_g, L0_mix_kln_b, L0_mix_vln_g, L0_mix_vln_b, L0_mix_w1, L0_mix_b1, L0_mix_w2, L0_mix_b2)[0]
    x = x + _L0_ffn_ref(_layernorm(x, axis=-1)[None], L0_ffn_gamma, L0_ffn_beta, L0_ffn_Wr, L0_ffn_br, L0_ffn_W1, L0_ffn_b1, L0_ffn_W2, L0_ffn_b2)[0]
    return x

_drawn_inputs = setup_inputs


def setup_inputs(seed=0):
    import zlib

    import numpy as np

    out = dict(_drawn_inputs(seed))
    spreads = {'L0_gnn_b': (0.0, 0.1),
     'L0_gnn_b1': (0.0, 0.1),
     'L0_gnn_b2': (0.0, 0.1),
     'L0_mix_b_qkv': (0.0, 0.1),
     'L0_mix_kln_g': (1.0, 0.6),
     'L0_mix_kln_b': (0.0, 0.438),
     'L0_mix_vln_g': (1.0, 0.594),
     'L0_mix_vln_b': (0.0, 0.395),
     'L0_mix_b1': (0.0, 0.1),
     'L0_mix_b2': (0.0, 0.1),
     'L0_ffn_br': (0.0, 0.303)}
    factors = {'L0_ffn_gamma': 8.0,
     'L0_ffn_beta': 8.0,
     'L0_ffn_Wr': 3.168,
     'L0_ffn_b1': 23.436,
     'L0_ffn_b2': 8.0}
    for name, (base, spread) in spreads.items():
        noise = np.random.default_rng([zlib.crc32(name.encode()), seed]).standard_normal(out[name].shape)
        drawn = base * np.exp(spread * noise) if base else spread * noise
        out[name] = jnp.asarray(drawn.astype(out[name].dtype))
    for name, factor in factors.items():
        out[name] = (out[name] * factor).astype(out[name].dtype)
    return out
```

```python
from contextlib import ExitStack

import concourse.bass as bass
from concourse import mybir

P = 128
N_NODES, D, N_EDGES = 12500, 256, 200000
HEADS, HEADC = 8, 32
N_EXPERTS, HIDDEN = 8, 512
EPS = 1e-5
DC = D // P
HC = HIDDEN // P
BLOCKS = -(-N_NODES // P)
assert BLOCKS % 2 == 0
NODES = BLOCKS * P
PAIRS = BLOCKS // 2
COLS = 16
EDGE_COLS = BLOCKS * COLS
assert EDGE_COLS * P >= N_EDGES
STEP_TILES = 16
STEPS = 104
TILES = STEPS * STEP_TILES
assert TILES >= N_EDGES // P + BLOCKS
SLOTS = COLS + 1
DST_BITS = 14
assert NODES <= 1 << DST_BITS
RING = 4
assert STEPS <= P and STEPS % 2 == 0 and STEPS >= BLOCKS and STEP_TILES % (2 * RING) == 0
HEADS_PER_CHUNK = P // HEADC
AHEAD = 2
TOP = 2
X_UNROLL = 4
X_TILES = -(-(BLOCKS * TOP + N_EXPERTS - 1) // X_UNROLL) * X_UNROLL
X_TRIPS = X_TILES // X_UNROLL
UP = DC * HIDDEN + HC
DOWN = HC * D + D
CHUNK = 7
CHUNKS = BLOCKS // CHUNK
assert CHUNKS * CHUNK == BLOCKS and CHUNKS % 2 == 0

F32, I32, BF16 = mybir.dt.float32, mybir.dt.int32, mybir.dt.bfloat16
ALU = mybir.AluOpType
ACT = mybir.ActivationFunctionType
AX = mybir.AxisListType


def start_after(eng, sem, count):
    if not isinstance(count, int) or count > 0:
        eng.wait_ge(sem, count)


class Shared:
    pass


def gps_layer(nc, A, out):
    with ExitStack() as whole:
        k = Shared()
        k.nc, k.A, k.out = nc, A, out

        k.sems = []

        def sem(name):
            k.sems.append(nc.alloc_semaphore(name=name))
            return k.sems[-1]

        def phase_done():
            nc.clear_and_free_semaphores(k.sems)
            nc.all_engine_barrier()
            k.sems = []

        k.sem, k.phase_done = sem, phase_done
        k.sb = lambda name, shape, dt=F32, ctx=whole: ctx.enter_context(nc.sbuf_tensor(name, shape, dt))
        k.ps = lambda name, shape, ctx: ctx.enter_context(nc.psum_tensor(name, shape, F32))

        k.records = nc.dram_tensor("records", [P * TILES, 2], I32).ap()
        k.words_dram = nc.dram_tensor("words_dram", [STEPS, 1], I32).ap()
        k.xn_dram = nc.dram_tensor("xn_dram", [NODES + AHEAD * P, D], F32).ap()
        k.table = nc.dram_tensor("table", [NODES, D], F32).ap()
        k.part_dram = nc.dram_tensor("part_dram", [NODES + AHEAD * P, D], F32).ap()
        k.ffn_rows = nc.dram_tensor("ffn_rows", [NODES, D], F32).ap()
        k.y_rows = nc.dram_tensor("y_rows", [P * X_TILES, D], F32).ap()

        k.iota_row = k.sb("iota_row", [P, P])
        k.ident = k.sb("ident", [P, P])
        k.ones = k.sb("ones", [P, P])
        k.eps = k.sb("eps", [P, 1])
        k.arena = k.sb("arena", [P, 7 * DC * D])
        parts = iter(range(0, 7 * DC * D, DC * D))
        wide = lambda: k.arena[:, bass.ds(next(parts), DC * D)].rearrange("p (c n) -> p c n", c=DC)
        k.gcn_w = wide()
        k.gcn_w2 = wide()
        k.mix_w = wide()
        k.mix_w2 = wide()
        k.mix_w1 = wide()
        k.wqT = wide()
        biases = wide()
        k.bias_sum, k.bias_tmp = biases[:, 0, :], biases[:, 1, :]
        k.gcn_c = k.sb("gcn_c", [P, DC])
        k.mix_c = k.sb("mix_c", [P, DC])
        k.bq = k.sb("bq", [P, DC])
        k.mix_b1 = k.sb("mix_b1", [P, DC])
        k.kv_gb = k.sb("kv_gb", [P, 2])
        k.k_gb = k.sb("k_gb", [P, 2, HEADC])
        k.dinv = k.sb("dinv", [P, BLOCKS])
        k.words = k.sb("words", [1, STEPS], I32)

        with ExitStack() as sums:
            k.vsum = k.sb("vsum", [P, DC], F32, sums)
            k.deg = k.dinv
            k.vk, k.ksum = (k.mix_w[:, j, :].rearrange("p (c n) -> p c n", c=DC) for j in range(2))
            with ExitStack() as ctx:
                sort_phases(k, ctx)
            node_phases(k, sums)


def sort_phases(k, ctx):
    nc, A = k.nc, k.A
    sb = lambda name, shape, dt=F32: k.sb(name, shape, dt, ctx)
    s = Shared()
    s.src = sb("src", [P, EDGE_COLS], I32)
    s.dst = sb("dst", [P, EDGE_COLS], I32)
    s.ew = sb("ew", [P, EDGE_COLS])
    s.block_i = sb("block_i", [P, EDGE_COLS], I32)
    s.local_i = sb("local_i", [P, EDGE_COLS], I32)
    s.block_f = sb("block_f", [P, EDGE_COLS])
    s.local_f = sb("local_f", [P, EDGE_COLS])
    s.wkv = sb("wkv", [P, DC, 2 * D])
    s.bkv = sb("bkv", [1, 2 * D])
    s.valid = sb("valid", [P, BLOCKS])
    s.keep = sb("keep", [P, BLOCKS, SLOTS])
    s.onehot = sb("onehot", [P, 2, BLOCKS, SLOTS])
    s.count = sb("count", [P, 2, BLOCKS, SLOTS])
    setup(k, s)
    k.phase_done()
    sort_and_kv(k, s)
    k.phase_done()


def setup(k, s):
    nc, A = k.nc, k.A
    with ExitStack() as ctx:
        sb = lambda name, shape, dt=F32: k.sb(name, shape, dt, ctx)
        gcn_W = sb("gcn_W", [P, DC, D])
        gcn_W1 = sb("gcn_W1", [P, DC, D])
        gcn_b = sb("gcn_b", [P, DC])
        gcn_b1 = sb("gcn_b1", [P, DC])
        wqkv = sb("wqkv", [P, DC, 3 * D])
        bqkv = sb("bqkv", [1, 3 * D])
        wq = sb("wq", [P, DC, D])
        gcn_WT = sb("gcn_WT", [P, DC, D])
        kv_mean = sb("kv_mean", [P, DC, 2, HEADS])
        b_mean = sb("b_mean", [1, 2, HEADS])
        tri = sb("tri", [P, P])
        iota_i = sb("iota_i", [P, P], I32)
        block_b = sb("block_b", [P, EDGE_COLS], BF16)
        hits = sb("hits", [P, 2, EDGE_COLS], BF16)
        cnt = sb("cnt", [P, BLOCKS])
        zero = sb("zero", [P, TILES * 2], I32)
        total_i = sb("total_i", [P, BLOCKS], I32)
        tiles_i = sb("tiles_i", [P, BLOCKS], I32)
        tiles_f = sb("tiles_f", [P, BLOCKS])
        tile_end = sb("tile_end", [P, BLOCKS])
        tile_start = sb("tile_start", [P, BLOCKS])
        step_tile_i = sb("step_tile_i", [P, STEP_TILES], I32)
        step_tile = sb("step_tile", [P, STEP_TILES])
        step_hits = sb("step_hits", [P, 2, BLOCKS])
        begun = sb("begun", [P, STEP_TILES])
        grows = sb("grows", [P, STEP_TILES])
        pow2 = sb("pow2", [P, STEP_TILES])
        word_f = sb("word_f", [P, 1])
        word_i = sb("word_i", [P, 1], I32)
        psW = k.ps("psW", [P, 2, 512], ctx)
        psO = k.ps("psO", [P, 512], ctx)
        psC = k.ps("psC", [P, 512], ctx)

        src_in, ew_in, small_in, big_in = (k.sem(n) for n in ("src_in", "ew_in", "small_in", "big_in"))
        iota_made, consts_made, diag_made = k.sem("iota_made"), k.sem("consts_made"), k.sem("diag_made")
        zero_made, zeroed = k.sem("zero_made"), k.sem("zeroed")
        split_done, hist_done, offs = k.sem("split_done"), k.sem("hist_done"), k.sem("offs")
        prefix_done, wT_ready, wT_copied = k.sem("prefix_done"), k.sem("wT_ready"), k.sem("wT_copied")
        folded, fold_copied, wq_ready = k.sem("folded"), k.sem("fold_copied"), k.sem("wq_ready")
        centred, words_ready = k.sem("centred"), k.sem("words_ready")
        words_out, words_in = k.sem("words_out"), k.sem("words_in")

        rows = lambda w: w.rearrange("(c p) n -> p c n", p=P)
        col = lambda b: b.rearrange("(c p) -> p c", p=P)
        heads_q = A["b_qkv"].rearrange("(h t e) -> h t e", t=3, e=HEADC)

        with nc.Block() as block:
            @block.sync
            def _(sp):
                sp.dma_start(s.src[:, :], A["src"]).then_inc(src_in, 16)
                sp.dma_start(s.dst[:, :], A["dst"]).then_inc(ew_in, 16)
                sp.dma_start(s.ew[:, :], A["ew"]).then_inc(ew_in, 16)
                for dst, w in ((gcn_W, A["gnn_W"]), (gcn_W1, A["gnn_W1"]), (wqkv, A["w_qkv"]), (k.gcn_w2, A["gnn_W2"]),
                               (k.mix_w1, A["mix_w1"]), (k.mix_w2, A["mix_w2"])):
                    sp.dma_start(dst[:, :, :], rows(w)).then_inc(big_in, 16)
                sp.wait_ge(zero_made, 1)
                sp.dma_start(k.records.rearrange("(p t) w -> p (t w)", p=P), zero[:, :]).then_inc(zeroed, 16)
                pad = zero[:, 0:AHEAD * D].bitcast(F32).rearrange("p (t d) -> p t d", d=D)
                for behind in (k.xn_dram, k.part_dram):
                    sp.dma_start(behind[NODES:, :].rearrange("(t p) d -> p t d", p=P), pad).then_inc(zeroed, 16)
                sp.wait_ge(words_ready, 1)
                sp.dma_start(k.words_dram, word_i[0:STEPS, :]).then_inc(words_out, 16)
                sp.wait_ge(words_out, 16)
                sp.dma_start(k.words[:, :], k.words_dram.rearrange("b o -> o b")).then_inc(words_in, 16)
                sp.wait_ge(words_in, 16)
                sp.wait_ge(zeroed, 48)

            @block.scalar
            def _(act):
                with nc.allow_non_contiguous_dma(reason="columns of a few hundred words"):
                    for dst, b in ((gcn_b, A["gnn_b"]), (gcn_b1, A["gnn_b1"]), (k.mix_b1, A["mix_b1"])):
                        act.dma_start(dst[:, :], col(b)).then_inc(small_in, 16)
                    act.dma_start(bqkv[:, :], A["b_qkv"].rearrange("(a n) -> a n", a=1)).then_inc(small_in, 16)
                    act.dma_start(k.bias_sum, A["gnn_b2"].partition_broadcast(P)).then_inc(small_in, 16)
                    act.dma_start(k.bias_tmp, A["mix_b2"].partition_broadcast(P)).then_inc(small_in, 16)
                    act.dma_start(k.k_gb[:, 0, :], A["kln_g"].partition_broadcast(P)).then_inc(small_in, 16)
                    act.dma_start(k.k_gb[:, 1, :], A["kln_b"].partition_broadcast(P)).then_inc(small_in, 16)
                    for j, v in enumerate((A["vln_g"], A["vln_b"])):
                        for h in range(HEADS_PER_CHUNK):
                            act.dma_start(k.kv_gb[h * HEADC:(h + 1) * HEADC, j:j + 1],
                                          v.rearrange("(e o) -> e o", o=1)).then_inc(small_in, 16)
                    for c in range(DC):
                        for h in range(HEADS_PER_CHUNK):
                            act.dma_start(k.bq[h * HEADC:(h + 1) * HEADC, c:c + 1],
                                          heads_q[c * HEADS_PER_CHUNK + h, 0:1, :].rearrange("o e -> e o")
                                          ).then_inc(small_in, 16)
                for w, dst in enumerate((gcn_WT, k.wqT)):
                    act.wait_ge(wT_ready, w + 1)
                    act.activation(dst[:, :, :], psW[:, :, 0:D], ACT.Copy).then_inc(wT_copied, 1)
                act.wait_ge(folded, 1)
                act.activation(k.gcn_w[:, :, :], psO[:, :].rearrange("p (c n) -> p c n", c=DC),
                               ACT.Copy).then_inc(fold_copied, 1)

            @block.gpsimd
            def _(pool):
                pool.iota(iota_i[:, :], pattern=[[1, P]], base=0, channel_multiplier=0).then_inc(iota_made, 1)
                pool.iota(step_tile_i[:, :], pattern=[[1, STEP_TILES]], base=0,
                          channel_multiplier=STEP_TILES).then_inc(iota_made, 1)
                pool.memset(zero[:, :], 0).then_inc(zero_made, 1)
                pool.memset(k.ones[:, :], 1.0).then_inc(consts_made, 1)
                pool.memset(k.ident[:, :], 0.0).then_inc(consts_made, 1)
                pool.memset(tri[:, :], 1.0).then_inc(consts_made, 1)
                pool.memset(s.valid[:, :], 1.0).then_inc(consts_made, 1)
                pool.memset(k.eps[:, :], EPS).then_inc(consts_made, 1)
                pool.memset(s.keep[:, :, 1:], 1.0).then_inc(consts_made, 1)
                pool.memset(s.keep[:, :, 0:1], 0.0).then_inc(consts_made, 1)
                pool.wait_ge(consts_made, 7)
                pool.affine_select(out=k.ident[:, :], in_=k.ident[:, :], compare_op=ALU.not_equal, fill=1.0,
                                   base=0, pattern=[[-1, P]], channel_multiplier=1).then_inc(diag_made, 1)
                pool.affine_select(out=tri[:, :], in_=tri[:, :], compare_op=ALU.is_gt, fill=0.0,
                                   base=0, pattern=[[1, P]], channel_multiplier=-1).then_inc(diag_made, 1)
                pool.affine_select(out=s.valid[:, :], in_=s.valid[:, :], compare_op=ALU.is_ge, fill=0.0,
                                   base=N_NODES - 1, pattern=[[-P, BLOCKS]],
                                   channel_multiplier=-1).then_inc(diag_made, 1)

            @block.vector
            def _(dve):
                dve.wait_ge(iota_made, 2)
                dve.tensor_copy(k.iota_row[:, :], iota_i[:, :]).then_inc(split_done, 1)
                dve.tensor_copy(step_tile[:, :], step_tile_i[:, :]).then_inc(split_done, 1)
                dve.wait_ge(src_in, 16)
                dve.tensor_scalar(s.block_i[:, :], s.src[:, :], 7, None, ALU.arith_shift_right).then_inc(split_done, 1)
                dve.tensor_scalar(s.local_i[:, :], s.src[:, :], P - 1, None, ALU.bitwise_and).then_inc(split_done, 1)
                dve.wait_ge(split_done, 4)
                dve.tensor_copy(s.block_f[:, :], s.block_i[:, :]).then_inc(split_done, 1)
                dve.tensor_copy(block_b[:, :], s.block_i[:, :]).then_inc(split_done, 1)
                dve.tensor_copy(s.local_f[:, :], s.local_i[:, :]).then_inc(split_done, 1)
                dve.wait_ge(split_done, 7)
                dve.tensor_scalar(s.src[:, :], s.local_i[:, :], DST_BITS, None,
                                  ALU.logical_shift_left).then_inc(split_done, 1)
                dve.wait_ge(split_done, 8)
                dve.wait_ge(ew_in, 32)
                dve.tensor_tensor(s.dst[:, :], s.src[:, :], s.dst[:, :], ALU.bitwise_or).then_inc(split_done, 1)
                dve.wait_ge(split_done, 9)
                with dve.Fori(0, PAIRS) as i:
                    for u in range(2):
                        dve.wait_ge(hist_done, 2 * i + u)
                        dve.tensor_scalar(hits[:, u, :], block_b[:, :], k.iota_row[:, bass.ds(2 * i + u, 1)], 0.0,
                                          ALU.is_equal, ALU.add,
                                          accum_out=cnt[:, bass.ds(2 * i + u, 1)]).then_inc(hist_done, 1)
                dve.wait_ge(big_in, 6 * 16)
                dve.wait_ge(small_in, 16 * N_SMALL_DMAS)
                view = wqkv[:, :, :].rearrange("p c (h t e) -> p c t h e", t=3, e=HEADC)
                for c in range(DC):
                    dve.tensor_copy(wq[:, c, :].rearrange("p (h e) -> p h e", e=HEADC),
                                    view[:, c, 0, :, :]).then_inc(wq_ready, 1)
                for c in range(DC):
                    for t in range(2):
                        dve.tensor_reduce(kv_mean[:, c, t, :], view[:, c, 1 + t, :, :], AX.X, ALU.add).then_inc(centred, 1)
                bview = bqkv[:, :].rearrange("p (h t e) -> p t h e", t=3, e=HEADC)
                for t in range(2):
                    dve.tensor_reduce(b_mean[:, t, :], bview[:, 1 + t, :, :], AX.X, ALU.add).then_inc(centred, 1)
                dve.wait_ge(centred, 2 * DC + 2)
                for c in range(DC):
                    for t in range(2):
                        dve.scalar_tensor_tensor(
                            out=s.wkv[:, c, t * D:(t + 1) * D].rearrange("p (h e) -> p h e", e=HEADC),
                            in0=kv_mean[:, c, t, :].unsqueeze(2).to_broadcast([P, HEADS, HEADC]), scalar=-1.0 / HEADC,
                            in1=view[:, c, 1 + t, :, :], op0=ALU.mult, op1=ALU.add).then_inc(centred, 1)
                for t in range(2):
                    dve.scalar_tensor_tensor(
                        out=s.bkv[:, t * D:(t + 1) * D].rearrange("p (h e) -> p h e", e=HEADC),
                        in0=b_mean[:, t, :].unsqueeze(2).to_broadcast([1, HEADS, HEADC]), scalar=-1.0 / HEADC,
                        in1=bview[:, 1 + t, :, :], op0=ALU.mult, op1=ALU.add).then_inc(centred, 1)
                dve.tensor_tensor(k.bias_sum, k.bias_sum, k.bias_tmp, ALU.add).then_inc(centred, 1)
                dve.wait_ge(folded, 2)
                dve.tensor_tensor(k.gcn_c[:, :], psC[:, 256:256 + DC], gcn_b1[:, :], ALU.add).then_inc(fold_copied, 1)
                dve.wait_ge(prefix_done, 1)
                dve.tensor_scalar(total_i[:, :], psC[:, 128:128 + BLOCKS], float(P - 1), None, ALU.add).then_inc(offs, 1)
                dve.wait_ge(offs, 1)
                dve.tensor_scalar(tiles_i[:, :], total_i[:, :], 7, None, ALU.arith_shift_right).then_inc(offs, 1)
                dve.wait_ge(offs, 2)
                dve.tensor_scalar(tiles_f[:, :], tiles_i[:, :], 1.0, None, ALU.max).then_inc(offs, 1)
                dve.wait_ge(offs, 3)
                dve.tensor_tensor_scan(tile_end[:, :], k.ones[:, 0:BLOCKS], tiles_f[:, :], 0.0,
                                       ALU.mult, ALU.add).then_inc(offs, 1)
                dve.wait_ge(offs, 4)
                dve.tensor_tensor(tile_start[:, :], tile_end[:, :], tiles_f[:, :], ALU.subtract).then_inc(offs, 1)
                dve.wait_ge(offs, 5)
                dve.scalar_tensor_tensor(out=s.count[:, 1, :, SLOTS - 1], in0=tile_start[:, :], scalar=float(P),
                                         in1=psC[:, 0:BLOCKS], op0=ALU.mult, op1=ALU.add).then_inc(offs, 1)
                for t in range(STEP_TILES):
                    if t >= 2:
                        dve.wait_ge(offs, 6 + t - 1)
                    dve.tensor_scalar(step_hits[:, t % 2, :], tile_start[:, :], step_tile[:, t:t + 1], 0.0, ALU.is_le,
                                      ALU.add, accum_out=begun[:, t:t + 1]).then_inc(offs, 1)
                for t in range(1, STEP_TILES):
                    dve.memset(pow2[:, t:t + 1], float(1 << (t - 1))).then_inc(offs, 1)
                dve.memset(pow2[:, 0:1], float(1 << STEP_TILES)).then_inc(offs, 1)
                n = 6 + 2 * STEP_TILES
                dve.wait_ge(offs, n)
                dve.tensor_tensor(grows[:, 1:], begun[:, 1:], begun[:, 0:STEP_TILES - 1], ALU.subtract).then_inc(offs, 1)
                dve.tensor_scalar(grows[:, 0:1], begun[:, 0:1], -1.0, None, ALU.add).then_inc(offs, 1)
                dve.wait_ge(offs, n + 2)
                dve.tensor_tensor(begun[:, :], grows[:, :], pow2[:, :], ALU.mult).then_inc(offs, 1)
                dve.wait_ge(offs, n + 3)
                dve.tensor_reduce(word_f[:, :], begun[:, :], AX.X, ALU.add).then_inc(offs, 1)
                dve.wait_ge(offs, n + 4)
                dve.tensor_copy(word_i[:, :], word_f[:, :]).then_inc(words_ready, 1)

            @block.tensor
            def _(pe):
                pe.wait_ge(diag_made, 3)
                pe.wait_ge(big_in, 6 * 16)
                pe.wait_ge(small_in, 16 * N_SMALL_DMAS)
                for j in range(DC):
                    for c in range(DC):
                        last = pe.transpose(psW[:, j, c * P:(c + 1) * P], gcn_W[:, c, j * P:(j + 1) * P], k.ident[:, :])
                last.then_inc(wT_ready, 1)
                pe.wait_ge(wT_copied, 1)
                for c in range(DC):
                    for j in range(DC):
                        last = pe.matmul(psO[:, c * D:(c + 1) * D], gcn_WT[:, j, c * P:(c + 1) * P], gcn_W1[:, j, :],
                                         start=(j == 0), stop=(j == DC - 1))
                last.then_inc(folded, 1)
                for f in range(DC):
                    for j in range(DC):
                        last = pe.matmul(psC[:, 256 + f:257 + f], gcn_W1[:, j, f * P:(f + 1) * P], gcn_b[:, j:j + 1],
                                         start=(j == 0), stop=(j == DC - 1))
                last.then_inc(folded, 1)
                pe.wait_ge(wq_ready, DC)
                for j in range(DC):
                    for c in range(DC):
                        last = pe.transpose(psW[:, j, c * P:(c + 1) * P], wq[:, c, j * P:(j + 1) * P], k.ident[:, :])
                last.then_inc(wT_ready, 1)
                pe.wait_ge(hist_done, BLOCKS)
                pe.wait_ge(fold_copied, 2)
                pe.matmul(psC[:, 0:BLOCKS], tri[:, :], cnt[:, :], start=True, stop=True)
                pe.matmul(psC[:, 128:128 + BLOCKS], k.ones[:, :], cnt[:, :], start=True, stop=True).then_inc(prefix_done, 1)


N_SMALL_DMAS = 3 + 1 + 2 + 2 + 2 * HEADS_PER_CHUNK + DC * HEADS_PER_CHUNK


def sort_and_kv(k, s):
    nc, A = k.nc, k.A
    ctx = ExitStack()
    with ctx:
        sb = lambda name, shape, dt=F32: k.sb(name, shape, dt, ctx)
        x = sb("x", [P, 2, D])
        xn = sb("xn", [P, 2, D])
        xT = sb("xT", [P, DC, P])
        stats = sb("stats", [P, 2, 6])
        mv = sb("mv", [P, 2, 2])
        std = sb("std", [P, 2])
        rstd = sb("rstd", [P, 2])
        picked = sb("picked", [P, BLOCKS, COLS])
        rank = sb("rank", [P, COLS])
        pos = sb("pos", [P, COLS], I32)
        lane = sb("lane", [P, COLS], I32)
        tile = sb("tile", [P, COLS], I32)
        addr = sb("addr", [P, 2, COLS], I32)
        rec = sb("rec", [P, 2, COLS, 2], I32)
        local = sb("local", [P, COLS, P])
        sq = sb("sq", [P, 2 * D])
        ss = sb("ss", [P, 2 * HEADS])
        sd = sb("sd", [P, 2 * HEADS])
        rs = sb("rs", [P, 2 * HEADS])
        rsv = sb("rsv", [P, 2 * HEADS])
        kv = sb("kv", [P, 2 * D])
        zeros = sb("zeros", [P, 512])
        ps_xT = k.ps("ps_xT", [P, 512], ctx)
        ps_kv = k.ps("ps_kv", [P, 512], ctx)
        ps_deg = k.ps("ps_deg", [P, 512], ctx)
        ps_sum = k.ps("ps_sum", [P, 512], ctx)
        DEG = ps_deg[:, 0:BLOCKS]
        VSUM = ps_deg[:, 128:128 + DC]
        VK = ps_sum[:, 0:D]
        KSUM = ps_sum[:, D:2 * D]

        x_in = [k.sem(f"x_in{h}") for h in range(2)]
        xn_out = [k.sem(f"xn_out{h}") for h in range(2)]
        scattered = [k.sem(f"scattered{h}") for h in range(2)]
        (zeros_made, stats_done, mv_done, std_done, rstd_done, xn_done, slot0_done, onehot_done, count_done,
         picked_done, rank_done, pos_done, split2_done, addr_done, rec_done, local_done, deg_done, xT_done,
         xT_copied, kv_done, sq_done, ss_done, sd_done, rs_done, rsv_done, kvn_done, sums_done, all_summed,
         sums_out, pool_held) = (
            k.sem(name) for name in ("zeros_made stats_done mv_done std_done rstd_done xn_done slot0_done onehot_done count_done "
            "picked_done rank_done pos_done split2_done addr_done rec_done local_done deg_done xT_done "
            "xT_copied kv_done sq_done ss_done sd_done rs_done rsv_done kvn_done sums_done all_summed sums_out "
            "pool_held").split())
        DEG_CREDIT = 1

        def is_first(n):
            return isinstance(n, int) and n == 0

        def steps(eng, step):
            for h in range(2):
                step(h, h, 0)
            with eng.Fori(1, PAIRS) as i:
                for h in range(2):
                    step(2 * i + h, h, i)

        x_blocks = A["x"].rearrange("(t p) d -> p t d", p=P)
        xn_blocks = k.xn_dram.rearrange("(t p) d -> p t d", p=P)

        with nc.Block() as block:
            @block.sync
            def _(sp):
                for h in range(AHEAD):
                    sp.dma_start(x[:, h, :], x_blocks[:, h, :]).then_inc(x_in[h], 16)
                with sp.Fori(0, PAIRS) as i:
                    for h in range(2):
                        n = 2 * i + h
                        sp.wait_ge(xn_done, n + 1)
                        sp.dma_start(xn_blocks[:, bass.ds(n, 1), :], xn[:, h:h + 1, :]).then_inc(xn_out[h], 16)
                        sp.dma_start(x[:, h:h + 1, :], x_blocks[:, bass.ds(n + AHEAD, 1), :]).then_inc(x_in[h], 16)
                for h in range(2):
                    sp.wait_ge(x_in[h], 16 * (PAIRS + 1))
                for h in range(2):
                    sp.wait_ge(xn_out[h], 16 * PAIRS)

            @block.gpsimd
            def _(pool):
                with pool.Fori(0, PAIRS) as i:
                    for h in range(2):
                        pool.wait_ge(addr_done, 2 * i + h + 1)
                        pool.wait_ge(rec_done, 2 * (2 * i + h) + 2)
                        pool.sem_inc(pool_held, 1)
                        for c in range(COLS):
                            pool.indirect_dma_start(
                                out=k.records, out_offset=bass.IndirectOffsetOnAxis(addr[:, h, c:c + 1], 0),
                                in_=rec[:, h, c, :], in_offset=None, bounds_check=P * TILES - 1,
                                oob_is_err=False).then_inc(scattered[h], 16)
                for h in range(2):
                    pool.wait_ge(scattered[h], 16 * COLS * PAIRS)

            @block.scalar
            def _(act):
                def deviations(n):
                    act.wait_ge(ss_done, n + 1)
                    start_after(act, rs_done, n)
                    act.activation(sd[:, :], ss[:, :], ACT.Sqrt, bias=k.eps[:, :], scale=1.0 / HEADC).then_inc(sd_done, 1)

                def step(n, h, i):
                    act.wait_ge(mv_done, n + 1)
                    act.activation(std[:, h:h + 1], mv[:, h, 1:2], ACT.Sqrt, bias=k.eps[:, :]).then_inc(std_done, 1)
                    if not is_first(n):
                        deviations(n - 1)
                    act.wait_ge(xT_done, n + 1)
                    start_after(act, kv_done, n)
                    act.activation(xT[:, :, :], ps_xT[:, 0:D].rearrange("p (c n) -> p c n", c=DC),
                                   ACT.Identity).then_inc(xT_copied, 1)
                    act.wait_ge(kv_done, n + 1)
                    start_after(act, ss_done, n)
                    act.activation(sq[:, :], ps_kv[:, :], ACT.Square).then_inc(sq_done, 1)

                steps(act, step)
                deviations(BLOCKS - 1)
                act.wait_ge(all_summed, 1)
                act.activation(k.deg[:, :], DEG, ACT.Identity).then_inc(sums_out, 1)
                act.activation(k.vsum[:, :], VSUM, ACT.Identity).then_inc(sums_out, 1)
                act.activation(k.vk, VK.rearrange("p (c n) -> p c n", c=DC), ACT.Identity).then_inc(sums_out, 1)
                act.activation(k.ksum, KSUM.rearrange("p (c n) -> p c n", c=DC), ACT.Identity).then_inc(sums_out, 1)

            @block.vector
            def _(dve):
                dve.memset(zeros[:, :], 0.0).then_inc(zeros_made, 1)

                def squares(n):
                    dve.wait_ge(sq_done, n + 1)
                    start_after(dve, sd_done, n)
                    dve.tensor_reduce(ss[:, :], sq[:, :].rearrange("p (g e) -> p g e", e=HEADC), AX.X,
                                      ALU.add).then_inc(ss_done, 1)

                def inverses(n):
                    dve.wait_ge(sd_done, n + 1)
                    dve.reciprocal(rs[:, :], sd[:, :]).then_inc(rs_done, 1)

                def masked(n):
                    dve.wait_ge(rs_done, n + 1)
                    dve.tensor_scalar(rsv[:, :], rs[:, :], s.valid[:, bass.ds(n, 1)], None, ALU.mult).then_inc(rsv_done, 1)

                def scaled(n):
                    dve.wait_ge(rsv_done, n + 1)
                    start_after(dve, sums_done, n)
                    dve.tensor_tensor(kv[:, :].rearrange("p (g e) -> p g e", e=HEADC),
                                      ps_kv[:, :].rearrange("p (g e) -> p g e", e=HEADC),
                                      rsv[:, :].unsqueeze(2).to_broadcast([P, 2 * HEADS, HEADC]),
                                      ALU.mult).then_inc(kvn_done, 1)

                def step(n, h, i):
                    before = (lambda stage: None) if is_first(n) else (lambda stage: stage(n - 1))
                    dve.wait_ge(x_in[h], 16 * (i + 1))
                    dve.bn_stats(stats[:, h, :], x[:, h, :]).then_inc(stats_done, 1)
                    dve.wait_ge(deg_done, n - 1 + DEG_CREDIT)
                    start_after(dve, rank_done, n)
                    dve.tensor_copy(s.onehot[:, h, :, 0], s.count[:, 1 - h, :, SLOTS - 1]).then_inc(slot0_done, 1)
                    dve.tensor_tensor(
                        s.onehot[:, h, :, 1:],
                        k.iota_row[:, 0:BLOCKS].unsqueeze(2).to_broadcast([P, BLOCKS, COLS]),
                        s.block_f[:, bass.ds(n * COLS, COLS)].unsqueeze(1).to_broadcast([P, BLOCKS, COLS]),
                        ALU.is_equal).then_inc(onehot_done, 1)
                    before(squares)
                    dve.wait_ge(stats_done, n + 1)
                    dve.wait_ge(onehot_done, n + 1)
                    dve.tensor_tensor_scan(s.count[:, h, :, :].rearrange("p b c -> p (b c)"),
                                           s.keep[:, :, :].rearrange("p b c -> p (b c)"),
                                           s.onehot[:, h, :, :].rearrange("p b c -> p (b c)"), 0.0,
                                           ALU.mult, ALU.add).then_inc(count_done, 1)
                    dve.bn_aggr(mv[:, h, :], stats[:, h, :]).then_inc(mv_done, 1)
                    before(inverses)
                    dve.wait_ge(count_done, n + 1)
                    dve.tensor_tensor(picked[:, :, :], s.onehot[:, h, :, 1:], s.count[:, h, :, 1:],
                                      ALU.mult).then_inc(picked_done, 1)
                    dve.wait_ge(std_done, n + 1)
                    dve.reciprocal(rstd[:, h:h + 1], std[:, h:h + 1]).then_inc(rstd_done, 1)
                    before(masked)
                    start_after(dve, xn_out[h], 16 * i)
                    start_after(dve, xT_done, n)
                    dve.wait_ge(rstd_done, n + 1)
                    dve.tensor_scalar(xn[:, h, :], x[:, h, :], mv[:, h, 0:1], rstd[:, h:h + 1], ALU.subtract,
                                      ALU.mult).then_inc(xn_done, 1)
                    dve.wait_ge(picked_done, n + 1)
                    dve.tensor_reduce(rank[:, :], picked[:, :, :].rearrange("p b c -> p c b"), AX.X,
                                      ALU.add).then_inc(rank_done, 1)
                    before(scaled)
                    dve.wait_ge(rank_done, n + 1)
                    dve.tensor_scalar(pos[:, :], rank[:, :], -1.0, None, ALU.add).then_inc(pos_done, 1)
                    start_after(dve, scattered[h], 16 * COLS * i)
                    dve.tensor_copy(rec[:, h, :, 0], s.dst[:, bass.ds(n * COLS, COLS)]).then_inc(rec_done, 1)
                    dve.tensor_copy(rec[:, h, :, 1], s.ew[:, bass.ds(n * COLS, COLS)].bitcast(I32)).then_inc(rec_done, 1)
                    dve.wait_ge(pos_done, n + 1)
                    dve.tensor_scalar(lane[:, :], pos[:, :], P - 1, None, ALU.bitwise_and).then_inc(split2_done, 1)
                    dve.tensor_scalar(tile[:, :], pos[:, :], 7, None, ALU.logical_shift_right).then_inc(split2_done, 1)
                    dve.wait_ge(split2_done, 2 * n + 2)
                    dve.scalar_tensor_tensor(out=addr[:, h, :], in0=lane[:, :], scalar=float(TILES), in1=tile[:, :],
                                             op0=ALU.mult, op1=ALU.add).then_inc(addr_done, 1)
                    dve.wait_ge(deg_done, n + DEG_CREDIT)
                    for c in range(COLS):
                        dve.tensor_scalar(local[:, c, :], k.iota_row[:, :], s.local_f[:, bass.ds(n * COLS + c, 1)],
                                          s.ew[:, bass.ds(n * COLS + c, 1)], ALU.is_equal,
                                          ALU.mult).then_inc(local_done, 1)

                steps(dve, step)
                for stage in (squares, inverses, masked, scaled):
                    stage(BLOCKS - 1)

            @block.tensor
            def _(pe):
                acc = dict(start=False, stop=False, skip_group_check=True)
                pe.wait_ge(zeros_made, 1)
                for bank in (ps_deg, ps_sum):
                    pe.matmul(bank[:, :], zeros[:, 0:P], zeros[:, :], start=True, stop=False, skip_group_check=True)
                pe.sem_inc(deg_done, DEG_CREDIT)

                def sums(n):
                    pe.wait_ge(kvn_done, n + 1)
                    for c in range(DC):
                        v = kv[:, D + c * P:D + (c + 1) * P]
                        pe.matmul(VK[:, c * P:(c + 1) * P], v, kv[:, c * P:(c + 1) * P], **acc)
                        pe.matmul(VSUM[:, c:c + 1], v, k.ones[:, 0:1], **acc)
                    pe.matmul(KSUM, k.ones[:, :], kv[:, 0:D], **acc).then_inc(sums_done, 1)

                def step(n, h, i):
                    pe.wait_ge(xn_done, n + 1)
                    start_after(pe, xT_copied, n)
                    for c in range(DC):
                        last = pe.transpose(ps_xT[:, c * P:(c + 1) * P], xn[:, h, c * P:(c + 1) * P], k.ident[:, :])
                    last.then_inc(xT_done, 1)
                    if not is_first(n):
                        sums(n - 1)
                    pe.wait_ge(xT_copied, n + 1)
                    start_after(pe, kvn_done, n)
                    for c in range(DC):
                        pe.matmul(ps_kv[:, :], xT[:, c, :], s.wkv[:, c, :], start=(c == 0), stop=False)
                    pe.matmul(ps_kv[:, :], k.ones[0:1, :], s.bkv[0:1, :], start=False, stop=True).then_inc(kv_done, 1)
                    pe.wait_ge(onehot_done, n + 1)
                    for c in range(COLS):
                        pe.wait_ge(local_done, n * COLS + c + 1)
                        last = pe.matmul(DEG, local[:, c, :], s.onehot[:, h, :, 1 + c], **acc)
                    last.then_inc(deg_done, 1)

                steps(pe, step)
                sums(BLOCKS - 1)
                for bank in (ps_deg, ps_sum):
                    last = pe.matmul(bank[:, :], zeros[:, 0:P], zeros[:, :], start=False, stop=True, skip_group_check=True)
                last.then_inc(all_summed, 1)


def degrees_and_weights(k):
    nc, A = k.nc, k.A
    BUFS = 4
    with ExitStack() as ctx:
        sb = lambda name, shape, dt=F32: k.sb(name, shape, dt, ctx)
        rows_in = sb("rows_in", [P, BUFS, CHUNK, D])
        deg1 = sb("deg1", [P, BLOCKS])
        positive = sb("positive", [P, BLOCKS])
        guarded = sb("guarded", [P, BLOCKS])
        root = sb("root", [P, BLOCKS])
        inverse = sb("inverse", [P, BLOCKS])
        headmask = sb("headmask", [P, P])
        t1 = sb("t1", [P, DC, P])
        t2 = sb("t2", [P, DC, P])
        t3 = sb("t3", [P, DC, P])
        col = sb("col", [P, DC])
        kvT = sb("kvT", [P, DC, P])
        B = sb("B", [P, DC, D])
        ps_B = k.ps("ps_B", [P, 512], ctx)
        ps_M = k.ps("ps_M", [P, 512], ctx)
        ps_c = k.ps("ps_c", [P, 512], ctx)
        got = [k.sem(f"got{b}") for b in range(BUFS)]
        put = k.sem("put")
        (deg_step, root_done, dinv_done, scaled, mask_made, kv_step, kvT_done, B_done, B_copied, M_done) = (
            k.sem(name) for name in ("deg_step root_done dinv_done scaled mask_made kv_step kvT_done B_done B_copied M_done").split())
        src = k.xn_dram.rearrange("(t p) d -> p t d", p=P)
        dst = k.table.rearrange("(t p) d -> p t d", p=P)
        def store(sp, c):
            sp.wait_ge(scaled, (c + 1) * CHUNK)
            sp.dma_start(dst[:, c * CHUNK:(c + 1) * CHUNK, :], k.acc[:, c * CHUNK:(c + 1) * CHUNK, :]).then_inc(put, 16)

        with nc.Block() as block:
            @block.sync
            def _(sp):
                for c in range(CHUNKS):
                    if c >= BUFS:
                        sp.wait_ge(scaled, (c - BUFS + 1) * CHUNK)
                    sp.dma_start(rows_in[:, c % BUFS, :, :], src[:, c * CHUNK:(c + 1) * CHUNK, :]).then_inc(got[c % BUFS], 16)
                    if c >= 2:
                        store(sp, c - 2)
                for c in range(CHUNKS - 2, CHUNKS):
                    store(sp, c)
                sp.wait_ge(put, 16 * CHUNKS)

            @block.scalar
            def _(act):
                act.wait_ge(deg_step, 3)
                act.activation(root[:, :], guarded[:, :], ACT.Sqrt).then_inc(root_done, 1)
                act.wait_ge(dinv_done, 1)
                for c in range(CHUNKS):
                    act.wait_ge(got[c % BUFS], 16 * (c // BUFS + 1))
                    for t in range(CHUNK):
                        n = c * CHUNK + t
                        act.activation(k.acc[:, n, :], rows_in[:, c % BUFS, t, :], ACT.Copy,
                                       scale=k.dinv[:, n:n + 1]).then_inc(scaled, 1)

            @block.gpsimd
            def _(pool):
                pool.memset(headmask[:, :], 0.0).then_inc(mask_made, 1)
                pool.wait_ge(mask_made, 1)
                for h in range(HEADS_PER_CHUNK):
                    cut = slice(h * HEADC, (h + 1) * HEADC)
                    pool.memset(headmask[cut, cut], 1.0 / N_NODES).then_inc(mask_made, 1)

            @block.vector
            def _(dve):
                dve.tensor_scalar(deg1[:, :], k.deg[:, :], 1.0, None, ALU.add).then_inc(deg_step, 1)
                dve.wait_ge(deg_step, 1)
                dve.tensor_scalar(positive[:, :], deg1[:, :], 0.0, None, ALU.is_gt).then_inc(deg_step, 1)
                dve.tensor_scalar(guarded[:, :], deg1[:, :], 2.0 ** -100, None, ALU.max).then_inc(deg_step, 1)
                dve.wait_ge(root_done, 1)
                dve.reciprocal(inverse[:, :], root[:, :]).then_inc(deg_step, 1)
                dve.wait_ge(deg_step, 4)
                dve.tensor_tensor(k.dinv[:, :], inverse[:, :], positive[:, :], ALU.mult).then_inc(dinv_done, 1)
                g = k.k_gb[:, 0, :].unsqueeze(1).to_broadcast([P, HEADS_PER_CHUNK, HEADC])
                b = k.k_gb[:, 1, :].unsqueeze(1).to_broadcast([P, HEADS_PER_CHUNK, HEADC])
                hg, hb = k.kv_gb[:, 0:1], k.kv_gb[:, 1:2]
                by_head = lambda t, c: t[:, c, :].rearrange("p (h e) -> p h e", e=HEADC)
                dve.tensor_scalar(t1[:, :, :], k.vk[:, :, :], hg, None, ALU.mult).then_inc(kv_step, 1)
                dve.tensor_scalar(col[:, :], k.vsum[:, :], hg, None, ALU.mult).then_inc(kv_step, 1)
                dve.tensor_scalar(t3[:, 0, 0:1], hb, float(N_NODES), None, ALU.mult).then_inc(kv_step, 1)
                dve.wait_ge(kv_step, 3)
                dve.scalar_tensor_tensor(out=t2[:, :, :], in0=k.ksum[:, :, :], scalar=hb, in1=t1[:, :, :],
                                         op0=ALU.mult, op1=ALU.add).then_inc(kv_step, 1)
                dve.tensor_scalar(k.vsum[:, :], col[:, :], t3[:, 0, 0:1], None, ALU.add).then_inc(kv_step, 1)
                dve.wait_ge(kv_step, 5)
                for c in range(DC):
                    dve.tensor_tensor(by_head(t1, c), by_head(t2, c), g, ALU.mult).then_inc(kv_step, 1)
                dve.wait_ge(kv_step, 5 + DC)
                for c in range(DC):
                    dve.scalar_tensor_tensor(out=by_head(t3, c), in0=b, scalar=k.vsum[:, c:c + 1], in1=by_head(t1, c),
                                             op0=ALU.mult, op1=ALU.add).then_inc(kv_step, 1)
                dve.wait_ge(kv_step, 5 + 2 * DC)
                dve.wait_ge(mask_made, 1 + HEADS_PER_CHUNK)
                for c in range(DC):
                    dve.tensor_tensor(kvT[:, c, :], t3[:, c, :], headmask[:, :], ALU.mult).then_inc(kvT_done, 1)
                dve.wait_ge(B_done, 1)
                dve.tensor_copy(B[:, :, :], ps_B[:, :].rearrange("p (c n) -> p c n", c=DC)).then_inc(B_copied, 1)
                dve.wait_ge(M_done, 1)
                dve.tensor_tensor(k.mix_w[:, :, :], ps_M[:, :].rearrange("p (c n) -> p c n", c=DC), k.mix_w1[:, :, :],
                                  ALU.add).then_inc(kv_step, 1)
                dve.tensor_tensor(k.mix_c[:, :], ps_c[:, 0:DC], k.mix_b1[:, :], ALU.add).then_inc(kv_step, 1)

            @block.tensor
            def _(pe):
                pe.wait_ge(kvT_done, DC)
                for c in range(DC):
                    last = pe.matmul(ps_B[:, c * D:(c + 1) * D], kvT[:, c, :], k.mix_w1[:, c, :], start=True, stop=True)
                last.then_inc(B_done, 1)
                pe.wait_ge(B_copied, 1)
                for c in range(DC):
                    for j in range(DC):
                        pe.matmul(ps_M[:, c * D:(c + 1) * D], k.wqT[:, j, c * P:(c + 1) * P], B[:, j, :],
                                  start=(j == 0), stop=(j == DC - 1))
                for f in range(DC):
                    for j in range(DC):
                        last = pe.matmul(ps_c[:, f:f + 1], B[:, j, f * P:(f + 1) * P], k.bq[:, j:j + 1],
                                         start=(j == 0), stop=(j == DC - 1))
                last.then_inc(M_done, 1)


def node_phases(k, ctx):
    k.acc = k.sb("acc", [P, BLOCKS, D], F32, ctx)
    degrees_and_weights(k)
    k.phase_done()
    gather_and_mix(k)
    k.phase_done()
    k.gate_w = k.sb("gate_w", [P, TOP, BLOCKS], F32, ctx)
    k.pos = k.sb("pos4", [P, TOP, BLOCKS], I32, ctx)
    with ExitStack() as inner:
        k.up_all = k.sb("up_all", [P, N_EXPERTS, UP], F32, inner)
        k.down_all = k.sb("down_all", [P, N_EXPERTS, DOWN], F32, inner)
        k.expert_parts = lambda up, down: (
            up[:, 0:DC * HIDDEN].rearrange("p (c n) -> p c n", c=DC), up[:, DC * HIDDEN:UP],
            down[:, 0:HC * D].rearrange("p (c n) -> p c n", c=HC), down[:, HC * D:DOWN])
        k.expert_words = k.sb("expert_words", [P, X_TRIPS], I32, inner)
        k.gb = k.sb("gb", [P, 2, DC], F32, inner)
        k.weights_in = k.nc.alloc_semaphore(name="weights_in")
        k.ids = k.sb("ids", [P, X_TILES + X_UNROLL], I32, inner)
        with ExitStack() as routing:
            k.logits = k.sb("logits", [P, BLOCKS, N_EXPERTS], F32, routing)
            head(k)
            k.phase_done()
            route(k)
            k.phase_done()
        experts(k)
        k.sems.append(k.weights_in)
        k.phase_done()
    combine(k)
    k.phase_done()


def gather_and_mix(k):
    nc, A = k.nc, k.A
    with ExitStack() as ctx:
        sb = lambda name, shape, dt=F32: k.sb(name, shape, dt, ctx)
        recs = sb("recs", [P, TILES + STEP_TILES, 2], I32)
        idx = sb("idx", [P, 2, STEP_TILES], I32)
        loc_i = sb("loc_i", [P, 2, STEP_TILES], I32)
        loc = sb("loc", [P, 2, STEP_TILES])
        ewt = sb("ewt", [P, 2, STEP_TILES])
        rows = sb("rows", [P, STEP_TILES, D])
        pick = sb("pick", [P, 2, STEP_TILES, P])
        x = sb("x2", [P, 2, D])
        xn = sb("xn2", [P, 2, D])
        xT = sb("xT2", [P, DC, P])
        hT = sb("hT", [P, DC, P])
        part = sb("part", [P, 2, D])
        ps_sum = [k.ps(f"ps_seg{r}", [P, 512], ctx) for r in range(RING)]
        ps_xT = k.ps("ps_xT2", [P, 512], ctx)
        ps_h = k.ps("ps_h", [P, 512], ctx)
        ps_o = k.ps("ps_o", [P, 512], ctx)
        recs_in, cleared = k.sem("recs_in"), k.sem("cleared")
        got = [k.sem(f"row_in{t}") for t in range(STEP_TILES)]
        in_x = [k.sem(f"x2_in{h}") for h in range(2)]
        in_xn = [k.sem(f"xn2_in{h}") for h in range(2)]
        part_out = [k.sem(f"part_out{h}") for h in range(2)]
        (idx_done, loci_done, loc_done, ewt_done, pick_done, seg_done, added, xT2_done, xT2_copied, h_done,
         gelu_done, o_done, skip_done, skip2_done, part_done, gather_held) = (
            k.sem(name) for name in ("idx_done loci_done loc_done ewt_done pick_done seg_done added xT2_done xT2_copied h_done "
            "gelu_done o_done skip_done skip2_done part_done gather_held").split())
        by_block = lambda a: a.rearrange("(t p) d -> p t d", p=P)
        CREDIT, ADDED_CREDIT = STEP_TILES, 2 * RING
        loops = ((0, PAIRS, True), (PAIRS, STEPS // 2, False))

        def sums(t):
            return ps_sum[t // 2 % RING][:, t % 2 * D:t % 2 * D + D]

        with nc.Block() as block:
            @block.sync
            def _(sp):
                sp.dma_start(recs[:, 0:TILES, :], k.records.rearrange("(p t) w -> p t w", p=P)).then_inc(recs_in, 16)
                for h in range(AHEAD):
                    sp.dma_start(x[:, h, :], by_block(A["x"])[:, h, :]).then_inc(in_x[h], 16)
                    sp.dma_start(xn[:, h, :], by_block(k.xn_dram)[:, h, :]).then_inc(in_xn[h], 16)
                with sp.Fori(0, PAIRS) as i:
                    for h in range(2):
                        n = 2 * i + h
                        sp.wait_ge(xT2_done, n + 1)
                        sp.wait_ge(skip2_done, n + 1)
                        sp.dma_start(x[:, h:h + 1, :], by_block(A["x"])[:, bass.ds(n + AHEAD, 1), :]).then_inc(in_x[h], 16)
                        sp.dma_start(xn[:, h:h + 1, :],
                                     by_block(k.xn_dram)[:, bass.ds(n + AHEAD, 1), :]).then_inc(in_xn[h], 16)
                        sp.wait_ge(part_done, n + 1)
                        sp.dma_start(by_block(k.part_dram)[:, bass.ds(n, 1), :], part[:, h:h + 1, :]).then_inc(part_out[h], 16)
                for h in range(2):
                    sp.wait_ge(in_x[h], 16 * (PAIRS + 1))
                    sp.wait_ge(in_xn[h], 16 * (PAIRS + 1))
                for h in range(2):
                    sp.wait_ge(part_out[h], 16 * PAIRS)

            @block.gpsimd
            def _(pool):
                with pool.Fori(0, STEPS // 2) as i:
                    for h in range(2):
                        pool.wait_ge(idx_done, 2 * i + h + 1)
                        for t in range(STEP_TILES):
                            pool.wait_ge(seg_done, (2 * i + h) * STEP_TILES + t + 1)
                            pool.sem_inc(gather_held, 1)
                            pool.indirect_dma_start(
                                out=rows[:, t, :], out_offset=None, in_=k.table,
                                in_offset=bass.IndirectOffsetOnAxis(idx[:, h, t:t + 1], 0),
                                bounds_check=NODES - 1, oob_is_err=False).then_inc(got[t], 16)

            @block.scalar
            def _(act):
                with act.Fori(0, PAIRS) as i:
                    for h in range(2):
                        n = 2 * i + h
                        act.wait_ge(xT2_done, n + 1)
                        act.wait_ge(h_done, n)
                        act.activation(xT[:, :, :], ps_xT[:, 0:D].rearrange("p (c n) -> p c n", c=DC),
                                       ACT.Identity).then_inc(xT2_copied, 1)
                        act.wait_ge(h_done, n + 1)
                        act.wait_ge(o_done, n)
                        for f in range(DC):
                            act.activation(hT[:, f, :], ps_h[:, f * P:(f + 1) * P], ACT.Gelu,
                                           bias=k.mix_c[:, f:f + 1]).then_inc(gelu_done, 1)

            @block.vector
            def _(dve):
                dve.memset(recs[:, TILES:, :], 0).then_inc(cleared, 1)
                dve.wait_ge(recs_in, 16)
                dve.wait_ge(cleared, 1)

                def unpack(h, n):
                    now = recs[:, bass.ds(n * STEP_TILES, STEP_TILES), :]
                    dve.tensor_scalar(idx[:, h, :], now[:, :, 0], (1 << DST_BITS) - 1, None,
                                      ALU.bitwise_and).then_inc(idx_done, 1)
                    dve.tensor_scalar(loc_i[:, h, :], now[:, :, 0], DST_BITS, None,
                                      ALU.logical_shift_right).then_inc(loci_done, 1)
                    dve.tensor_copy(ewt[:, h, :].bitcast(I32), now[:, :, 1]).then_inc(ewt_done, 1)
                    dve.wait_ge(loci_done, n + 1)
                    dve.tensor_copy(loc[:, h, :], loc_i[:, h, :]).then_inc(loc_done, 1)

                def make_pick(h, t):
                    dve.tensor_scalar(pick[:, h, t, :], k.iota_row[:, :], loc[:, h, t:t + 1], ewt[:, h, t:t + 1],
                                      ALU.is_equal, ALU.mult).then_inc(pick_done, 1)

                def block_register(value):
                    return nc.s_assert_within(dve.snap(dve.to_reg(value)), 0, BLOCKS - 1,
                                              skip_runtime_bounds_check_because="a tile's block is counted among BLOCKS")

                dve.sem_inc(added, ADDED_CREDIT)
                unpack(0, 0)
                dve.wait_ge(loc_done, 1)
                for t in range(STEP_TILES):
                    make_pick(0, t)

                def step(i, h, mlp):
                    n = 2 * i + h
                    word = dve.value_load(k.words[0:1, bass.ds(n, 1)])
                    first = n * STEP_TILES
                    dve.wait_ge(seg_done, first + CREDIT)
                    unpack(1 - h, n + 1)
                    dve.wait_ge(loc_done, n + 2)
                    blk = block_register(word >> STEP_TILES)
                    for t in range(STEP_TILES):
                        make_pick(1 - h, t)
                        if mlp and t == STEP_TILES // 2:
                            dve.wait_ge(in_x[h], 16 * (i + 1))
                            dve.wait_ge(part_out[h], 16 * i)
                            dve.tensor_tensor(part[:, h, :], x[:, h, :], k.bias_sum, ALU.add).then_inc(skip_done, 1)
                            dve.wait_ge(in_xn[h], 16 * (i + 1))
                            dve.wait_ge(skip_done, n + 1)
                            dve.tensor_tensor(part[:, h, :], part[:, h, :], xn[:, h, :], ALU.add).then_inc(skip2_done, 1)
                        if t % 2 == 0:
                            continue
                        dve.wait_ge(seg_done, first + t + 1 + CREDIT)
                        for u in (t - 1, t):
                            if u > 0:
                                blk = block_register(blk + ((word >> (u - 1)) & 1))
                            dve.wait_ge(added, first + u + ADDED_CREDIT)
                            here = k.acc[:, bass.ds(blk, 1), :]
                            dve.tensor_tensor(here, here, sums(u).unsqueeze(1), ALU.add).then_inc(added, 1)
                    if mlp:
                        dve.wait_ge(o_done, n + 1)
                        dve.wait_ge(skip2_done, n + 1)
                        dve.tensor_tensor(part[:, h, :], part[:, h, :], ps_o[:, 0:D], ALU.add).then_inc(part_done, 1)

                for start, end, mlp in loops:
                    with dve.Fori(start, end) as i:
                        for h in range(2):
                            step(i, h, mlp)

            @block.tensor
            def _(pe):
                pe.sem_inc(seg_done, CREDIT)

                def step(i, h, mlp):
                    n = 2 * i + h
                    first = n * STEP_TILES
                    for t in range(STEP_TILES):
                        pe.wait_ge(got[t], 16 * (n + 1))
                        pe.wait_ge(pick_done, first + t + 1)
                        if t % 2 == 0:
                            pe.wait_ge(added, first + t + 2 - 2 * RING + ADDED_CREDIT)
                        pe.matmul(sums(t), pick[:, h, t, :], rows[:, t, :], start=True, stop=True).then_inc(seg_done, 1)
                        if mlp and t == 2:
                            pe.wait_ge(in_xn[h], 16 * (i + 1))
                            pe.wait_ge(xT2_copied, n)
                            for c in range(DC):
                                last = pe.transpose(ps_xT[:, c * P:(c + 1) * P], xn[:, h, c * P:(c + 1) * P], k.ident[:, :])
                            last.then_inc(xT2_done, 1)
                        if mlp and t == 5:
                            pe.wait_ge(xT2_copied, n + 1)
                            pe.wait_ge(gelu_done, DC * n)
                            for f in range(DC):
                                for c in range(DC):
                                    last = pe.matmul(ps_h[:, f * P:(f + 1) * P], k.mix_w[:, c, f * P:(f + 1) * P],
                                                     xT[:, c, :], start=(c == 0), stop=(c == DC - 1))
                            last.then_inc(h_done, 1)
                        if mlp and t == 9:
                            pe.wait_ge(gelu_done, DC * n + DC)
                            pe.wait_ge(part_done, n)
                            for f in range(DC):
                                last = pe.matmul(ps_o[:, 0:D], hT[:, f, :], k.mix_w2[:, f, :],
                                                 start=(f == 0), stop=(f == DC - 1))
                            last.then_inc(o_done, 1)

                for start, end, mlp in loops:
                    with pe.Fori(start, end) as i:
                        for h in range(2):
                            step(i, h, mlp)


def head(k):
    nc, A = k.nc, k.A
    STAGES = 4
    PEELED = STAGES
    with ExitStack() as ctx:
        sb = lambda name, shape, dt=F32: k.sb(name, shape, dt, ctx)
        part = sb("part3", [P, 2, D])
        h7 = sb("h7", [P, 2, D])
        hT = sb("h7T", [P, DC, 2 * P])
        rT = sb("rT", [P, DC, 2 * P])
        stats = sb("stats3", [P, 2, 6])
        mv = sb("mv3", [P, 2, 2])
        std = sb("std3", [P, 2])
        rstd = sb("rstd3", [P, 2])
        xl = sb("xl", [P, 2, D])
        fT = sb("fT", [P, DC, 2 * P])
        wr = sb("wr", [P, DC, N_EXPERTS])
        br = sb("br", [P, N_EXPERTS])
        eps2 = sb("eps2", [P, 1])
        ps_T, ps_h, ps_o, ps_f, ps_l = (k.ps(f"ps3_{n}", [P, 512], ctx) for n in "T h o f l".split())
        in_part, rows_out, consts_in = k.sem("part_in"), k.sem("rows_out"), k.sem("consts_in")
        (eps2_made, h7_done, h7T_done, h7T_copied, hid_done, relu_done, gout_done, x1_done, stats_done, mv_done, std_done,
         rstd_done, xl_done, f_done, fT_copied, lg_done, lgb_done, held) = (
            k.sem("head_" + name) for name in (
                "eps2_made h7_done h7T_done h7T_copied hid_done relu_done gout_done x1_done stats_done mv_done std_done "
                "rstd_done xl_done f_done fT_copied lg_done lgb_done held").split())
        by_block = lambda a: a.rearrange("(t p) d -> p t d", p=P)
        halves = lambda bank: bank[:, :].rearrange("p (c n) -> p c n", c=2)
        both = range(2)

        def trips(eng, body):
            for i in range(PEELED):
                body(i, [s for s in range(STAGES) if i >= s])
            with eng.Fori(PEELED, PAIRS) as i:
                body(i, range(STAGES))
            for i in range(PAIRS, PAIRS + STAGES - 1):
                body(i, [s for s in range(STAGES) if i - s < PAIRS])

        with nc.Block() as block:
            @block.sync
            def _(sp):
                sp.dma_start(part[:, :, :], by_block(k.part_dram)[:, 0:2, :]).then_inc(in_part, 16)

                def body(i, stages):
                    if 2 in stages:
                        j = i - 2
                        sp.wait_ge(xl_done, 2 * j + 2)
                        sp.dma_start(by_block(k.ffn_rows)[:, bass.ds(2 * j, 2), :], xl[:, :, :]).then_inc(rows_out, 16)
                    if 1 in stages:
                        j = i - 1
                        sp.wait_ge(x1_done, j + 1)
                        sp.dma_start(part[:, :, :], by_block(k.part_dram)[:, bass.ds(2 * j + 2, 2), :]).then_inc(in_part, 16)

                trips(sp, body)
                sp.wait_ge(in_part, 16 * (PAIRS + 1))
                sp.wait_ge(rows_out, 16 * PAIRS)

            @block.scalar
            def _(act):
                with nc.allow_non_contiguous_dma(reason="columns of a few hundred words"):
                    for t, (dst, b) in enumerate(((k.gb[:, 0, :], A["gamma"]), (k.gb[:, 1, :], A["beta"]))):
                        act.dma_start(dst, b.rearrange("(c p) -> p c", p=P)).then_inc(consts_in, 16)
                act.dma_start(wr[:, :, :], A["Wr"].rearrange("(c p) e -> p c e", p=P)).then_inc(consts_in, 16)
                act.dma_start(br[:, :], A["br"].partition_broadcast(P)).then_inc(consts_in, 16)
                for e in range(N_EXPERTS):
                    up, b1, down, b2 = k.expert_parts(k.up_all[:, e, :], k.down_all[:, e, :])
                    act.dma_start(up, A["W1"][e].rearrange("(c p) n -> p c n", p=P)).then_inc(k.weights_in, 16)
                    act.dma_start(down, A["W2"][e].rearrange("(c p) n -> p c n", p=P)).then_inc(k.weights_in, 16)
                    act.dma_start(b2, A["b2"][e].partition_broadcast(P)).then_inc(k.weights_in, 16)
                    with nc.allow_non_contiguous_dma(reason="an expert's first bias, features on partitions"):
                        act.dma_start(b1, A["b1"][e].rearrange("(c p) -> p c", p=P)).then_inc(k.weights_in, 16)
                act.wait_ge(consts_in, 64)
                act.wait_ge(eps2_made, 1)

                def body(i, stages):
                    if 0 in stages:
                        start_after(act, h7T_done, i)
                        for h in both:
                            act.activation(h7[:, h:h + 1, :], k.acc[:, bass.ds(2 * i + h, 1), :], ACT.Copy,
                                           scale=k.dinv[:, bass.ds(2 * i + h, 1)]).then_inc(h7_done, 1)
                    if 1 in stages:
                        j = i - 1
                        act.wait_ge(hid_done, j + 1)
                        start_after(act, gout_done, j)
                        for f in range(DC):
                            act.activation(rT[:, f, :], halves(ps_h)[:, f, :], ACT.Relu,
                                           bias=k.gcn_c[:, f:f + 1]).then_inc(relu_done, 1)
                    if 2 in stages:
                        j = i - 2
                        act.wait_ge(mv_done, 2 * j + 2)
                        start_after(act, rstd_done, j)
                        act.activation(std[:, :], mv[:, :, 1], ACT.Sqrt, bias=eps2[:, :], scale=1.0 + EPS).then_inc(std_done, 1)
                    if 3 in stages:
                        j = i - 3
                        act.wait_ge(f_done, j + 1)
                        start_after(act, lg_done, j)
                        for c in range(DC):
                            act.activation(fT[:, c, :], halves(ps_f)[:, c, :], ACT.Identity, scale=k.gb[:, 0, c:c + 1],
                                           bias=k.gb[:, 1, c:c + 1]).then_inc(fT_copied, 1)
                    if 0 in stages:
                        act.wait_ge(h7T_done, i + 1)
                        start_after(act, hid_done, i)
                        act.activation(hT[:, :, :], halves(ps_T), ACT.Copy).then_inc(h7T_copied, 1)

                trips(act, body)

            @block.vector
            def _(dve):
                dve.memset(eps2[:, :], EPS * EPS).then_inc(eps2_made, 1)
                dve.wait_ge(consts_in, 64)

                def body(i, stages):
                    if 2 in stages:
                        j = i - 2
                        dve.wait_ge(x1_done, j + 1)
                        dve.sem_inc(held, 1)
                        for h in both:
                            dve.bn_stats(stats[:, h, :], k.acc[:, bass.ds(2 * j + h, 1), :][:, 0, :]).then_inc(stats_done, 1)
                        dve.wait_ge(stats_done, 2 * j + 2)
                        dve.sem_inc(held, 1)
                        for h in both:
                            dve.bn_aggr(mv[:, h, :], stats[:, h, :]).then_inc(mv_done, 1)
                        dve.wait_ge(std_done, j + 1)
                        dve.reciprocal(rstd[:, :], std[:, :]).then_inc(rstd_done, 1)
                        start_after(dve, rows_out, 16 * j)
                        start_after(dve, f_done, j)
                        dve.wait_ge(rstd_done, j + 1)
                        for h in both:
                            dve.tensor_scalar(xl[:, h:h + 1, :], k.acc[:, bass.ds(2 * j + h, 1), :], mv[:, h, 0:1],
                                              rstd[:, h:h + 1], ALU.subtract, ALU.mult).then_inc(xl_done, 1)
                    if 3 in stages:
                        j = i - 3
                        dve.wait_ge(lg_done, j + 1)
                        dve.tensor_tensor(k.logits[:, bass.ds(2 * j, 2), :],
                                          ps_l[:, 0:2 * N_EXPERTS].rearrange("p (h e) -> p h e", h=2),
                                          br[:, :].unsqueeze(1).to_broadcast([P, 2, N_EXPERTS]), ALU.add).then_inc(lgb_done, 1)
                    if 1 in stages:
                        j = i - 1
                        dve.wait_ge(gout_done, j + 1)
                        dve.wait_ge(in_part, 16 * (j + 1))
                        dve.tensor_tensor(k.acc[:, bass.ds(2 * j, 2), :], halves(ps_o), part[:, :, :], ALU.add).then_inc(x1_done, 1)

                trips(dve, body)

            @block.tensor
            def _(pe):
                pe.wait_ge(consts_in, 64)

                def turn(bank, rows):
                    for c in range(DC):
                        for h in both:
                            last = pe.transpose(halves(bank)[:, c, h * P:(h + 1) * P], rows[:, h, c * P:(c + 1) * P], k.ident[:, :])
                    return last

                def body(i, stages):
                    if 1 in stages:
                        j = i - 1
                        pe.wait_ge(h7T_copied, j + 1)
                        start_after(pe, relu_done, DC * j)
                        for f in range(DC):
                            for c in range(DC):
                                last = pe.matmul(halves(ps_h)[:, f, :], k.gcn_w[:, c, f * P:(f + 1) * P],
                                                 hT[:, c, :], start=(c == 0), stop=(c == DC - 1))
                        last.then_inc(hid_done, 1)
                    if 3 in stages:
                        j = i - 3
                        pe.wait_ge(xl_done, 2 * j + 2)
                        start_after(pe, fT_copied, DC * j)
                        turn(ps_f, xl).then_inc(f_done, 1)
                    if 0 in stages:
                        pe.wait_ge(h7_done, 2 * i + 2)
                        start_after(pe, h7T_copied, i)
                        turn(ps_T, h7).then_inc(h7T_done, 1)
                    if 1 in stages:
                        j = i - 1
                        pe.wait_ge(relu_done, DC * j + DC)
                        start_after(pe, x1_done, j)
                        for h in both:
                            for f in range(DC):
                                last = pe.matmul(halves(ps_o)[:, h, :], rT[:, f, h * P:(h + 1) * P], k.gcn_w2[:, f, :],
                                                 start=(f == 0), stop=(f == DC - 1))
                        last.then_inc(gout_done, 1)
                    if 3 in stages:
                        j = i - 3
                        pe.wait_ge(fT_copied, DC * j + DC)
                        start_after(pe, lgb_done, j)
                        for h in both:
                            for c in range(DC):
                                last = pe.matmul(ps_l[:, h * N_EXPERTS:(h + 1) * N_EXPERTS], fT[:, c, h * P:(h + 1) * P],
                                                 wr[:, c, :], start=(c == 0), stop=(c == DC - 1))
                        last.then_inc(lg_done, 1)

                trips(pe, body)


def route(k):
    nc = k.nc
    with ExitStack() as ctx:
        sb = lambda name, shape, dt=F32: k.sb(name, shape, dt, ctx)
        rev = sb("rev", [P, N_EXPERTS])
        best = sb("best", [P, TOP, BLOCKS])
        first = sb("first", [P, BLOCKS])
        score = sb("score", [P, BLOCKS, N_EXPERTS])
        hit = sb("hit", [P, N_EXPERTS, TOP, BLOCKS])
        gap = sb("gap", [P, BLOCKS])
        e2, den = gap, first
        tri = sb("tri4", [P, P])
        flat = lambda t: t.rearrange("p e i -> p (e i)")
        hit_flat = hit[:, :, :, :].rearrange("p e j b -> p (e j b)")
        SLOT = 2 * TOP
        size = N_EXPERTS * TOP * BLOCKS
        keep, count = (k.arena[:, n * size:(n + 1) * size].rearrange("p (e i) -> p e i", e=N_EXPERTS) for n in range(2))
        rest = k.arena[:, 2 * size:]
        place, tile_no = rest[:, 0:TOP * BLOCKS], rest[:, TOP * BLOCKS:TOP * BLOCKS + X_TILES + X_UNROLL]
        total_i = sb("total4_i", [P, N_EXPERTS], I32)
        tiles_i = sb("tiles4_i", [P, N_EXPERTS], I32)
        tiles = sb("tiles4", [P, N_EXPERTS])
        tile_end = sb("tile4_end", [P, N_EXPERTS])
        tile_start = sb("tile4_start", [P, N_EXPERTS])
        base = sb("base4", [P, N_EXPERTS])
        lane_i = place.bitcast(I32)
        tile_i = sb("tile4", [P, TOP * BLOCKS], I32)
        tile_no_i = sb("tile_no_i", [P, X_TILES + X_UNROLL], I32)
        tile_e = sb("tile_e", [P, X_TILES + X_UNROLL])
        word = sb("word4", [P, X_TRIPS])
        row_id = sb("row_id", [P, BLOCKS], I32)
        spare = flat(keep)
        lane, tile, ident_no = (spare[:, n * 256:n * 256 + w] for n, w in enumerate((TOP * BLOCKS, TOP * BLOCKS, BLOCKS)))
        zeros = spare[:, 768:768 + X_TILES]
        at_lane = hit_flat[:, 0:SLOT * P].rearrange("p (s n) -> p s n", s=SLOT)
        at_tile = hit_flat[:, SLOT * P:SLOT * (P + X_TILES)].rearrange("p (s n) -> p s n", s=SLOT)
        ps_n = k.ps("ps4_n", [P, 512], ctx)
        ps_id = k.ps("ps4_id", [P, 512], ctx)
        (step, gap_done, e2_done, tri_made, made, counted, prefix_done, routed, lane_made, tile_made, placed,
         all_placed, zeros_made) = (
            k.sem("route_" + name) for name in (
                "step gap_done e2_done tri_made made counted prefix_done routed lane_made tile_made placed "
                "all_placed zeros_made").split())
        shape = [P, BLOCKS, N_EXPERTS]
        per_row = lambda t: t.unsqueeze(2).to_broadcast(shape)
        by_row = lambda j: hit[:, :, j, :].rearrange("p e b -> p b e")
        by_expert = lambda t: t[:, :].unsqueeze(2).to_broadcast([P, N_EXPERTS, TOP * BLOCKS])
        hits = hit[:, :, :, :].rearrange("p e j b -> p e (j b)")
        logits = k.logits[:, :, :]
        LOWEST = -3.0e38
        with nc.Block() as block:
            @block.scalar
            def _(act):
                act.wait_ge(gap_done, 1)
                act.activation(e2[:, :], gap[:, :], ACT.Exp).then_inc(e2_done, 1)

            @block.gpsimd
            def _(pool):
                pool.memset(tri[:, :], 1.0).then_inc(tri_made, 1)
                pool.memset(keep[:, :, 1:], 1.0).then_inc(made, 1)
                pool.memset(keep[:, :, 0:1], 0.0).then_inc(made, 1)
                pool.iota(tile_no_i[:, :], pattern=[[1, X_TILES + X_UNROLL]], base=0, channel_multiplier=0).then_inc(made, 1)
                pool.iota(row_id[:, :], pattern=[[P, BLOCKS]], base=0, channel_multiplier=1).then_inc(made, 1)
                pool.wait_ge(tri_made, 1)
                pool.affine_select(out=tri[:, :], in_=tri[:, :], compare_op=ALU.is_gt, fill=0.0,
                                   base=0, pattern=[[1, P]], channel_multiplier=-1).then_inc(made, 1)

            @block.vector
            def _(dve):
                steps = [0]

                def after_last(op):
                    op.then_inc(step, 1)
                    steps[0] += 1
                    dve.wait_ge(step, steps[0])

                after_last(dve.tensor_scalar(rev[:, :], k.iota_row[:, 0:N_EXPERTS], -1.0, float(N_EXPERTS), ALU.mult, ALU.add))
                rev_all = rev[:, :].unsqueeze(1).to_broadcast(shape)
                for j in range(TOP):
                    after_last(dve.tensor_reduce(best[:, j, :], logits, AX.X, ALU.max))
                    after_last(dve.tensor_tensor(score[:, :, :], logits, per_row(best[:, j, :]), ALU.is_equal))
                    after_last(dve.tensor_tensor(score[:, :, :], score[:, :, :], rev_all, ALU.mult))
                    after_last(dve.tensor_reduce(first[:, :], score[:, :, :], AX.X, ALU.max))
                    after_last(dve.tensor_tensor(by_row(j), rev_all, per_row(first[:, :]), ALU.is_equal))
                    if j + 1 < TOP:
                        after_last(dve.scalar_tensor_tensor(out=logits, in0=by_row(j), scalar=LOWEST, in1=logits,
                                                            op0=ALU.mult, op1=ALU.add))
                dve.tensor_tensor(gap[:, :], best[:, 1, :], best[:, 0, :], ALU.subtract).then_inc(gap_done, 1)
                dve.wait_ge(made, 5)
                dve.tensor_tensor_scan(flat(count[:, :, :]), flat(keep[:, :, :]), flat(hits), 0.0, ALU.mult,
                                       ALU.add).then_inc(counted, 1)
                dve.wait_ge(e2_done, 1)
                after_last(dve.tensor_scalar(den[:, :], e2[:, :], 1.0, None, ALU.add))
                after_last(dve.reciprocal(k.gate_w[:, 0, :], den[:, :]))
                after_last(dve.tensor_tensor(k.gate_w[:, 1, :], k.gate_w[:, 0, :], e2[:, :], ALU.mult))
                dve.wait_ge(prefix_done, 1)
                after_last(dve.tensor_scalar(total_i[:, :], ps_n[:, N_EXPERTS:2 * N_EXPERTS], float(P - 1), None, ALU.add))
                after_last(dve.tensor_scalar(tiles_i[:, :], total_i[:, :], 7, None, ALU.arith_shift_right))
                after_last(dve.tensor_copy(tiles[:, :], tiles_i[:, :]))
                after_last(dve.tensor_tensor_scan(tile_end[:, :], k.ones[:, 0:N_EXPERTS], tiles[:, :], 0.0, ALU.mult, ALU.add))
                after_last(dve.tensor_tensor(tile_start[:, :], tile_end[:, :], tiles[:, :], ALU.subtract))
                after_last(dve.scalar_tensor_tensor(out=base[:, :], in0=tile_start[:, :], scalar=float(P),
                                                    in1=ps_n[:, 0:N_EXPERTS], op0=ALU.mult, op1=ALU.add))
                after_last(dve.tensor_tensor(count[:, :, :], count[:, :, :], by_expert(base), ALU.add))
                after_last(dve.tensor_tensor(count[:, :, :], count[:, :, :], hits, ALU.mult))
                after_last(dve.tensor_reduce(place, count[:, :, :].rearrange("p e i -> p i e"), AX.X, ALU.add))
                pos = k.pos[:, :, :].rearrange("p j b -> p (j b)")
                after_last(dve.tensor_scalar(pos, place, -1.0, None, ALU.add))
                dve.tensor_scalar(lane_i, pos, P - 1, None, ALU.bitwise_and).then_inc(routed, 1)
                dve.tensor_scalar(tile_i[:, :], pos, 7, None, ALU.logical_shift_right).then_inc(routed, 1)
                dve.tensor_copy(ident_no, row_id[:, :]).then_inc(routed, 1)
                dve.tensor_copy(tile_no, tile_no_i[:, :]).then_inc(routed, 1)
                dve.memset(zeros, 0.0).then_inc(zeros_made, 1)
                dve.wait_ge(routed, 4)
                after_last(dve.tensor_copy(lane, lane_i))
                after_last(dve.tensor_copy(tile, tile_i[:, :]))
                with dve.Fori(0, PAIRS) as i:
                    for h in range(2):
                        for j in range(TOP):
                            slot = h * TOP + j
                            n = j * BLOCKS + 2 * i + h
                            dve.wait_ge(placed, SLOT * i + slot + 1)
                            dve.tensor_scalar(at_lane[:, slot, :], k.iota_row[:, :], lane[:, bass.ds(n, 1)],
                                              ident_no[:, bass.ds(2 * i + h, 1)], ALU.is_equal, ALU.mult).then_inc(lane_made, 1)
                            dve.tensor_scalar(at_tile[:, slot, :], tile_no[:, 0:X_TILES], tile[:, bass.ds(n, 1)], None,
                                              ALU.is_equal).then_inc(tile_made, 1)
                dve.memset(k.ids[:, X_TILES:], 0).then_inc(routed, 1)
                dve.wait_ge(all_placed, 1)
                after_last(dve.tensor_copy(k.ids[:, 0:X_TILES], ps_id[:, 0:X_TILES]))
                after_last(dve.tensor_scalar(tile_e[:, :], tile_no, tile_start[:, 1:2], None, ALU.is_ge))
                for e in range(2, N_EXPERTS):
                    after_last(dve.scalar_tensor_tensor(out=tile_e[:, :], in0=tile_no, scalar=tile_start[:, e:e + 1],
                                                        in1=tile_e[:, :], op0=ALU.is_ge, op1=ALU.add))
                of = lambda u: tile_e[:, u:u + X_TILES].rearrange("p (i u) -> p i u", u=X_UNROLL)[:, :, 0]
                after_last(dve.tensor_copy(word[:, :], of(0)))
                for u in range(1, X_UNROLL + 1):
                    after_last(dve.scalar_tensor_tensor(out=word[:, :], in0=of(u), scalar=float(N_EXPERTS ** u),
                                                        in1=word[:, :], op0=ALU.mult, op1=ALU.add))
                after_last(dve.tensor_copy(k.expert_words[:, :], word[:, :]))

            @block.tensor
            def _(pe):
                pe.wait_ge(counted, 1)
                pe.wait_ge(made, 5)
                last = count[:, :, TOP * BLOCKS - 1]
                pe.matmul(ps_n[:, 0:N_EXPERTS], tri[:, :], last, start=True, stop=True)
                pe.matmul(ps_n[:, N_EXPERTS:2 * N_EXPERTS], k.ones[:, :], last, start=True, stop=True).then_inc(prefix_done, 1)
                pe.wait_ge(zeros_made, 1)
                ids = ps_id[:, 0:X_TILES]
                pe.matmul(ids, zeros[:, 0:P], zeros, start=True, stop=False, skip_group_check=True)
                pe.sem_inc(placed, SLOT)
                with pe.Fori(0, PAIRS) as i:
                    for slot in range(SLOT):
                        pe.wait_ge(lane_made, SLOT * i + slot + 1)
                        pe.wait_ge(tile_made, SLOT * i + slot + 1)
                        pe.matmul(ids, at_lane[:, slot, :], at_tile[:, slot, :], start=False, stop=False,
                                  skip_group_check=True).then_inc(placed, 1)
                pe.matmul(ids, zeros[:, 0:P], zeros, start=False, stop=True, skip_group_check=True).then_inc(all_placed, 1)


def experts(k):
    nc, A = k.nc, k.A
    with ExitStack() as ctx:
        sb = lambda name, shape, dt=F32: k.sb(name, shape, dt, ctx)
        spans = iter(range(0, k.arena.shape[1], D))

        def room(slots, columns):
            taken = [next(spans) for _ in range(slots * columns // D)]
            return k.arena[:, taken[0]:taken[0] + slots * columns].rearrange("p (s n) -> p s n", s=slots)

        xrow = room(X_UNROLL, D)
        xT = room(2, DC * P)
        hT = room(2, HC * P)
        y = room(2, D)
        up_now = sb("up_now", [P, 2, UP])
        down_now = sb("down_now", [P, 2, DOWN])
        ids = k.ids
        idx = sb("idx5", [P, X_UNROLL], I32)
        ps_x = [k.ps(f"ps5_x{j}", [P, 512], ctx) for j in range(2)]
        ps_h = [k.ps(f"ps5_h{j}", [P, 512], ctx) for j in range(2)]
        ps_y = [k.ps(f"ps5_y{j}", [P, 512], ctx) for j in range(2)]
        (idx_done, x_done, xT_copied, up_copied, down_copied, hid_done, gelu_done, down_done, y_done,
         held) = (
            k.sem("tile_" + name) for name in (
                "idx_done x_done xT_copied up_copied down_copied hid_done gelu_done down_done y_done "
                "held").split())
        got = [k.sem(f"xrow_in{u}") for u in range(X_UNROLL)]
        y_out = [k.sem(f"y_out{j}") for j in range(2)]
        parts = [k.expert_parts(up_now[:, j, :], down_now[:, j, :]) for j in range(2)]
        N_WEIGHTS = 4 * N_EXPERTS

        def trips(eng, body):
            for u in range(X_UNROLL):
                body(u, u, 0)
            with eng.Fori(1, X_TRIPS - 1) as i:
                for u in range(X_UNROLL):
                    body(X_UNROLL * i + u, u, i)
            for u in range(X_UNROLL):
                body(X_TILES - X_UNROLL + u, u, X_TRIPS - 1)

        with nc.Block() as block:
            @block.sync
            def _(sp):
                def body(t, u, i):
                    sp.wait_ge(y_done, t + 1)
                    sp.dma_start(k.y_rows[bass.ds(t * P, P), :], y[:, u % 2, :]).then_inc(y_out[u % 2], 16)

                trips(sp, body)
                for j in range(2):
                    sp.wait_ge(y_out[j], 16 * X_TILES // 2)

            @block.gpsimd
            def _(pool):
                def body(t, u, i):
                    pool.wait_ge(idx_done, t + 1)
                    pool.sem_inc(held, 1)
                    pool.indirect_dma_start(out=xrow[:, u, :], out_offset=None, in_=k.ffn_rows,
                                            in_offset=bass.IndirectOffsetOnAxis(idx[:, u:u + 1], 0),
                                            bounds_check=NODES - 1, oob_is_err=False).then_inc(got[u], 16)

                trips(pool, body)

            @block.scalar
            def _(act):
                def transposed(t, slot):
                    act.wait_ge(x_done, t + 1)
                    start_after(act, hid_done, t - 1)
                    for c in range(DC):
                        act.activation(xT[:, slot, c * P:(c + 1) * P], ps_x[slot][:, c * P:(c + 1) * P], ACT.Identity,
                                       scale=k.gb[:, 0, c:c + 1], bias=k.gb[:, 1, c:c + 1]).then_inc(xT_copied, 1)

                transposed(0, 0)

                def body(t, u, i):
                    slot = u % 2
                    if not (isinstance(t, int) and t + 1 == X_TILES):
                        transposed(t + 1, 1 - slot)
                    act.wait_ge(hid_done, t + 1)
                    start_after(act, down_done, t - 1)
                    for c in range(HC):
                        act.activation(hT[:, slot, c * P:(c + 1) * P], ps_h[slot][:, c * P:(c + 1) * P], ACT.Gelu,
                                       bias=parts[slot][1][:, c:c + 1]).then_inc(gelu_done, 1)

                trips(act, body)

            @block.vector
            def _(dve):
                for u in range(X_UNROLL):
                    dve.tensor_copy(idx[:, u:u + 1], ids[:, u:u + 1]).then_inc(idx_done, 1)
                dve.wait_ge(k.weights_in, 16 * N_WEIGHTS)

                def finish(t, slot, uses):
                    dve.wait_ge(down_done, t + 1)
                    start_after(dve, y_out[slot], 16 * uses)
                    dve.tensor_tensor(y[:, slot, :], ps_y[slot][:, 0:D], parts[slot][3], ALU.add).then_inc(y_done, 1)

                expert = [dve.snap(dve.value_load(k.expert_words[0:1, 0:1]) & (N_EXPERTS - 1), min_val=0, max_val=N_EXPERTS - 1)]
                dve.tensor_copy(up_now[:, 0:1, :], k.up_all[:, bass.ds(expert[0], 1), :]).then_inc(up_copied, 1)

                def body(t, u, i):
                    slot = u % 2
                    if u == 0:
                        k.word = dve.value_load(k.expert_words[0:1, bass.ds(i, 1)])
                    e = [dve.snap((k.word >> (3 * v)) & (N_EXPERTS - 1), min_val=0, max_val=N_EXPERTS - 1) for v in (u, u + 1)]
                    start_after(dve, y_done, t - 1)
                    start_after(dve, down_done, t - 1)
                    dve.tensor_copy(down_now[:, slot:slot + 1, :], k.down_all[:, bass.ds(e[0], 1), :]).then_inc(down_copied, 1)
                    start_after(dve, gelu_done, HC * t)
                    dve.tensor_copy(up_now[:, 1 - slot:2 - slot, :], k.up_all[:, bass.ds(e[1], 1), :]).then_inc(up_copied, 1)
                    dve.wait_ge(x_done, t + 1)
                    dve.tensor_copy(idx[:, u:u + 1], ids[:, bass.ds(t + X_UNROLL, 1)]).then_inc(idx_done, 1)
                    if not (isinstance(t, int) and t == 0):
                        finish(t - 1, 1 - slot, 2 * i + (u - 1) // 2 if u > 0 else 2 * i - 1)

                trips(dve, body)
                finish(X_TILES - 1, (X_TILES - 1) % 2, X_TILES // 2 - 1)

            @block.tensor
            def _(pe):
                def turn(t, u, i):
                    pe.wait_ge(got[u], 16 * (i + 1))
                    start_after(pe, xT_copied, DC * (t - 1))
                    for c in range(DC):
                        last = pe.transpose(ps_x[u % 2][:, c * P:(c + 1) * P], xrow[:, u, c * P:(c + 1) * P], k.ident[:, :])
                    last.then_inc(x_done, 1)

                def down(t, slot):
                    pe.wait_ge(gelu_done, HC * t + HC)
                    pe.wait_ge(down_copied, t + 1)
                    start_after(pe, y_done, t - 1)
                    for c in range(HC):
                        last = pe.matmul(ps_y[slot][:, 0:D], hT[:, slot, c * P:(c + 1) * P], parts[slot][2][:, c, :],
                                         start=(c == 0), stop=(c == HC - 1))
                    last.then_inc(down_done, 1)

                turn(0, 0, 0)

                def body(t, u, i):
                    slot = u % 2
                    if not (isinstance(t, int) and t + 1 == X_TILES):
                        turn(t + 1, (u + 1) % X_UNROLL, i + (u + 1) // X_UNROLL)
                    pe.wait_ge(xT_copied, DC * t + DC)
                    pe.wait_ge(up_copied, t + 1)
                    start_after(pe, gelu_done, HC * (t - 1))
                    for c in range(HC):
                        for d in range(DC):
                            last = pe.matmul(ps_h[slot][:, c * P:(c + 1) * P], parts[slot][0][:, d, c * P:(c + 1) * P],
                                             xT[:, slot, d * P:(d + 1) * P], start=(d == 0), stop=(d == DC - 1))
                    last.then_inc(hid_done, 1)
                    if not (isinstance(t, int) and t == 0):
                        down(t - 1, 1 - slot)

                trips(pe, body)
                down(X_TILES - 1, (X_TILES - 1) % 2)


def combine(k):
    nc = k.nc
    with ExitStack() as ctx:
        sb = lambda name, shape, dt=F32: k.sb(name, shape, dt, ctx)
        idx = sb("idx6", [P, 2, TOP, CHUNK], I32)
        rows = sb("rows6", [P, 2, TOP, CHUNK, D])
        got = [k.sem(f"y_in{h}") for h in range(2)]
        idx_done, added, out_done, held = (k.sem("combine_" + n) for n in "idx_done added out_done held".split())
        out_v = k.out.rearrange("(t p) d -> p t d", p=P)
        OPS = TOP * CHUNK
        with nc.Block() as block:
            @block.sync
            def _(sp):
                with sp.Fori(0, CHUNKS) as c:
                    sp.wait_ge(added, OPS * (c + 1))
                    sp.dma_start(out_v[:, bass.ds(c * CHUNK, CHUNK), :], k.acc[:, bass.ds(c * CHUNK, CHUNK), :]).then_inc(out_done, 16)
                sp.wait_ge(out_done, 16 * CHUNKS)

            @block.gpsimd
            def _(pool):
                with pool.Fori(0, CHUNKS // 2) as i:
                    for h in range(2):
                        pool.wait_ge(idx_done, 2 * i + h + 1)
                        pool.sem_inc(held, 1)
                        for j in range(TOP):
                            for b in range(CHUNK):
                                pool.indirect_dma_start(
                                    out=rows[:, h, j, b, :], out_offset=None, in_=k.y_rows,
                                    in_offset=bass.IndirectOffsetOnAxis(idx[:, h, j, b:b + 1], 0),
                                    bounds_check=P * X_TILES - 1, oob_is_err=False).then_inc(got[h], 16)

            @block.vector
            def _(dve):
                def indices(h, c):
                    dve.tensor_copy(idx[:, h, :, :], k.pos[:, :, bass.ds(c * CHUNK, CHUNK)]).then_inc(idx_done, 1)

                def add(h, c, turn):
                    dve.wait_ge(got[h], 16 * OPS * (turn + 1))
                    for j in range(TOP):
                        if j > 0:
                            dve.wait_ge(added, OPS * c + CHUNK * j)
                        for b in range(CHUNK):
                            n = c * CHUNK + b
                            here = k.acc[:, bass.ds(n, 1), :]
                            dve.scalar_tensor_tensor(out=here, in0=rows[:, h, j, b:b + 1, :],
                                                     scalar=k.gate_w[:, j, bass.ds(n, 1)], in1=here, op0=ALU.mult,
                                                     op1=ALU.add).then_inc(added, 1)

                for h in range(2):
                    indices(h, h)
                with dve.Fori(0, CHUNKS // 2 - 1) as i:
                    for h in range(2):
                        add(h, 2 * i + h, i)
                        dve.wait_ge(added, OPS * (2 * i + h + 1))
                        indices(h, 2 * i + h + 2)
                for h in range(2):
                    add(h, CHUNKS - 2 + h, CHUNKS // 2 - 1)


_NAMES = {
    "gnn_W": "L0_gnn_W", "gnn_b": "L0_gnn_b", "gnn_W1": "L0_gnn_W1", "gnn_b1": "L0_gnn_b1", "gnn_W2": "L0_gnn_W2",
    "gnn_b2": "L0_gnn_b2", "w_qkv": "L0_mix_w_qkv", "b_qkv": "L0_mix_b_qkv", "kln_g": "L0_mix_kln_g",
    "kln_b": "L0_mix_kln_b", "vln_g": "L0_mix_vln_g", "vln_b": "L0_mix_vln_b", "mix_w1": "L0_mix_w1",
    "mix_b1": "L0_mix_b1", "mix_w2": "L0_mix_w2", "mix_b2": "L0_mix_b2", "gamma": "L0_ffn_gamma",
    "beta": "L0_ffn_beta", "Wr": "L0_ffn_Wr", "br": "L0_ffn_br", "W1": "L0_ffn_W1", "b1": "L0_ffn_b1",
    "W2": "L0_ffn_W2", "b2": "L0_ffn_b2",
}


def kernel(**inputs):
    import numpy as np
    import concourse.bacc as bacc
    from concourse.bass_utils import run_bass_kernel_spmd

    def padded(a, n, fill):
        a = np.asarray(a)
        return np.concatenate([a, np.full((n - a.shape[0],) + a.shape[1:], fill, a.dtype)])

    edges = P * EDGE_COLS
    arrays = {
        "x": padded(inputs["x"], NODES + AHEAD * P, 0),
        "src": padded(inputs["src"], edges, NODES).reshape(P, EDGE_COLS),
        "dst": padded(inputs["dst"], edges, 0).reshape(P, EDGE_COLS),
        "ew": padded(inputs["edge_weight"], edges, 0).reshape(P, EDGE_COLS),
    }
    for short, name in _NAMES.items():
        arrays[short] = np.ascontiguousarray(inputs[name])
    nc = bacc.Bacc("TRN2", target_bir_lowering=False, num_devices=1)
    aps = {n: nc.dram_tensor(f"in_{n}", a.shape, mybir.dt.from_np(a.dtype), kind="ExternalInput").ap()
           for n, a in arrays.items()}
    out = nc.dram_tensor("out", [NODES, D], F32, kind="ExternalOutput").ap()
    gps_layer(nc, aps, out)
    r = run_bass_kernel_spmd(nc, [{f"in_{n}": a for n, a in arrays.items()}], core_ids=[0])
    return r.results[0]["out"][:N_NODES]
```

```python
from contextlib import ExitStack

import concourse.bass as bass
from concourse import mybir

P = 128
N_NODES, D, N_EDGES = 12500, 256, 200000
HEADS, HEADC = 8, 32
N_EXPERTS, HIDDEN = 8, 512
EPS = 1e-5
DC = D // P
HC = HIDDEN // P
BLOCKS = -(-N_NODES // P)
assert BLOCKS % 2 == 0
NODES = BLOCKS * P
PAIRS = BLOCKS // 2
COLS = 16
EDGE_COLS = BLOCKS * COLS
assert EDGE_COLS * P >= N_EDGES
STEP_TILES = 16
STEPS = 104
TILES = STEPS * STEP_TILES
assert TILES >= N_EDGES // P + BLOCKS
SLOTS = COLS + 1
DST_BITS = 14
assert NODES <= 1 << DST_BITS
RING = 4
assert STEPS <= P and STEPS % 2 == 0 and STEPS >= BLOCKS and STEP_TILES % (2 * RING) == 0
HEADS_PER_CHUNK = P // HEADC
AHEAD = 2
TOP = 2
X_UNROLL = 4
HALVES = 2
HALF = BLOCKS // HALVES
GROUPS = HALVES * N_EXPERTS
HALF_TILES = HALF * TOP + N_EXPERTS - 1
X_TILES = -(-(BLOCKS * TOP + GROUPS - 1) // X_UNROLL) * X_UNROLL
X_TRIPS = X_TILES // X_UNROLL
UP = DC * HIDDEN + HC
DOWN = HC * D + D
CHUNK = 7
CHUNKS = BLOCKS // CHUNK
assert CHUNKS * CHUNK == BLOCKS and CHUNKS % 2 == 0
HALF_CHUNKS = HALF // CHUNK
assert HALF_CHUNKS * CHUNK == HALF and HALF_CHUNKS % 2 == 1

F32, I32, BF16 = mybir.dt.float32, mybir.dt.int32, mybir.dt.bfloat16
ALU = mybir.AluOpType
ACT = mybir.ActivationFunctionType
AX = mybir.AxisListType


def start_after(eng, sem, count):
    if not isinstance(count, int) or count > 0:
        eng.wait_ge(sem, count)


class Shared:
    pass


def gps_layer(nc, A, out):
    with ExitStack() as whole:
        k = Shared()
        k.nc, k.A, k.out = nc, A, out

        k.sems = []

        def sem(name):
            k.sems.append(nc.alloc_semaphore(name=name))
            return k.sems[-1]

        def phase_done():
            nc.clear_and_free_semaphores(k.sems)
            nc.all_engine_barrier()
            k.sems = []

        k.sem, k.phase_done = sem, phase_done
        k.sb = lambda name, shape, dt=F32, ctx=whole: ctx.enter_context(nc.sbuf_tensor(name, shape, dt))
        k.ps = lambda name, shape, ctx: ctx.enter_context(nc.psum_tensor(name, shape, F32))

        k.records = nc.dram_tensor("records", [P * TILES, 2], I32).ap()
        k.words_dram = nc.dram_tensor("words_dram", [STEPS, 1], I32).ap()
        k.xn_dram = nc.dram_tensor("xn_dram", [NODES + AHEAD * P, D], F32).ap()
        k.table = nc.dram_tensor("table", [NODES, D], F32).ap()
        k.part_dram = nc.dram_tensor("part_dram", [NODES + AHEAD * P, D], F32).ap()
        k.ffn_rows = nc.dram_tensor("ffn_rows", [NODES, D], F32).ap()
        k.y_rows = nc.dram_tensor("y_rows", [P * X_TILES, D], F32).ap()

        k.iota_row = k.sb("iota_row", [P, P])
        k.ident = k.sb("ident", [P, P])
        k.ones = k.sb("ones", [P, P])
        k.eps = k.sb("eps", [P, 1])
        k.arena = k.sb("arena", [P, 7 * DC * D])
        parts = iter(range(0, 7 * DC * D, DC * D))
        wide = lambda: k.arena[:, bass.ds(next(parts), DC * D)].rearrange("p (c n) -> p c n", c=DC)
        k.gcn_w = wide()
        k.gcn_w2 = wide()
        k.mix_w = wide()
        k.mix_w2 = wide()
        k.mix_w1 = wide()
        k.wqT = wide()
        biases = wide()
        k.bias_sum, k.bias_tmp = biases[:, 0, :], biases[:, 1, :]
        k.gcn_c = k.sb("gcn_c", [P, DC])
        k.mix_c = k.sb("mix_c", [P, DC])
        k.bq = k.sb("bq", [P, DC])
        k.mix_b1 = k.sb("mix_b1", [P, DC])
        k.kv_gb = k.sb("kv_gb", [P, 2])
        k.k_gb = k.sb("k_gb", [P, 2, HEADC])
        k.dinv = k.sb("dinv", [P, BLOCKS])
        k.words = k.sb("words", [1, STEPS], I32)

        with ExitStack() as sums:
            k.vsum = k.sb("vsum", [P, DC], F32, sums)
            k.acc = k.sb("acc", [P, BLOCKS, D], F32, sums)
            k.deg = k.dinv
            k.vk, k.ksum = (k.mix_w[:, j, :].rearrange("p (c n) -> p c n", c=DC) for j in range(2))
            with ExitStack() as ctx:
                sort_phases(k, ctx)
            node_phases(k, sums)


def sort_phases(k, ctx):
    nc, A = k.nc, k.A
    sb = lambda name, shape, dt=F32: k.sb(name, shape, dt, ctx)
    s = Shared()
    s.dst = sb("dst", [P, EDGE_COLS], I32)
    s.ew = sb("ew", [P, EDGE_COLS])
    s.block_f = sb("block_f", [P, EDGE_COLS])
    s.local_f = sb("local_f", [P, EDGE_COLS])
    s.wkv = sb("wkv", [P, DC, 2 * D])
    s.bkv = sb("bkv", [1, 2 * D])
    s.valid = sb("valid", [P, BLOCKS])
    s.keep = sb("keep", [P, BLOCKS, SLOTS])
    s.onehot = sb("onehot", [P, 2, BLOCKS, SLOTS])
    s.count = sb("count", [P, 2, BLOCKS, SLOTS])
    setup(k, s)
    k.phase_done()
    sort_and_kv(k, s)
    k.phase_done()


def setup(k, s):
    nc, A = k.nc, k.A
    with ExitStack() as ctx:
        sb = lambda name, shape, dt=F32: k.sb(name, shape, dt, ctx)
        room = k.acc[:, :, :].rearrange("p t d -> p (t d)")
        taken = [0]

        def lent(columns, dt=F32):
            taken[0] += columns
            return room[:, taken[0] - columns:taken[0]].bitcast(dt)

        src, block_i, local_i = (lent(EDGE_COLS, I32) for _ in range(3))
        zero = lent(TILES * 2, I32)
        block_b = lent(EDGE_COLS // 2, BF16)
        hits, signs = (lent(EDGE_COLS, BF16).rearrange("p (u n) -> p u n", u=2) for _ in range(2))
        gcn_W = sb("gcn_W", [P, DC, D])
        gcn_W1 = sb("gcn_W1", [P, DC, D])
        gcn_b = sb("gcn_b", [P, DC])
        gcn_b1 = sb("gcn_b1", [P, DC])
        wqkv = sb("wqkv", [P, DC, 3 * D])
        bqkv = sb("bqkv", [1, 3 * D])
        wq = sb("wq", [P, DC, D])
        gcn_WT = sb("gcn_WT", [P, DC, D])
        kv_mean = sb("kv_mean", [P, DC, 2, HEADS])
        b_mean = sb("b_mean", [1, 2, HEADS])
        tri = sb("tri", [P, P])
        iota_i = sb("iota_i", [P, P], I32)
        BY_DVE = 64
        BY_ACT = BLOCKS - BY_DVE
        assert BY_DVE % 2 == 0 and BY_ACT % 2 == 0
        HIST_CREDIT = 2
        half_less_b = sb("half_less_b", [P, BY_ACT + 2])
        sign_sum = sb("sign_sum", [P, BY_ACT + 2])
        sign_fall = sb("sign_fall", [P, BY_ACT])
        cnt = sb("cnt", [P, BLOCKS])
        total_i = sb("total_i", [P, BLOCKS], I32)
        tiles_i = sb("tiles_i", [P, BLOCKS], I32)
        tiles_f = sb("tiles_f", [P, BLOCKS])
        tile_end = sb("tile_end", [P, BLOCKS])
        tile_start = sb("tile_start", [P, BLOCKS])
        step_tile_i = sb("step_tile_i", [P, STEP_TILES], I32)
        step_tile = sb("step_tile", [P, STEP_TILES])
        step_hits = sb("step_hits", [P, 2, BLOCKS])
        begun = sb("begun", [P, STEP_TILES])
        grows = sb("grows", [P, STEP_TILES])
        pow2 = sb("pow2", [P, STEP_TILES])
        word_f = sb("word_f", [P, 1])
        word_i = sb("word_i", [P, 1], I32)
        psW = k.ps("psW", [P, 2, 512], ctx)
        psO = k.ps("psO", [P, 512], ctx)
        psC = k.ps("psC", [P, 512], ctx)

        src_in, ew_in, small_in, big_in = (k.sem(n) for n in ("src_in", "ew_in", "small_in", "big_in"))
        iota_made, consts_made, diag_made = k.sem("iota_made"), k.sem("consts_made"), k.sem("diag_made")
        zero_made, zeroed = k.sem("zero_made"), k.sem("zeroed")
        split_done, hist_done, offs = k.sem("split_done"), k.sem("hist_done"), k.sem("offs")
        block_b_made, signs_done = k.sem("block_b_made"), k.sem("signs_done")
        prefix_done, wT_ready, wT_copied = k.sem("prefix_done"), k.sem("wT_ready"), k.sem("wT_copied")
        folded, fold_copied, wq_ready = k.sem("folded"), k.sem("fold_copied"), k.sem("wq_ready")
        centred, words_ready = k.sem("centred"), k.sem("words_ready")
        words_out, words_in = k.sem("words_out"), k.sem("words_in")

        rows = lambda w: w.rearrange("(c p) n -> p c n", p=P)
        col = lambda b: b.rearrange("(c p) -> p c", p=P)
        heads_q = A["b_qkv"].rearrange("(h t e) -> h t e", t=3, e=HEADC)

        with nc.Block() as block:
            @block.sync
            def _(sp):
                sp.dma_start(src, A["src"]).then_inc(src_in, 16)
                sp.dma_start(s.dst[:, :], A["dst"]).then_inc(ew_in, 16)
                sp.dma_start(s.ew[:, :], A["ew"]).then_inc(ew_in, 16)
                for dst, w in ((gcn_W, A["gnn_W"]), (gcn_W1, A["gnn_W1"]), (wqkv, A["w_qkv"]), (k.gcn_w2, A["gnn_W2"]),
                               (k.mix_w1, A["mix_w1"]), (k.mix_w2, A["mix_w2"])):
                    sp.dma_start(dst[:, :, :], rows(w)).then_inc(big_in, 16)
                sp.wait_ge(zero_made, 1)
                sp.dma_start(k.records.rearrange("(p t) w -> p (t w)", p=P), zero).then_inc(zeroed, 16)
                pad = zero[:, 0:AHEAD * D].bitcast(F32).rearrange("p (t d) -> p t d", d=D)
                for behind in (k.xn_dram, k.part_dram):
                    sp.dma_start(behind[NODES:, :].rearrange("(t p) d -> p t d", p=P), pad).then_inc(zeroed, 16)
                sp.wait_ge(words_ready, 1)
                sp.dma_start(k.words_dram, word_i[0:STEPS, :]).then_inc(words_out, 16)
                sp.wait_ge(words_out, 16)
                sp.dma_start(k.words[:, :], k.words_dram.rearrange("b o -> o b")).then_inc(words_in, 16)
                sp.wait_ge(words_in, 16)
                sp.wait_ge(zeroed, 48)

            @block.scalar
            def _(act):
                with nc.allow_non_contiguous_dma(reason="columns of a few hundred words"):
                    for dst, b in ((gcn_b, A["gnn_b"]), (gcn_b1, A["gnn_b1"]), (k.mix_b1, A["mix_b1"])):
                        act.dma_start(dst[:, :], col(b)).then_inc(small_in, 16)
                    act.dma_start(bqkv[:, :], A["b_qkv"].rearrange("(a n) -> a n", a=1)).then_inc(small_in, 16)
                    act.dma_start(k.bias_sum, A["gnn_b2"].partition_broadcast(P)).then_inc(small_in, 16)
                    act.dma_start(k.bias_tmp, A["mix_b2"].partition_broadcast(P)).then_inc(small_in, 16)
                    act.dma_start(k.k_gb[:, 0, :], A["kln_g"].partition_broadcast(P)).then_inc(small_in, 16)
                    act.dma_start(k.k_gb[:, 1, :], A["kln_b"].partition_broadcast(P)).then_inc(small_in, 16)
                    for j, v in enumerate((A["vln_g"], A["vln_b"])):
                        for h in range(HEADS_PER_CHUNK):
                            act.dma_start(k.kv_gb[h * HEADC:(h + 1) * HEADC, j:j + 1],
                                          v.rearrange("(e o) -> e o", o=1)).then_inc(small_in, 16)
                    for c in range(DC):
                        for h in range(HEADS_PER_CHUNK):
                            act.dma_start(k.bq[h * HEADC:(h + 1) * HEADC, c:c + 1],
                                          heads_q[c * HEADS_PER_CHUNK + h, 0:1, :].rearrange("o e -> e o")
                                          ).then_inc(small_in, 16)
                act.wait_ge(block_b_made, 2)

                def sum_signs(n, u):
                    start_after(act, signs_done, n - 1)
                    act.activation(signs[:, u, :], block_b, ACT.Sign, bias=half_less_b[:, bass.ds(n, 1)],
                                   accum_out=sign_sum[:, bass.ds(n, 1)]).then_inc(signs_done, 1)

                for u in range(2):
                    sum_signs(u, u)
                with act.Fori(1, BY_ACT // 2 + 1) as i:
                    for u in range(2):
                        sum_signs(2 * i + u, u)
                for w, dst in enumerate((gcn_WT, k.wqT)):
                    act.wait_ge(wT_ready, w + 1)
                    act.activation(dst[:, :, :], psW[:, :, 0:D], ACT.Copy).then_inc(wT_copied, 1)
                act.wait_ge(folded, 1)
                act.activation(k.gcn_w[:, :, :], psO[:, :].rearrange("p (c n) -> p c n", c=DC),
                               ACT.Copy).then_inc(fold_copied, 1)

            @block.gpsimd
            def _(pool):
                pool.iota(iota_i[:, :], pattern=[[1, P]], base=0, channel_multiplier=0).then_inc(iota_made, 1)
                pool.iota(step_tile_i[:, :], pattern=[[1, STEP_TILES]], base=0,
                          channel_multiplier=STEP_TILES).then_inc(iota_made, 1)
                pool.memset(zero, 0).then_inc(zero_made, 1)
                pool.memset(k.ones[:, :], 1.0).then_inc(consts_made, 1)
                pool.memset(k.ident[:, :], 0.0).then_inc(consts_made, 1)
                pool.memset(tri[:, :], 1.0).then_inc(consts_made, 1)
                pool.memset(s.valid[:, :], 1.0).then_inc(consts_made, 1)
                pool.memset(k.eps[:, :], EPS).then_inc(consts_made, 1)
                pool.memset(s.keep[:, :, 1:], 1.0).then_inc(consts_made, 1)
                pool.memset(s.keep[:, :, 0:1], 0.0).then_inc(consts_made, 1)
                pool.wait_ge(consts_made, 7)
                pool.affine_select(out=k.ident[:, :], in_=k.ident[:, :], compare_op=ALU.not_equal, fill=1.0,
                                   base=0, pattern=[[-1, P]], channel_multiplier=1).then_inc(diag_made, 1)
                pool.affine_select(out=tri[:, :], in_=tri[:, :], compare_op=ALU.is_gt, fill=0.0,
                                   base=0, pattern=[[1, P]], channel_multiplier=-1).then_inc(diag_made, 1)
                pool.affine_select(out=s.valid[:, :], in_=s.valid[:, :], compare_op=ALU.is_ge, fill=0.0,
                                   base=N_NODES - 1, pattern=[[-P, BLOCKS]],
                                   channel_multiplier=-1).then_inc(diag_made, 1)

            @block.vector
            def _(dve):
                dve.wait_ge(iota_made, 2)
                dve.tensor_copy(k.iota_row[:, :], iota_i[:, :]).then_inc(split_done, 1)
                dve.tensor_copy(step_tile[:, :], step_tile_i[:, :]).then_inc(split_done, 1)
                dve.wait_ge(src_in, 16)
                dve.tensor_scalar(block_i, src, 7, None, ALU.arith_shift_right).then_inc(split_done, 1)
                dve.tensor_scalar(local_i, src, P - 1, None, ALU.bitwise_and).then_inc(split_done, 1)
                dve.wait_ge(split_done, 4)
                dve.tensor_copy(s.block_f[:, :], block_i).then_inc(split_done, 1)
                dve.tensor_copy(block_b, block_i).then_inc(block_b_made, 1)
                dve.tensor_scalar(half_less_b[:, :], k.iota_row[:, BY_DVE:BLOCKS + 2], -1.0, 0.5, ALU.mult,
                                  ALU.add).then_inc(block_b_made, 1)
                dve.tensor_copy(s.local_f[:, :], local_i).then_inc(split_done, 1)
                dve.wait_ge(split_done, 6)
                dve.tensor_scalar(src, local_i, DST_BITS, None,
                                  ALU.logical_shift_left).then_inc(split_done, 1)
                dve.wait_ge(split_done, 7)
                dve.wait_ge(ew_in, 32)
                dve.tensor_tensor(s.dst[:, :], src, s.dst[:, :], ALU.bitwise_or).then_inc(split_done, 1)
                dve.wait_ge(split_done, 8)
                dve.wait_ge(block_b_made, 2)
                dve.sem_inc(hist_done, HIST_CREDIT)
                with dve.Fori(0, BY_DVE // 2) as i:
                    for u in range(2):
                        dve.wait_ge(hist_done, 2 * i + u - 1 + HIST_CREDIT)
                        dve.tensor_scalar(hits[:, u, :], block_b, k.iota_row[:, bass.ds(2 * i + u, 1)], 0.0,
                                          ALU.is_equal, ALU.add,
                                          accum_out=cnt[:, bass.ds(2 * i + u, 1)]).then_inc(hist_done, 1)
                dve.wait_ge(signs_done, BY_ACT + 2)
                dve.tensor_tensor(sign_fall[:, :], sign_sum[:, 0:BY_ACT], sign_sum[:, 1:BY_ACT + 1], ALU.subtract).then_inc(split_done, 1)
                dve.wait_ge(split_done, 9)
                dve.tensor_scalar(cnt[:, BY_DVE:], sign_fall[:, :], 0.5, None, ALU.mult).then_inc(hist_done, 1)
                dve.wait_ge(big_in, 6 * 16)
                dve.wait_ge(small_in, 16 * N_SMALL_DMAS)
                view = wqkv[:, :, :].rearrange("p c (h t e) -> p c t h e", t=3, e=HEADC)
                for c in range(DC):
                    dve.tensor_copy(wq[:, c, :].rearrange("p (h e) -> p h e", e=HEADC),
                                    view[:, c, 0, :, :]).then_inc(wq_ready, 1)
                for c in range(DC):
                    for t in range(2):
                        dve.tensor_reduce(kv_mean[:, c, t, :], view[:, c, 1 + t, :, :], AX.X, ALU.add).then_inc(centred, 1)
                bview = bqkv[:, :].rearrange("p (h t e) -> p t h e", t=3, e=HEADC)
                for t in range(2):
                    dve.tensor_reduce(b_mean[:, t, :], bview[:, 1 + t, :, :], AX.X, ALU.add).then_inc(centred, 1)
                dve.wait_ge(centred, 2 * DC + 2)
                for c in range(DC):
                    for t in range(2):
                        dve.scalar_tensor_tensor(
                            out=s.wkv[:, c, t * D:(t + 1) * D].rearrange("p (h e) -> p h e", e=HEADC),
                            in0=kv_mean[:, c, t, :].unsqueeze(2).to_broadcast([P, HEADS, HEADC]), scalar=-1.0 / HEADC,
                            in1=view[:, c, 1 + t, :, :], op0=ALU.mult, op1=ALU.add).then_inc(centred, 1)
                for t in range(2):
                    dve.scalar_tensor_tensor(
                        out=s.bkv[:, t * D:(t + 1) * D].rearrange("p (h e) -> p h e", e=HEADC),
                        in0=b_mean[:, t, :].unsqueeze(2).to_broadcast([1, HEADS, HEADC]), scalar=-1.0 / HEADC,
                        in1=bview[:, 1 + t, :, :], op0=ALU.mult, op1=ALU.add).then_inc(centred, 1)
                dve.tensor_tensor(k.bias_sum, k.bias_sum, k.bias_tmp, ALU.add).then_inc(centred, 1)
                dve.wait_ge(folded, 2)
                dve.tensor_tensor(k.gcn_c[:, :], psC[:, 256:256 + DC], gcn_b1[:, :], ALU.add).then_inc(fold_copied, 1)
                dve.wait_ge(prefix_done, 1)
                dve.tensor_scalar(total_i[:, :], psC[:, 128:128 + BLOCKS], float(P - 1), None, ALU.add).then_inc(offs, 1)
                dve.wait_ge(offs, 1)
                dve.tensor_scalar(tiles_i[:, :], total_i[:, :], 7, None, ALU.arith_shift_right).then_inc(offs, 1)
                dve.wait_ge(offs, 2)
                dve.tensor_scalar(tiles_f[:, :], tiles_i[:, :], 1.0, None, ALU.max).then_inc(offs, 1)
                dve.wait_ge(offs, 3)
                dve.tensor_tensor_scan(tile_end[:, :], k.ones[:, 0:BLOCKS], tiles_f[:, :], 0.0,
                                       ALU.mult, ALU.add).then_inc(offs, 1)
                dve.wait_ge(offs, 4)
                dve.tensor_tensor(tile_start[:, :], tile_end[:, :], tiles_f[:, :], ALU.subtract).then_inc(offs, 1)
                dve.wait_ge(offs, 5)
                dve.scalar_tensor_tensor(out=s.count[:, 1, :, SLOTS - 1], in0=tile_start[:, :], scalar=float(P),
                                         in1=psC[:, 0:BLOCKS], op0=ALU.mult, op1=ALU.add).then_inc(offs, 1)
                for t in range(STEP_TILES):
                    if t >= 2:
                        dve.wait_ge(offs, 6 + t - 1)
                    dve.tensor_scalar(step_hits[:, t % 2, :], tile_start[:, :], step_tile[:, t:t + 1], 0.0, ALU.is_le,
                                      ALU.add, accum_out=begun[:, t:t + 1]).then_inc(offs, 1)
                for t in range(1, STEP_TILES):
                    dve.memset(pow2[:, t:t + 1], float(1 << (t - 1))).then_inc(offs, 1)
                dve.memset(pow2[:, 0:1], float(1 << STEP_TILES)).then_inc(offs, 1)
                n = 6 + 2 * STEP_TILES
                dve.wait_ge(offs, n)
                dve.tensor_tensor(grows[:, 1:], begun[:, 1:], begun[:, 0:STEP_TILES - 1], ALU.subtract).then_inc(offs, 1)
                dve.tensor_scalar(grows[:, 0:1], begun[:, 0:1], -1.0, None, ALU.add).then_inc(offs, 1)
                dve.wait_ge(offs, n + 2)
                dve.tensor_tensor(begun[:, :], grows[:, :], pow2[:, :], ALU.mult).then_inc(offs, 1)
                dve.wait_ge(offs, n + 3)
                dve.tensor_reduce(word_f[:, :], begun[:, :], AX.X, ALU.add).then_inc(offs, 1)
                dve.wait_ge(offs, n + 4)
                dve.tensor_copy(word_i[:, :], word_f[:, :]).then_inc(words_ready, 1)

            @block.tensor
            def _(pe):
                pe.wait_ge(diag_made, 3)
                pe.wait_ge(big_in, 6 * 16)
                pe.wait_ge(small_in, 16 * N_SMALL_DMAS)
                for j in range(DC):
                    for c in range(DC):
                        last = pe.transpose(psW[:, j, c * P:(c + 1) * P], gcn_W[:, c, j * P:(j + 1) * P], k.ident[:, :])
                last.then_inc(wT_ready, 1)
                pe.wait_ge(wT_copied, 1)
                for c in range(DC):
                    for j in range(DC):
                        last = pe.matmul(psO[:, c * D:(c + 1) * D], gcn_WT[:, j, c * P:(c + 1) * P], gcn_W1[:, j, :],
                                         start=(j == 0), stop=(j == DC - 1))
                last.then_inc(folded, 1)
                for f in range(DC):
                    for j in range(DC):
                        last = pe.matmul(psC[:, 256 + f:257 + f], gcn_W1[:, j, f * P:(f + 1) * P], gcn_b[:, j:j + 1],
                                         start=(j == 0), stop=(j == DC - 1))
                last.then_inc(folded, 1)
                pe.wait_ge(wq_ready, DC)
                for j in range(DC):
                    for c in range(DC):
                        last = pe.transpose(psW[:, j, c * P:(c + 1) * P], wq[:, c, j * P:(j + 1) * P], k.ident[:, :])
                last.then_inc(wT_ready, 1)
                pe.wait_ge(hist_done, BY_DVE + 1 + HIST_CREDIT)
                pe.wait_ge(fold_copied, 2)
                pe.matmul(psC[:, 0:BLOCKS], tri[:, :], cnt[:, :], start=True, stop=True)
                pe.matmul(psC[:, 128:128 + BLOCKS], k.ones[:, :], cnt[:, :], start=True, stop=True).then_inc(prefix_done, 1)


N_SMALL_DMAS = 3 + 1 + 2 + 2 + 2 * HEADS_PER_CHUNK + DC * HEADS_PER_CHUNK


def sort_and_kv(k, s):
    nc, A = k.nc, k.A
    ctx = ExitStack()
    with ctx:
        sb = lambda name, shape, dt=F32: k.sb(name, shape, dt, ctx)
        x = sb("x", [P, 2, D])
        xn = sb("xn", [P, 2, D])
        xT = sb("xT", [P, DC, P])
        stats = sb("stats", [P, 2, 6])
        mv = sb("mv", [P, 2, 2])
        std = sb("std", [P, 2])
        rstd = sb("rstd", [P, 2])
        picked = sb("picked", [P, BLOCKS, COLS])
        rank = sb("rank", [P, COLS])
        pos = sb("pos", [P, COLS], I32)
        lane = sb("lane", [P, COLS], I32)
        tile = sb("tile", [P, COLS], I32)
        addr = sb("addr", [P, 2, COLS], I32)
        rec = sb("rec", [P, 2, COLS, 2], I32)
        local = sb("local", [P, COLS, P])
        sq = sb("sq", [P, 2 * D])
        ss = sb("ss", [P, 2 * HEADS])
        sd = sb("sd", [P, 2 * HEADS])
        rs = sb("rs", [P, 2 * HEADS])
        rsv = sb("rsv", [P, 2 * HEADS])
        kv = sb("kv", [P, 2 * D])
        zeros = sb("zeros", [P, 512])
        ps_xT = k.ps("ps_xT", [P, 512], ctx)
        ps_kv = k.ps("ps_kv", [P, 512], ctx)
        ps_deg = k.ps("ps_deg", [P, 512], ctx)
        ps_sum = k.ps("ps_sum", [P, 512], ctx)
        DEG = ps_deg[:, 0:BLOCKS]
        VSUM = ps_deg[:, 128:128 + DC]
        VK = ps_sum[:, 0:D]
        KSUM = ps_sum[:, D:2 * D]

        x_in = [k.sem(f"x_in{h}") for h in range(2)]
        xn_out = [k.sem(f"xn_out{h}") for h in range(2)]
        scattered = [k.sem(f"scattered{h}") for h in range(2)]
        (zeros_made, stats_done, mv_done, std_done, rstd_done, xn_done, slot0_done, onehot_done, count_done,
         picked_done, rank_done, pos_done, split2_done, addr_done, rec_done, local_done, deg_done, xT_done,
         xT_copied, kv_done, sq_done, ss_done, sd_done, rs_done, rsv_done, kvn_done, sums_done, all_summed,
         sums_out, pool_held, row_kept) = (
            k.sem(name) for name in ("zeros_made stats_done mv_done std_done rstd_done xn_done slot0_done onehot_done count_done "
            "picked_done rank_done pos_done split2_done addr_done rec_done local_done deg_done xT_done "
            "xT_copied kv_done sq_done ss_done sd_done rs_done rsv_done kvn_done sums_done all_summed sums_out "
            "pool_held row_kept").split())
        DEG_CREDIT = 1

        def is_first(n):
            return isinstance(n, int) and n == 0

        def steps(eng, step):
            for h in range(2):
                step(h, h, 0)
            with eng.Fori(1, PAIRS) as i:
                for h in range(2):
                    step(2 * i + h, h, i)

        x_blocks = A["x"].rearrange("(t p) d -> p t d", p=P)
        xn_blocks = k.xn_dram.rearrange("(t p) d -> p t d", p=P)

        with nc.Block() as block:
            @block.sync
            def _(sp):
                for h in range(AHEAD):
                    sp.dma_start(x[:, h, :], x_blocks[:, h, :]).then_inc(x_in[h], 16)
                with sp.Fori(0, PAIRS) as i:
                    for h in range(2):
                        n = 2 * i + h
                        sp.wait_ge(xn_done, n + 1)
                        sp.dma_start(xn_blocks[:, bass.ds(n, 1), :], xn[:, h:h + 1, :]).then_inc(xn_out[h], 16)
                        sp.dma_start(x[:, h:h + 1, :], x_blocks[:, bass.ds(n + AHEAD, 1), :]).then_inc(x_in[h], 16)
                for h in range(2):
                    sp.wait_ge(x_in[h], 16 * (PAIRS + 1))
                for h in range(2):
                    sp.wait_ge(xn_out[h], 16 * PAIRS)

            @block.gpsimd
            def _(pool):
                with pool.Fori(0, PAIRS) as i:
                    for h in range(2):
                        pool.wait_ge(addr_done, 2 * i + h + 1)
                        pool.wait_ge(rec_done, 2 * (2 * i + h) + 2)
                        pool.sem_inc(pool_held, 1)
                        for c in range(COLS):
                            pool.indirect_dma_start(
                                out=k.records, out_offset=bass.IndirectOffsetOnAxis(addr[:, h, c:c + 1], 0),
                                in_=rec[:, h, c, :], in_offset=None, bounds_check=P * TILES - 1,
                                oob_is_err=False).then_inc(scattered[h], 16)
                for h in range(2):
                    pool.wait_ge(scattered[h], 16 * COLS * PAIRS)

            @block.scalar
            def _(act):
                def deviations(n):
                    act.wait_ge(ss_done, n + 1)
                    start_after(act, rs_done, n)
                    act.activation(sd[:, :], ss[:, :], ACT.Sqrt, bias=k.eps[:, :], scale=1.0 / HEADC).then_inc(sd_done, 1)

                def step(n, h, i):
                    act.wait_ge(mv_done, n + 1)
                    act.activation(std[:, h:h + 1], mv[:, h, 1:2], ACT.Sqrt, bias=k.eps[:, :]).then_inc(std_done, 1)
                    if not is_first(n):
                        deviations(n - 1)
                    act.wait_ge(xn_done, n + 1)
                    act.activation(k.acc[:, bass.ds(n, 1), :], xn[:, h:h + 1, :], ACT.Identity).then_inc(row_kept, 1)
                    act.wait_ge(xT_done, n + 1)
                    start_after(act, kv_done, n)
                    act.activation(xT[:, :, :], ps_xT[:, 0:D].rearrange("p (c n) -> p c n", c=DC),
                                   ACT.Identity).then_inc(xT_copied, 1)
                    act.wait_ge(kv_done, n + 1)
                    start_after(act, ss_done, n)
                    act.activation(sq[:, :], ps_kv[:, :], ACT.Square).then_inc(sq_done, 1)

                steps(act, step)
                deviations(BLOCKS - 1)
                act.wait_ge(all_summed, 1)
                act.activation(k.deg[:, :], DEG, ACT.Identity).then_inc(sums_out, 1)
                act.activation(k.vsum[:, :], VSUM, ACT.Identity).then_inc(sums_out, 1)
                act.activation(k.vk, VK.rearrange("p (c n) -> p c n", c=DC), ACT.Identity).then_inc(sums_out, 1)
                act.activation(k.ksum, KSUM.rearrange("p (c n) -> p c n", c=DC), ACT.Identity).then_inc(sums_out, 1)

            @block.vector
            def _(dve):
                dve.memset(zeros[:, :], 0.0).then_inc(zeros_made, 1)

                def squares(n):
                    dve.wait_ge(sq_done, n + 1)
                    start_after(dve, sd_done, n)
                    dve.tensor_reduce(ss[:, :], sq[:, :].rearrange("p (g e) -> p g e", e=HEADC), AX.X,
                                      ALU.add).then_inc(ss_done, 1)

                def inverses(n):
                    dve.wait_ge(sd_done, n + 1)
                    dve.reciprocal(rs[:, :], sd[:, :]).then_inc(rs_done, 1)

                def masked(n):
                    dve.wait_ge(rs_done, n + 1)
                    dve.tensor_scalar(rsv[:, :], rs[:, :], s.valid[:, bass.ds(n, 1)], None, ALU.mult).then_inc(rsv_done, 1)

                def scaled(n):
                    dve.wait_ge(rsv_done, n + 1)
                    start_after(dve, sums_done, n)
                    dve.tensor_tensor(kv[:, :].rearrange("p (g e) -> p g e", e=HEADC),
                                      ps_kv[:, :].rearrange("p (g e) -> p g e", e=HEADC),
                                      rsv[:, :].unsqueeze(2).to_broadcast([P, 2 * HEADS, HEADC]),
                                      ALU.mult).then_inc(kvn_done, 1)

                def step(n, h, i):
                    before = (lambda stage: None) if is_first(n) else (lambda stage: stage(n - 1))
                    dve.wait_ge(x_in[h], 16 * (i + 1))
                    dve.bn_stats(stats[:, h, :], x[:, h, :]).then_inc(stats_done, 1)
                    dve.wait_ge(deg_done, n - 1 + DEG_CREDIT)
                    start_after(dve, rank_done, n)
                    dve.tensor_copy(s.onehot[:, h, :, 0], s.count[:, 1 - h, :, SLOTS - 1]).then_inc(slot0_done, 1)
                    dve.tensor_tensor(
                        s.onehot[:, h, :, 1:],
                        k.iota_row[:, 0:BLOCKS].unsqueeze(2).to_broadcast([P, BLOCKS, COLS]),
                        s.block_f[:, bass.ds(n * COLS, COLS)].unsqueeze(1).to_broadcast([P, BLOCKS, COLS]),
                        ALU.is_equal).then_inc(onehot_done, 1)
                    before(squares)
                    dve.wait_ge(stats_done, n + 1)
                    dve.wait_ge(onehot_done, n + 1)
                    dve.tensor_tensor_scan(s.count[:, h, :, :].rearrange("p b c -> p (b c)"),
                                           s.keep[:, :, :].rearrange("p b c -> p (b c)"),
                                           s.onehot[:, h, :, :].rearrange("p b c -> p (b c)"), 0.0,
                                           ALU.mult, ALU.add).then_inc(count_done, 1)
                    dve.bn_aggr(mv[:, h, :], stats[:, h, :]).then_inc(mv_done, 1)
                    before(inverses)
                    dve.wait_ge(count_done, n + 1)
                    dve.tensor_tensor(picked[:, :, :], s.onehot[:, h, :, 1:], s.count[:, h, :, 1:],
                                      ALU.mult).then_inc(picked_done, 1)
                    dve.wait_ge(std_done, n + 1)
                    dve.reciprocal(rstd[:, h:h + 1], std[:, h:h + 1]).then_inc(rstd_done, 1)
                    before(masked)
                    start_after(dve, row_kept, n - 1)
                    start_after(dve, xn_out[h], 16 * i)
                    start_after(dve, xT_done, n)
                    dve.wait_ge(rstd_done, n + 1)
                    dve.tensor_scalar(xn[:, h, :], x[:, h, :], mv[:, h, 0:1], rstd[:, h:h + 1], ALU.subtract,
                                      ALU.mult).then_inc(xn_done, 1)
                    dve.wait_ge(picked_done, n + 1)
                    dve.tensor_reduce(rank[:, :], picked[:, :, :].rearrange("p b c -> p c b"), AX.X,
                                      ALU.add).then_inc(rank_done, 1)
                    before(scaled)
                    dve.wait_ge(rank_done, n + 1)
                    dve.tensor_scalar(pos[:, :], rank[:, :], -1.0, None, ALU.add).then_inc(pos_done, 1)
                    start_after(dve, scattered[h], 16 * COLS * i)
                    dve.tensor_copy(rec[:, h, :, 0], s.dst[:, bass.ds(n * COLS, COLS)]).then_inc(rec_done, 1)
                    dve.tensor_copy(rec[:, h, :, 1], s.ew[:, bass.ds(n * COLS, COLS)].bitcast(I32)).then_inc(rec_done, 1)
                    dve.wait_ge(pos_done, n + 1)
                    dve.tensor_scalar(lane[:, :], pos[:, :], P - 1, None, ALU.bitwise_and).then_inc(split2_done, 1)
                    dve.tensor_scalar(tile[:, :], pos[:, :], 7, None, ALU.logical_shift_right).then_inc(split2_done, 1)
                    dve.wait_ge(split2_done, 2 * n + 2)
                    dve.scalar_tensor_tensor(out=addr[:, h, :], in0=lane[:, :], scalar=float(TILES), in1=tile[:, :],
                                             op0=ALU.mult, op1=ALU.add).then_inc(addr_done, 1)
                    dve.wait_ge(deg_done, n + DEG_CREDIT)
                    for c in range(COLS):
                        dve.tensor_scalar(local[:, c, :], k.iota_row[:, :], s.local_f[:, bass.ds(n * COLS + c, 1)],
                                          s.ew[:, bass.ds(n * COLS + c, 1)], ALU.is_equal,
                                          ALU.mult).then_inc(local_done, 1)

                steps(dve, step)
                for stage in (squares, inverses, masked, scaled):
                    stage(BLOCKS - 1)

            @block.tensor
            def _(pe):
                acc = dict(start=False, stop=False, skip_group_check=True)
                pe.wait_ge(zeros_made, 1)
                for bank in (ps_deg, ps_sum):
                    pe.matmul(bank[:, :], zeros[:, 0:P], zeros[:, :], start=True, stop=False, skip_group_check=True)
                pe.sem_inc(deg_done, DEG_CREDIT)

                def sums(n):
                    pe.wait_ge(kvn_done, n + 1)
                    for c in range(DC):
                        v = kv[:, D + c * P:D + (c + 1) * P]
                        pe.matmul(VK[:, c * P:(c + 1) * P], v, kv[:, c * P:(c + 1) * P], **acc)
                        pe.matmul(VSUM[:, c:c + 1], v, k.ones[:, 0:1], **acc)
                    pe.matmul(KSUM, k.ones[:, :], kv[:, 0:D], **acc).then_inc(sums_done, 1)

                def step(n, h, i):
                    pe.wait_ge(xn_done, n + 1)
                    start_after(pe, xT_copied, n)
                    for c in range(DC):
                        last = pe.transpose(ps_xT[:, c * P:(c + 1) * P], xn[:, h, c * P:(c + 1) * P], k.ident[:, :])
                    last.then_inc(xT_done, 1)
                    if not is_first(n):
                        sums(n - 1)
                    pe.wait_ge(xT_copied, n + 1)
                    start_after(pe, kvn_done, n)
                    for c in range(DC):
                        pe.matmul(ps_kv[:, :], xT[:, c, :], s.wkv[:, c, :], start=(c == 0), stop=False)
                    pe.matmul(ps_kv[:, :], k.ones[0:1, :], s.bkv[0:1, :], start=False, stop=True).then_inc(kv_done, 1)
                    pe.wait_ge(onehot_done, n + 1)
                    for c in range(COLS):
                        pe.wait_ge(local_done, n * COLS + c + 1)
                        last = pe.matmul(DEG, local[:, c, :], s.onehot[:, h, :, 1 + c], **acc)
                    last.then_inc(deg_done, 1)

                steps(pe, step)
                sums(BLOCKS - 1)
                for bank in (ps_deg, ps_sum):
                    last = pe.matmul(bank[:, :], zeros[:, 0:P], zeros[:, :], start=False, stop=True, skip_group_check=True)
                last.then_inc(all_summed, 1)


def degrees_and_weights(k):
    nc, A = k.nc, k.A
    BY_ACT = 4
    with ExitStack() as ctx:
        sb = lambda name, shape, dt=F32: k.sb(name, shape, dt, ctx)
        deg1 = sb("deg1", [P, BLOCKS])
        positive = sb("positive", [P, BLOCKS])
        guarded = sb("guarded", [P, BLOCKS])
        root = sb("root", [P, BLOCKS])
        inverse = sb("inverse", [P, BLOCKS])
        headmask = sb("headmask", [P, P])
        t1 = sb("t1", [P, DC, P])
        t2 = sb("t2", [P, DC, P])
        t3 = sb("t3", [P, DC, P])
        col = sb("col", [P, DC])
        kvT = sb("kvT", [P, DC, P])
        B = sb("B", [P, DC, D])
        ps_B = k.ps("ps_B", [P, 512], ctx)
        ps_M = k.ps("ps_M", [P, 512], ctx)
        ps_c = k.ps("ps_c", [P, 512], ctx)
        put = k.sem("put")
        (deg_step, root_done, dinv_done, act_scaled, dve_scaled, mask_made, kv_step, kvT_done, B_done, B_copied, M_done) = (
            k.sem(name) for name in ("deg_step root_done dinv_done act_scaled dve_scaled mask_made kv_step kvT_done B_done B_copied M_done").split())
        dst = k.table.rearrange("(t p) d -> p t d", p=P)

        with nc.Block() as block:
            @block.sync
            def _(sp):
                for c in range(CHUNKS):
                    sp.wait_ge(act_scaled, (c + 1) * BY_ACT)
                    sp.wait_ge(dve_scaled, (c + 1) * (CHUNK - BY_ACT))
                    sp.dma_start(dst[:, c * CHUNK:(c + 1) * CHUNK, :], k.acc[:, c * CHUNK:(c + 1) * CHUNK, :]).then_inc(put, 16)
                sp.wait_ge(put, 16 * CHUNKS)

            @block.scalar
            def _(act):
                act.wait_ge(deg_step, 3)
                act.activation(root[:, :], guarded[:, :], ACT.Sqrt).then_inc(root_done, 1)
                act.wait_ge(dinv_done, 1)
                for c in range(CHUNKS):
                    for n in range(c * CHUNK, c * CHUNK + BY_ACT):
                        act.activation(k.acc[:, n, :], k.acc[:, n, :], ACT.Copy, scale=k.dinv[:, n:n + 1]).then_inc(act_scaled, 1)

            @block.gpsimd
            def _(pool):
                pool.memset(headmask[:, :], 0.0).then_inc(mask_made, 1)
                pool.wait_ge(mask_made, 1)
                for h in range(HEADS_PER_CHUNK):
                    cut = slice(h * HEADC, (h + 1) * HEADC)
                    pool.memset(headmask[cut, cut], 1.0 / N_NODES).then_inc(mask_made, 1)

            @block.vector
            def _(dve):
                dve.tensor_scalar(deg1[:, :], k.deg[:, :], 1.0, None, ALU.add).then_inc(deg_step, 1)
                dve.wait_ge(deg_step, 1)
                dve.tensor_scalar(positive[:, :], deg1[:, :], 0.0, None, ALU.is_gt).then_inc(deg_step, 1)
                dve.tensor_scalar(guarded[:, :], deg1[:, :], 2.0 ** -100, None, ALU.max).then_inc(deg_step, 1)
                dve.wait_ge(root_done, 1)
                dve.reciprocal(inverse[:, :], root[:, :]).then_inc(deg_step, 1)
                dve.wait_ge(deg_step, 4)
                dve.tensor_tensor(k.dinv[:, :], inverse[:, :], positive[:, :], ALU.mult).then_inc(dinv_done, 1)
                dve.wait_ge(dinv_done, 1)
                for c in range(CHUNKS):
                    for n in range(c * CHUNK + BY_ACT, (c + 1) * CHUNK):
                        dve.tensor_scalar(k.acc[:, n, :], k.acc[:, n, :], k.dinv[:, n:n + 1], None, ALU.mult).then_inc(dve_scaled, 1)
                g = k.k_gb[:, 0, :].unsqueeze(1).to_broadcast([P, HEADS_PER_CHUNK, HEADC])
                b = k.k_gb[:, 1, :].unsqueeze(1).to_broadcast([P, HEADS_PER_CHUNK, HEADC])
                hg, hb = k.kv_gb[:, 0:1], k.kv_gb[:, 1:2]
                by_head = lambda t, c: t[:, c, :].rearrange("p (h e) -> p h e", e=HEADC)
                dve.tensor_scalar(t1[:, :, :], k.vk[:, :, :], hg, None, ALU.mult).then_inc(kv_step, 1)
                dve.tensor_scalar(col[:, :], k.vsum[:, :], hg, None, ALU.mult).then_inc(kv_step, 1)
                dve.tensor_scalar(t3[:, 0, 0:1], hb, float(N_NODES), None, ALU.mult).then_inc(kv_step, 1)
                dve.wait_ge(kv_step, 3)
                dve.scalar_tensor_tensor(out=t2[:, :, :], in0=k.ksum[:, :, :], scalar=hb, in1=t1[:, :, :],
                                         op0=ALU.mult, op1=ALU.add).then_inc(kv_step, 1)
                dve.tensor_scalar(k.vsum[:, :], col[:, :], t3[:, 0, 0:1], None, ALU.add).then_inc(kv_step, 1)
                dve.wait_ge(kv_step, 5)
                for c in range(DC):
                    dve.tensor_tensor(by_head(t1, c), by_head(t2, c), g, ALU.mult).then_inc(kv_step, 1)
                dve.wait_ge(kv_step, 5 + DC)
                for c in range(DC):
                    dve.scalar_tensor_tensor(out=by_head(t3, c), in0=b, scalar=k.vsum[:, c:c + 1], in1=by_head(t1, c),
                                             op0=ALU.mult, op1=ALU.add).then_inc(kv_step, 1)
                dve.wait_ge(kv_step, 5 + 2 * DC)
                dve.wait_ge(mask_made, 1 + HEADS_PER_CHUNK)
                for c in range(DC):
                    dve.tensor_tensor(kvT[:, c, :], t3[:, c, :], headmask[:, :], ALU.mult).then_inc(kvT_done, 1)
                dve.wait_ge(B_done, 1)
                dve.tensor_copy(B[:, :, :], ps_B[:, :].rearrange("p (c n) -> p c n", c=DC)).then_inc(B_copied, 1)
                dve.wait_ge(M_done, 1)
                dve.tensor_tensor(k.mix_w[:, :, :], ps_M[:, :].rearrange("p (c n) -> p c n", c=DC), k.mix_w1[:, :, :],
                                  ALU.add).then_inc(kv_step, 1)
                dve.tensor_tensor(k.mix_c[:, :], ps_c[:, 0:DC], k.mix_b1[:, :], ALU.add).then_inc(kv_step, 1)

            @block.tensor
            def _(pe):
                pe.wait_ge(kvT_done, DC)
                for c in range(DC):
                    last = pe.matmul(ps_B[:, c * D:(c + 1) * D], kvT[:, c, :], k.mix_w1[:, c, :], start=True, stop=True)
                last.then_inc(B_done, 1)
                pe.wait_ge(B_copied, 1)
                for c in range(DC):
                    for j in range(DC):
                        pe.matmul(ps_M[:, c * D:(c + 1) * D], k.wqT[:, j, c * P:(c + 1) * P], B[:, j, :],
                                  start=(j == 0), stop=(j == DC - 1))
                for f in range(DC):
                    for j in range(DC):
                        last = pe.matmul(ps_c[:, f:f + 1], B[:, j, f * P:(f + 1) * P], k.bq[:, j:j + 1],
                                         start=(j == 0), stop=(j == DC - 1))
                last.then_inc(M_done, 1)


def node_phases(k, ctx):
    degrees_and_weights(k)
    k.phase_done()
    gather_and_mix(k)
    k.phase_done()
    k.gate_w = k.sb("gate_w", [P, TOP, BLOCKS], F32, ctx)
    k.pos = k.sb("pos4", [P, HALVES, TOP, HALF], I32, ctx)
    with ExitStack() as inner:
        k.up_all = k.sb("up_all", [P, N_EXPERTS, UP], F32, inner)
        k.down_all = k.sb("down_all", [P, N_EXPERTS, DOWN], F32, inner)
        k.expert_parts = lambda up, down: (
            up[:, 0:DC * HIDDEN].rearrange("p (c n) -> p c n", c=DC), up[:, DC * HIDDEN:UP],
            down[:, 0:HC * D].rearrange("p (c n) -> p c n", c=HC), down[:, HC * D:DOWN])
        k.expert_words = k.sb("expert_words", [P, X_TRIPS], I32, inner)
        k.gb = k.sb("gb", [P, 2, DC], F32, inner)
        k.weights_in = k.nc.alloc_semaphore(name="weights_in")
        k.ids = k.sb("ids", [P, X_TILES + X_UNROLL], I32, inner)
        with ExitStack() as routing:
            k.logits = k.sb("logits", [P, BLOCKS, N_EXPERTS], F32, routing)
            head(k)
            k.phase_done()
            route(k)
            k.phase_done()
        experts(k)
        k.sems.append(k.weights_in)
        k.phase_done()
    combine(k)
    k.phase_done()


def gather_and_mix(k):
    nc, A = k.nc, k.A
    with ExitStack() as ctx:
        sb = lambda name, shape, dt=F32: k.sb(name, shape, dt, ctx)
        recs = sb("recs", [P, TILES + STEP_TILES, 2], I32)
        idx = sb("idx", [P, 2, STEP_TILES], I32)
        loc_i = sb("loc_i", [P, 2, STEP_TILES], I32)
        loc = sb("loc", [P, 2, STEP_TILES])
        ewt = sb("ewt", [P, 2, STEP_TILES])
        rows = sb("rows", [P, STEP_TILES, D])
        pick = sb("pick", [P, 2, STEP_TILES, P])
        x = sb("x2", [P, 2, D])
        xn = sb("xn2", [P, 2, D])
        xT = sb("xT2", [P, DC, P])
        hT = sb("hT", [P, DC, P])
        part = sb("part", [P, 2, D])
        ps_sum = [k.ps(f"ps_seg{r}", [P, 512], ctx) for r in range(RING)]
        ps_xT = k.ps("ps_xT2", [P, 512], ctx)
        ps_h = k.ps("ps_h", [P, 512], ctx)
        ps_o = k.ps("ps_o", [P, 512], ctx)
        recs_in, cleared = k.sem("recs_in"), k.sem("cleared")
        got = [k.sem(f"row_in{t}") for t in range(STEP_TILES)]
        in_x = [k.sem(f"x2_in{h}") for h in range(2)]
        in_xn = [k.sem(f"xn2_in{h}") for h in range(2)]
        part_out = [k.sem(f"part_out{h}") for h in range(2)]
        (idx_done, loci_done, loc_done, ewt_done, pick_done, seg_done, added, xT2_done, xT2_copied, h_done,
         gelu_done, o_done, skip_done, skip2_done, part_done, gather_held) = (
            k.sem(name) for name in ("idx_done loci_done loc_done ewt_done pick_done seg_done added xT2_done xT2_copied h_done "
            "gelu_done o_done skip_done skip2_done part_done gather_held").split())
        by_block = lambda a: a.rearrange("(t p) d -> p t d", p=P)
        CREDIT, ADDED_CREDIT, OUT_CREDIT = STEP_TILES, 2 * RING, 16
        H_CREDIT, O_CREDIT, X_CREDIT, PART_CREDIT, GELU_CREDIT = 1, 1, 1, 1, DC
        loops = ((0, PAIRS, True), (PAIRS, STEPS // 2, False))

        def sums(t):
            return ps_sum[t // 2 % RING][:, t % 2 * D:t % 2 * D + D]

        with nc.Block() as block:
            @block.sync
            def _(sp):
                sp.dma_start(recs[:, 0:TILES, :], k.records.rearrange("(p t) w -> p t w", p=P)).then_inc(recs_in, 16)
                for h in range(AHEAD):
                    sp.dma_start(x[:, h, :], by_block(A["x"])[:, h, :]).then_inc(in_x[h], 16)
                    sp.dma_start(xn[:, h, :], by_block(k.xn_dram)[:, h, :]).then_inc(in_xn[h], 16)
                for h in range(2):
                    sp.sem_inc(part_out[h], OUT_CREDIT)
                with sp.Fori(0, PAIRS) as i:
                    for h in range(2):
                        n = 2 * i + h
                        sp.wait_ge(xT2_done, n + 1)
                        sp.wait_ge(skip2_done, n + 1)
                        sp.dma_start(x[:, h:h + 1, :], by_block(A["x"])[:, bass.ds(n + AHEAD, 1), :]).then_inc(in_x[h], 16)
                        sp.dma_start(xn[:, h:h + 1, :],
                                     by_block(k.xn_dram)[:, bass.ds(n + AHEAD, 1), :]).then_inc(in_xn[h], 16)
                        sp.wait_ge(part_done, n + 1 + PART_CREDIT)
                        sp.dma_start(by_block(k.part_dram)[:, bass.ds(n, 1), :], part[:, h:h + 1, :]).then_inc(part_out[h], 16)
                for h in range(2):
                    sp.wait_ge(in_x[h], 16 * (PAIRS + 1))
                    sp.wait_ge(in_xn[h], 16 * (PAIRS + 1))
                for h in range(2):
                    sp.wait_ge(part_out[h], 16 * PAIRS + OUT_CREDIT)

            @block.gpsimd
            def _(pool):
                with pool.Fori(0, STEPS // 2) as i:
                    for h in range(2):
                        pool.wait_ge(idx_done, 2 * i + h + 1)
                        for t in range(STEP_TILES):
                            pool.wait_ge(seg_done, (2 * i + h) * STEP_TILES + t + 1)
                            pool.sem_inc(gather_held, 1)
                            pool.indirect_dma_start(
                                out=rows[:, t, :], out_offset=None, in_=k.table,
                                in_offset=bass.IndirectOffsetOnAxis(idx[:, h, t:t + 1], 0),
                                bounds_check=NODES - 1, oob_is_err=False).then_inc(got[t], 16)

            @block.scalar
            def _(act):
                act.sem_inc(xT2_copied, X_CREDIT)
                act.sem_inc(gelu_done, GELU_CREDIT)
                with act.Fori(0, PAIRS) as i:
                    for h in range(2):
                        n = 2 * i + h
                        act.wait_ge(xT2_done, n + 1)
                        act.wait_ge(h_done, n + H_CREDIT)
                        act.activation(xT[:, :, :], ps_xT[:, 0:D].rearrange("p (c n) -> p c n", c=DC),
                                       ACT.Identity).then_inc(xT2_copied, 1)
                        act.wait_ge(h_done, n + 1 + H_CREDIT)
                        act.wait_ge(o_done, n + O_CREDIT)
                        for f in range(DC):
                            act.activation(hT[:, f, :], ps_h[:, f * P:(f + 1) * P], ACT.Gelu,
                                           bias=k.mix_c[:, f:f + 1]).then_inc(gelu_done, 1)

            @block.vector
            def _(dve):
                dve.memset(recs[:, TILES:, :], 0).then_inc(cleared, 1)
                dve.wait_ge(recs_in, 16)
                dve.wait_ge(cleared, 1)

                def unpack(h, n):
                    now = recs[:, bass.ds(n * STEP_TILES, STEP_TILES), :]
                    dve.tensor_scalar(idx[:, h, :], now[:, :, 0], (1 << DST_BITS) - 1, None,
                                      ALU.bitwise_and).then_inc(idx_done, 1)
                    dve.tensor_scalar(loc_i[:, h, :], now[:, :, 0], DST_BITS, None,
                                      ALU.logical_shift_right).then_inc(loci_done, 1)
                    dve.tensor_copy(ewt[:, h, :].bitcast(I32), now[:, :, 1]).then_inc(ewt_done, 1)
                    dve.wait_ge(loci_done, n + 1)
                    dve.tensor_copy(loc[:, h, :], loc_i[:, h, :]).then_inc(loc_done, 1)

                def make_pick(h, t):
                    dve.tensor_scalar(pick[:, h, t, :], k.iota_row[:, :], loc[:, h, t:t + 1], ewt[:, h, t:t + 1],
                                      ALU.is_equal, ALU.mult).then_inc(pick_done, 1)

                def block_register(value):
                    return nc.s_assert_within(dve.snap(dve.to_reg(value)), 0, BLOCKS - 1,
                                              skip_runtime_bounds_check_because="a tile's block is counted among BLOCKS")

                dve.sem_inc(added, ADDED_CREDIT)
                dve.sem_inc(part_done, PART_CREDIT)
                unpack(0, 0)
                dve.wait_ge(loc_done, 1)
                for t in range(STEP_TILES):
                    make_pick(0, t)

                def step(i, h, mlp):
                    n = 2 * i + h
                    word = dve.value_load(k.words[0:1, bass.ds(n, 1)])
                    first = n * STEP_TILES
                    dve.wait_ge(seg_done, first + CREDIT)
                    unpack(1 - h, n + 1)
                    dve.wait_ge(loc_done, n + 2)
                    blk = block_register(word >> STEP_TILES)
                    for t in range(STEP_TILES):
                        make_pick(1 - h, t)
                        if mlp and t == STEP_TILES // 2:
                            dve.wait_ge(in_x[h], 16 * (i + 1))
                            dve.wait_ge(part_out[h], 16 * i + OUT_CREDIT)
                            dve.tensor_tensor(part[:, h, :], x[:, h, :], k.bias_sum, ALU.add).then_inc(skip_done, 1)
                            dve.wait_ge(in_xn[h], 16 * (i + 1))
                            dve.wait_ge(skip_done, n + 1)
                            dve.tensor_tensor(part[:, h, :], part[:, h, :], xn[:, h, :], ALU.add).then_inc(skip2_done, 1)
                        if t % 2 == 0:
                            continue
                        dve.wait_ge(seg_done, first + t + 1 + CREDIT)
                        for u in (t - 1, t):
                            if u > 0:
                                blk = block_register(blk + ((word >> (u - 1)) & 1))
                            dve.wait_ge(added, first + u + ADDED_CREDIT)
                            here = k.acc[:, bass.ds(blk, 1), :]
                            dve.tensor_tensor(here, here, sums(u).unsqueeze(1), ALU.add).then_inc(added, 1)
                    if mlp:
                        dve.wait_ge(o_done, n + 1 + O_CREDIT)
                        dve.wait_ge(skip2_done, n + 1)
                        dve.tensor_tensor(part[:, h, :], part[:, h, :], ps_o[:, 0:D], ALU.add).then_inc(part_done, 1)

                for start, end, mlp in loops:
                    with dve.Fori(start, end) as i:
                        for h in range(2):
                            step(i, h, mlp)

            @block.tensor
            def _(pe):
                pe.sem_inc(seg_done, CREDIT)
                pe.sem_inc(h_done, H_CREDIT)
                pe.sem_inc(o_done, O_CREDIT)

                def step(i, h, mlp):
                    n = 2 * i + h
                    first = n * STEP_TILES
                    for t in range(STEP_TILES):
                        pe.wait_ge(got[t], 16 * (n + 1))
                        pe.wait_ge(pick_done, first + t + 1)
                        if t % 2 == 0:
                            pe.wait_ge(added, first + t + 2 - 2 * RING + ADDED_CREDIT)
                        pe.matmul(sums(t), pick[:, h, t, :], rows[:, t, :], start=True, stop=True).then_inc(seg_done, 1)
                        if mlp and t == 2:
                            pe.wait_ge(in_xn[h], 16 * (i + 1))
                            pe.wait_ge(xT2_copied, n + X_CREDIT)
                            for c in range(DC):
                                last = pe.transpose(ps_xT[:, c * P:(c + 1) * P], xn[:, h, c * P:(c + 1) * P], k.ident[:, :])
                            last.then_inc(xT2_done, 1)
                        if mlp and t == 5:
                            pe.wait_ge(xT2_copied, n + 1 + X_CREDIT)
                            pe.wait_ge(gelu_done, DC * n + GELU_CREDIT)
                            for f in range(DC):
                                for c in range(DC):
                                    last = pe.matmul(ps_h[:, f * P:(f + 1) * P], k.mix_w[:, c, f * P:(f + 1) * P],
                                                     xT[:, c, :], start=(c == 0), stop=(c == DC - 1))
                            last.then_inc(h_done, 1)
                        if mlp and t == 9:
                            pe.wait_ge(gelu_done, DC * n + DC + GELU_CREDIT)
                            pe.wait_ge(part_done, n + PART_CREDIT)
                            for f in range(DC):
                                last = pe.matmul(ps_o[:, 0:D], hT[:, f, :], k.mix_w2[:, f, :],
                                                 start=(f == 0), stop=(f == DC - 1))
                            last.then_inc(o_done, 1)

                for start, end, mlp in loops:
                    with pe.Fori(start, end) as i:
                        for h in range(2):
                            step(i, h, mlp)


def head(k):
    nc, A = k.nc, k.A
    STAGES = 4
    PEELED = STAGES
    with ExitStack() as ctx:
        sb = lambda name, shape, dt=F32: k.sb(name, shape, dt, ctx)
        part = sb("part3", [P, 2, D])
        h7 = sb("h7", [P, 2, D])
        hT = sb("h7T", [P, DC, 2 * P])
        rT = sb("rT", [P, DC, 2 * P])
        stats = sb("stats3", [P, 2, 6])
        mv = sb("mv3", [P, 2, 2])
        std = sb("std3", [P, 2])
        rstd = sb("rstd3", [P, 2])
        xl = sb("xl", [P, 2, D])
        fT = sb("fT", [P, DC, 2 * P])
        wr = sb("wr", [P, DC, N_EXPERTS])
        br = sb("br", [P, N_EXPERTS])
        eps2 = sb("eps2", [P, 1])
        ps_T, ps_h, ps_o, ps_f, ps_l = (k.ps(f"ps3_{n}", [P, 512], ctx) for n in "T h o f l".split())
        in_part, rows_out, consts_in = k.sem("part_in"), k.sem("rows_out"), k.sem("consts_in")
        (eps2_made, h7_done, h7T_done, h7T_copied, hid_done, relu_done, gout_done, x1_done, stats_done, mv_done, std_done,
         rstd_done, xl_done, f_done, fT_copied, lg_done, lgb_done, held) = (
            k.sem("head_" + name) for name in (
                "eps2_made h7_done h7T_done h7T_copied hid_done relu_done gout_done x1_done stats_done mv_done std_done "
                "rstd_done xl_done f_done fT_copied lg_done lgb_done held").split())
        by_block = lambda a: a.rearrange("(t p) d -> p t d", p=P)
        halves = lambda bank: bank[:, :].rearrange("p (c n) -> p c n", c=2)
        both = range(2)

        def trips(eng, body):
            for i in range(PEELED):
                body(i, [s for s in range(STAGES) if i >= s])
            with eng.Fori(PEELED, PAIRS) as i:
                body(i, range(STAGES))
            for i in range(PAIRS, PAIRS + STAGES - 1):
                body(i, [s for s in range(STAGES) if i - s < PAIRS])

        with nc.Block() as block:
            @block.sync
            def _(sp):
                sp.dma_start(part[:, :, :], by_block(k.part_dram)[:, 0:2, :]).then_inc(in_part, 16)

                def body(i, stages):
                    if 2 in stages:
                        j = i - 2
                        sp.wait_ge(xl_done, 2 * j + 2)
                        sp.dma_start(by_block(k.ffn_rows)[:, bass.ds(2 * j, 2), :], xl[:, :, :]).then_inc(rows_out, 16)
                    if 1 in stages:
                        j = i - 1
                        sp.wait_ge(x1_done, j + 1)
                        sp.dma_start(part[:, :, :], by_block(k.part_dram)[:, bass.ds(2 * j + 2, 2), :]).then_inc(in_part, 16)

                trips(sp, body)
                sp.wait_ge(in_part, 16 * (PAIRS + 1))
                sp.wait_ge(rows_out, 16 * PAIRS)

            @block.scalar
            def _(act):
                with nc.allow_non_contiguous_dma(reason="columns of a few hundred words"):
                    for t, (dst, b) in enumerate(((k.gb[:, 0, :], A["gamma"]), (k.gb[:, 1, :], A["beta"]))):
                        act.dma_start(dst, b.rearrange("(c p) -> p c", p=P)).then_inc(consts_in, 16)
                act.dma_start(wr[:, :, :], A["Wr"].rearrange("(c p) e -> p c e", p=P)).then_inc(consts_in, 16)
                act.dma_start(br[:, :], A["br"].partition_broadcast(P)).then_inc(consts_in, 16)
                for e in range(N_EXPERTS):
                    up, b1, down, b2 = k.expert_parts(k.up_all[:, e, :], k.down_all[:, e, :])
                    act.dma_start(up, A["W1"][e].rearrange("(c p) n -> p c n", p=P)).then_inc(k.weights_in, 16)
                    act.dma_start(down, A["W2"][e].rearrange("(c p) n -> p c n", p=P)).then_inc(k.weights_in, 16)
                    act.dma_start(b2, A["b2"][e].partition_broadcast(P)).then_inc(k.weights_in, 16)
                    with nc.allow_non_contiguous_dma(reason="an expert's first bias, features on partitions"):
                        act.dma_start(b1, A["b1"][e].rearrange("(c p) -> p c", p=P)).then_inc(k.weights_in, 16)
                act.wait_ge(consts_in, 64)
                act.wait_ge(eps2_made, 1)

                def body(i, stages):
                    if 0 in stages:
                        start_after(act, h7T_done, i)
                        for h in both:
                            act.activation(h7[:, h:h + 1, :], k.acc[:, bass.ds(2 * i + h, 1), :], ACT.Copy,
                                           scale=k.dinv[:, bass.ds(2 * i + h, 1)]).then_inc(h7_done, 1)
                    if 1 in stages:
                        j = i - 1
                        act.wait_ge(hid_done, j + 1)
                        start_after(act, gout_done, j)
                        for f in range(DC):
                            act.activation(rT[:, f, :], halves(ps_h)[:, f, :], ACT.Relu,
                                           bias=k.gcn_c[:, f:f + 1]).then_inc(relu_done, 1)
                    if 2 in stages:
                        j = i - 2
                        act.wait_ge(mv_done, 2 * j + 2)
                        start_after(act, rstd_done, j)
                        act.activation(std[:, :], mv[:, :, 1], ACT.Sqrt, bias=eps2[:, :], scale=1.0 + EPS).then_inc(std_done, 1)
                    if 3 in stages:
                        j = i - 3
                        act.wait_ge(f_done, j + 1)
                        start_after(act, lg_done, j)
                        for c in range(DC):
                            act.activation(fT[:, c, :], halves(ps_f)[:, c, :], ACT.Identity, scale=k.gb[:, 0, c:c + 1],
                                           bias=k.gb[:, 1, c:c + 1]).then_inc(fT_copied, 1)
                    if 0 in stages:
                        act.wait_ge(h7T_done, i + 1)
                        start_after(act, hid_done, i)
                        act.activation(hT[:, :, :], halves(ps_T), ACT.Copy).then_inc(h7T_copied, 1)

                trips(act, body)

            @block.vector
            def _(dve):
                dve.memset(eps2[:, :], EPS * EPS).then_inc(eps2_made, 1)
                dve.wait_ge(consts_in, 64)

                def body(i, stages):
                    if 2 in stages:
                        j = i - 2
                        dve.wait_ge(x1_done, j + 1)
                        dve.sem_inc(held, 1)
                        for h in both:
                            dve.bn_stats(stats[:, h, :], k.acc[:, bass.ds(2 * j + h, 1), :][:, 0, :]).then_inc(stats_done, 1)
                        dve.wait_ge(stats_done, 2 * j + 2)
                        dve.sem_inc(held, 1)
                        for h in both:
                            dve.bn_aggr(mv[:, h, :], stats[:, h, :]).then_inc(mv_done, 1)
                        dve.wait_ge(std_done, j + 1)
                        dve.reciprocal(rstd[:, :], std[:, :]).then_inc(rstd_done, 1)
                        start_after(dve, rows_out, 16 * j)
                        start_after(dve, f_done, j)
                        dve.wait_ge(rstd_done, j + 1)
                        for h in both:
                            dve.tensor_scalar(xl[:, h:h + 1, :], k.acc[:, bass.ds(2 * j + h, 1), :], mv[:, h, 0:1],
                                              rstd[:, h:h + 1], ALU.subtract, ALU.mult).then_inc(xl_done, 1)
                    if 3 in stages:
                        j = i - 3
                        dve.wait_ge(lg_done, j + 1)
                        dve.tensor_tensor(k.logits[:, bass.ds(2 * j, 2), :],
                                          ps_l[:, 0:2 * N_EXPERTS].rearrange("p (h e) -> p h e", h=2),
                                          br[:, :].unsqueeze(1).to_broadcast([P, 2, N_EXPERTS]), ALU.add).then_inc(lgb_done, 1)
                    if 1 in stages:
                        j = i - 1
                        dve.wait_ge(gout_done, j + 1)
                        dve.wait_ge(in_part, 16 * (j + 1))
                        dve.tensor_tensor(k.acc[:, bass.ds(2 * j, 2), :], halves(ps_o), part[:, :, :], ALU.add).then_inc(x1_done, 1)

                trips(dve, body)

            @block.tensor
            def _(pe):
                pe.wait_ge(consts_in, 64)

                def turn(bank, rows):
                    for c in range(DC):
                        for h in both:
                            last = pe.transpose(halves(bank)[:, c, h * P:(h + 1) * P], rows[:, h, c * P:(c + 1) * P], k.ident[:, :])
                    return last

                def body(i, stages):
                    if 1 in stages:
                        j = i - 1
                        pe.wait_ge(h7T_copied, j + 1)
                        start_after(pe, relu_done, DC * j)
                        for f in range(DC):
                            for c in range(DC):
                                last = pe.matmul(halves(ps_h)[:, f, :], k.gcn_w[:, c, f * P:(f + 1) * P],
                                                 hT[:, c, :], start=(c == 0), stop=(c == DC - 1))
                        last.then_inc(hid_done, 1)
                    if 3 in stages:
                        j = i - 3
                        pe.wait_ge(xl_done, 2 * j + 2)
                        start_after(pe, fT_copied, DC * j)
                        turn(ps_f, xl).then_inc(f_done, 1)
                    if 0 in stages:
                        pe.wait_ge(h7_done, 2 * i + 2)
                        start_after(pe, h7T_copied, i)
                        turn(ps_T, h7).then_inc(h7T_done, 1)
                    if 1 in stages:
                        j = i - 1
                        pe.wait_ge(relu_done, DC * j + DC)
                        start_after(pe, x1_done, j)
                        for h in both:
                            for f in range(DC):
                                last = pe.matmul(halves(ps_o)[:, h, :], rT[:, f, h * P:(h + 1) * P], k.gcn_w2[:, f, :],
                                                 start=(f == 0), stop=(f == DC - 1))
                        last.then_inc(gout_done, 1)
                    if 3 in stages:
                        j = i - 3
                        pe.wait_ge(fT_copied, DC * j + DC)
                        start_after(pe, lgb_done, j)
                        for h in both:
                            for c in range(DC):
                                last = pe.matmul(ps_l[:, h * N_EXPERTS:(h + 1) * N_EXPERTS], fT[:, c, h * P:(h + 1) * P],
                                                 wr[:, c, :], start=(c == 0), stop=(c == DC - 1))
                        last.then_inc(lg_done, 1)

                trips(pe, body)


def route(k):
    nc = k.nc
    with ExitStack() as ctx:
        sb = lambda name, shape, dt=F32: k.sb(name, shape, dt, ctx)
        rev = sb("rev", [P, N_EXPERTS])
        best = sb("best", [P, TOP, BLOCKS])
        first = sb("first", [P, BLOCKS])
        score = sb("score", [P, BLOCKS, N_EXPERTS])
        hit = sb("hit", [P, GROUPS, TOP, HALF])
        gap = sb("gap", [P, BLOCKS])
        e2, den = gap, first
        tri = sb("tri4", [P, P])
        flat = lambda t: t.rearrange("p e i -> p (e i)")
        hit_flat = hit[:, :, :, :].rearrange("p e j b -> p (e j b)")
        SLOT = HALVES * TOP
        LANES_BY_ACT = [f * TOP for f in range(HALVES)]
        LANES_BY_DVE = [slot for slot in range(SLOT) if slot not in LANES_BY_ACT]
        size = GROUPS * TOP * HALF
        keep, count = (k.arena[:, n * size:(n + 1) * size].rearrange("p (e i) -> p e i", e=GROUPS) for n in range(2))
        rest = k.arena[:, 2 * size:]
        place, tile_no = rest[:, 0:TOP * BLOCKS], rest[:, TOP * BLOCKS:TOP * BLOCKS + X_TILES + X_UNROLL]
        total_i = sb("total4_i", [P, GROUPS], I32)
        tiles_i = sb("tiles4_i", [P, GROUPS], I32)
        tiles = sb("tiles4", [P, GROUPS])
        tile_end = sb("tile4_end", [P, GROUPS])
        tile_start = sb("tile4_start", [P, GROUPS])
        base = sb("base4", [P, GROUPS])
        lane_i = place.bitcast(I32)
        tile_i = sb("tile4", [P, TOP * BLOCKS], I32)
        tile_no_i = sb("tile_no_i", [P, X_TILES + X_UNROLL], I32)
        tile_e = sb("tile_e", [P, X_TILES + X_UNROLL])
        word = sb("word4", [P, X_TRIPS])
        row_id = sb("row_id", [P, BLOCKS], I32)
        spare = flat(keep)
        lane, tile, ident_no = (spare[:, n * 256:n * 256 + w] for n, w in enumerate((TOP * BLOCKS, TOP * BLOCKS, BLOCKS)))
        zeros = spare[:, 768:768 + X_TILES]
        minus_lane = spare[:, 1024:1024 + TOP * BLOCKS]
        distance = spare[:, 1280:1280 + HALVES * P].rearrange("p (m n) -> p m n", m=HALVES)
        at_lane = hit_flat[:, 0:SLOT * P].rearrange("p (s n) -> p s n", s=SLOT)
        at_tile = hit_flat[:, SLOT * P:SLOT * (P + X_TILES)].rearrange("p (s n) -> p s n", s=SLOT)
        ps_n = k.ps("ps4_n", [P, 512], ctx)
        ps_id = k.ps("ps4_id", [P, 512], ctx)
        (step, gap_done, e2_done, tri_made, made, counted, prefix_done, routed, lane_made, tile_made, placed,
         all_placed, zeros_made, lanes_ready, distance_made, act_made) = (
            k.sem("route_" + name) for name in (
                "step gap_done e2_done tri_made made counted prefix_done routed lane_made tile_made placed "
                "all_placed zeros_made lanes_ready distance_made act_made").split())
        shape = [P, BLOCKS, N_EXPERTS]
        per_row = lambda t: t.unsqueeze(2).to_broadcast(shape)
        of_half = lambda t, f: t[:, f * HALF:(f + 1) * HALF, :]
        by_row = lambda f, j: hit[:, f * N_EXPERTS:(f + 1) * N_EXPERTS, j, :].rearrange("p e b -> p b e")
        by_group = lambda t: t[:, :].unsqueeze(2).to_broadcast([P, GROUPS, TOP * HALF])
        SPANS = ((0, HALF_TILES), (HALF * TOP, X_TILES))
        hits = hit[:, :, :, :].rearrange("p e j b -> p e (j b)")
        logits = k.logits[:, :, :]
        LOWEST = -3.0e38
        with nc.Block() as block:
            @block.scalar
            def _(act):
                act.wait_ge(gap_done, 1)
                act.activation(e2[:, :], gap[:, :], ACT.Exp).then_inc(e2_done, 1)
                act.wait_ge(lanes_ready, 1)
                with act.Fori(0, HALF_CHUNKS) as c:
                    for i in (CHUNK * c + b for b in range(CHUNK)):
                        for m, slot in enumerate(LANES_BY_ACT):
                            f, j = divmod(slot, TOP)
                            act.activation(distance[:, m, :], k.iota_row[:, :], ACT.Abs,
                                           bias=minus_lane[:, bass.ds(f * TOP * HALF + j * HALF + i, 1)]).then_inc(distance_made, 1)
                        for m, slot in enumerate(LANES_BY_ACT):
                            act.wait_ge(placed, SLOT * i + slot + 1)
                            act.wait_ge(distance_made, len(LANES_BY_ACT) * i + m + 1)
                            act.activation(at_lane[:, slot, :], distance[:, m, :], ACT.Relu, scale=-1.0,
                                           bias=k.ones[:, 0:1]).then_inc(act_made, 1)
                        act.wait_ge(act_made, len(LANES_BY_ACT) * (i + 1))

            @block.gpsimd
            def _(pool):
                pool.memset(tri[:, :], 1.0).then_inc(tri_made, 1)
                pool.memset(keep[:, :, 1:], 1.0).then_inc(made, 1)
                pool.memset(keep[:, :, 0:1], 0.0).then_inc(made, 1)
                pool.iota(tile_no_i[:, :], pattern=[[1, X_TILES + X_UNROLL]], base=0, channel_multiplier=0).then_inc(made, 1)
                pool.iota(row_id[:, :], pattern=[[P, BLOCKS]], base=0, channel_multiplier=1).then_inc(made, 1)
                pool.wait_ge(tri_made, 1)
                pool.affine_select(out=tri[:, :], in_=tri[:, :], compare_op=ALU.is_gt, fill=0.0,
                                   base=0, pattern=[[1, P]], channel_multiplier=-1).then_inc(made, 1)

            @block.vector
            def _(dve):
                steps = [0]

                def after_last(op):
                    op.then_inc(step, 1)
                    steps[0] += 1
                    dve.wait_ge(step, steps[0])

                after_last(dve.tensor_scalar(rev[:, :], k.iota_row[:, 0:N_EXPERTS], -1.0, float(N_EXPERTS), ALU.mult, ALU.add))
                rev_all = rev[:, :].unsqueeze(1).to_broadcast(shape)
                for j in range(TOP):
                    after_last(dve.tensor_reduce(best[:, j, :], logits, AX.X, ALU.max))
                    after_last(dve.tensor_tensor(score[:, :, :], logits, per_row(best[:, j, :]), ALU.is_equal))
                    after_last(dve.tensor_tensor(score[:, :, :], score[:, :, :], rev_all, ALU.mult))
                    after_last(dve.tensor_reduce(first[:, :], score[:, :, :], AX.X, ALU.max))
                    for f in range(HALVES):
                        after_last(dve.tensor_tensor(by_row(f, j), of_half(rev_all, f), of_half(per_row(first[:, :]), f), ALU.is_equal))
                        if j + 1 < TOP:
                            after_last(dve.scalar_tensor_tensor(out=of_half(logits, f), in0=by_row(f, j), scalar=LOWEST,
                                                                in1=of_half(logits, f), op0=ALU.mult, op1=ALU.add))
                dve.tensor_tensor(gap[:, :], best[:, 1, :], best[:, 0, :], ALU.subtract).then_inc(gap_done, 1)
                dve.wait_ge(made, 5)
                dve.tensor_tensor_scan(flat(count[:, :, :]), flat(keep[:, :, :]), flat(hits), 0.0, ALU.mult,
                                       ALU.add).then_inc(counted, 1)
                dve.wait_ge(e2_done, 1)
                after_last(dve.tensor_scalar(den[:, :], e2[:, :], 1.0, None, ALU.add))
                after_last(dve.reciprocal(k.gate_w[:, 0, :], den[:, :]))
                after_last(dve.tensor_tensor(k.gate_w[:, 1, :], k.gate_w[:, 0, :], e2[:, :], ALU.mult))
                dve.wait_ge(prefix_done, 1)
                after_last(dve.tensor_scalar(total_i[:, :], ps_n[:, GROUPS:2 * GROUPS], float(P - 1), None, ALU.add))
                after_last(dve.tensor_scalar(tiles_i[:, :], total_i[:, :], 7, None, ALU.arith_shift_right))
                after_last(dve.tensor_copy(tiles[:, :], tiles_i[:, :]))
                after_last(dve.tensor_tensor_scan(tile_end[:, :], k.ones[:, 0:GROUPS], tiles[:, :], 0.0, ALU.mult, ALU.add))
                after_last(dve.tensor_tensor(tile_start[:, :], tile_end[:, :], tiles[:, :], ALU.subtract))
                after_last(dve.scalar_tensor_tensor(out=base[:, :], in0=tile_start[:, :], scalar=float(P),
                                                    in1=ps_n[:, 0:GROUPS], op0=ALU.mult, op1=ALU.add))
                after_last(dve.tensor_tensor(count[:, :, :], count[:, :, :], by_group(base), ALU.add))
                after_last(dve.tensor_tensor(count[:, :, :], count[:, :, :], hits, ALU.mult))
                for f in range(HALVES):
                    after_last(dve.tensor_reduce(place[:, f * TOP * HALF:(f + 1) * TOP * HALF],
                                                 count[:, f * N_EXPERTS:(f + 1) * N_EXPERTS, :].rearrange("p e i -> p i e"),
                                                 AX.X, ALU.add))
                pos = k.pos[:, :, :, :].rearrange("p f j b -> p (f j b)")
                after_last(dve.tensor_scalar(pos, place, -1.0, None, ALU.add))
                dve.tensor_scalar(lane_i, pos, P - 1, None, ALU.bitwise_and).then_inc(routed, 1)
                dve.tensor_scalar(tile_i[:, :], pos, 7, None, ALU.logical_shift_right).then_inc(routed, 1)
                dve.tensor_copy(ident_no, row_id[:, :]).then_inc(routed, 1)
                dve.tensor_copy(tile_no, tile_no_i[:, :]).then_inc(routed, 1)
                dve.memset(zeros, 0.0).then_inc(zeros_made, 1)
                dve.wait_ge(routed, 4)
                after_last(dve.tensor_copy(lane, lane_i))
                dve.tensor_scalar(minus_lane, lane, -1.0, None, ALU.mult).then_inc(lanes_ready, 1)
                after_last(dve.tensor_copy(tile, tile_i[:, :]))
                with dve.Fori(0, HALF_CHUNKS) as c:
                    for i in (CHUNK * c + b for b in range(CHUNK)):
                        for f in range(HALVES):
                            number = ident_no[:, bass.ds(f * HALF + i, 1)]
                            for j in range(TOP):
                                slot = f * TOP + j
                                n = f * TOP * HALF + j * HALF + i
                                dve.wait_ge(placed, SLOT * i + slot + 1)
                                start, end = SPANS[f]
                                if slot in LANES_BY_ACT:
                                    dve.tensor_scalar(at_tile[:, slot, 0:end - start], tile_no[:, start:end], tile[:, bass.ds(n, 1)],
                                                      number, ALU.is_equal, ALU.mult).then_inc(tile_made, 1)
                                else:
                                    dve.tensor_scalar(at_lane[:, slot, :], k.iota_row[:, :], lane[:, bass.ds(n, 1)],
                                                      number, ALU.is_equal, ALU.mult).then_inc(lane_made, 1)
                                    dve.tensor_scalar(at_tile[:, slot, 0:end - start], tile_no[:, start:end], tile[:, bass.ds(n, 1)],
                                                      None, ALU.is_equal).then_inc(tile_made, 1)
                dve.memset(k.ids[:, X_TILES:], 0).then_inc(routed, 1)
                dve.wait_ge(all_placed, 1)
                after_last(dve.tensor_copy(k.ids[:, 0:X_TILES], ps_id[:, 0:X_TILES]))
                after_last(dve.tensor_scalar(tile_e[:, :], tile_no, tile_start[:, 1:2], None, ALU.is_ge))
                for e in range(2, GROUPS):
                    after_last(dve.scalar_tensor_tensor(out=tile_e[:, :], in0=tile_no, scalar=tile_start[:, e:e + 1],
                                                        in1=tile_e[:, :], op0=ALU.is_ge, op1=ALU.add))
                of = lambda u: tile_e[:, u:u + X_TILES].rearrange("p (i u) -> p i u", u=X_UNROLL)[:, :, 0]
                after_last(dve.tensor_copy(word[:, :], of(0)))
                for u in range(1, X_UNROLL + 1):
                    after_last(dve.scalar_tensor_tensor(out=word[:, :], in0=of(u), scalar=float(GROUPS ** u),
                                                        in1=word[:, :], op0=ALU.mult, op1=ALU.add))
                after_last(dve.tensor_copy(k.expert_words[:, :], word[:, :]))

            @block.tensor
            def _(pe):
                pe.wait_ge(counted, 1)
                pe.wait_ge(made, 5)
                last = count[:, :, TOP * HALF - 1]
                pe.matmul(ps_n[:, 0:GROUPS], tri[:, :], last, start=True, stop=True)
                pe.matmul(ps_n[:, GROUPS:2 * GROUPS], k.ones[:, :], last, start=True, stop=True).then_inc(prefix_done, 1)
                pe.wait_ge(zeros_made, 1)
                ids = ps_id[:, 0:X_TILES]
                pe.matmul(ids, zeros[:, 0:P], zeros, start=True, stop=False, skip_group_check=True)
                pe.sem_inc(placed, SLOT)
                by_act = len(LANES_BY_ACT)
                with pe.Fori(0, HALF_CHUNKS) as c:
                    for i in (CHUNK * c + b for b in range(CHUNK)):
                        for slot in range(SLOT):
                            start, end = SPANS[slot // TOP]
                            if slot in LANES_BY_ACT:
                                pe.wait_ge(act_made, by_act * i + LANES_BY_ACT.index(slot) + 1)
                            else:
                                pe.wait_ge(lane_made, (SLOT - by_act) * i + LANES_BY_DVE.index(slot) + 1)
                            pe.wait_ge(tile_made, SLOT * i + slot + 1)
                            pe.matmul(ids[:, start:end], at_lane[:, slot, :], at_tile[:, slot, 0:end - start], start=False,
                                      stop=False, skip_group_check=True).then_inc(placed, 1)
                pe.matmul(ids, zeros[:, 0:P], zeros, start=False, stop=True, skip_group_check=True).then_inc(all_placed, 1)


def experts(k):
    nc, A = k.nc, k.A
    with ExitStack() as ctx:
        sb = lambda name, shape, dt=F32: k.sb(name, shape, dt, ctx)
        spans = iter(range(0, k.arena.shape[1], D))

        def room(slots, columns):
            taken = [next(spans) for _ in range(slots * columns // D)]
            return k.arena[:, taken[0]:taken[0] + slots * columns].rearrange("p (s n) -> p s n", s=slots)

        xrow = room(X_UNROLL, D)
        xT = room(2, DC * P)
        hT = room(2, HC * P)
        y = room(2, D)
        back = room(TOP, D)
        up_now = sb("up_now", [P, 2, UP])
        down_now = sb("down_now", [P, 2, DOWN])
        ids = k.ids
        idx = sb("idx5", [P, X_UNROLL], I32)
        back_idx = sb("back_idx", [P, TOP], I32)
        ps_x = [k.ps(f"ps5_x{j}", [P, 512], ctx) for j in range(2)]
        ps_h = [k.ps(f"ps5_h{j}", [P, 512], ctx) for j in range(2)]
        ps_y = [k.ps(f"ps5_y{j}", [P, 512], ctx) for j in range(2)]
        (idx_done, x_done, xT_copied, up_copied, down_copied, hid_done, gelu_done, down_done, y_done,
         held) = (
            k.sem("tile_" + name) for name in (
                "idx_done x_done xT_copied up_copied down_copied hid_done gelu_done down_done y_done "
                "held").split())
        got = [k.sem(f"xrow_in{u}") for u in range(X_UNROLL)]
        y_out = [k.sem(f"y_out{j}") for j in range(2)]
        back_in = [k.sem(f"back_in{j}") for j in range(TOP)]
        back_idx_done, back_added = k.sem("back_idx_done"), k.sem("back_added")
        parts = [k.expert_parts(up_now[:, j, :], down_now[:, j, :]) for j in range(2)]
        N_WEIGHTS = 4 * N_EXPERTS
        GROUP_BITS = GROUPS.bit_length() - 1
        assert 1 << GROUP_BITS == GROUPS

        BACK_FROM = X_TRIPS - (HALF + 1) // 2
        STORED = (HALF_TILES + 1) // 2
        assert 2 * STORED <= (BACK_FROM - 1) * X_UNROLL and X_UNROLL == 2 * TOP

        def trips(eng, body, back=None, before_back=None):
            def beside(c, u, block, tail):
                if back:
                    back(c, u % TOP, block, tail)

            for u in range(X_UNROLL):
                body(u, u, 0)
            with eng.Fori(1, BACK_FROM) as i:
                for u in range(X_UNROLL):
                    body(X_UNROLL * i + u, u, i)
            if before_back:
                before_back()
            with eng.Fori(BACK_FROM, X_TRIPS - 1) as i:
                for u in range(X_UNROLL):
                    body(X_UNROLL * i + u, u, i)
                    beside(X_UNROLL * (i - BACK_FROM) + u, u, 2 * (i - BACK_FROM) + u // TOP, False)
            for u in range(X_UNROLL):
                body(X_TILES - X_UNROLL + u, u, X_TRIPS - 1)
                if u < TOP:
                    beside((HALF - 1) * TOP + u, u, HALF - 1, True)

        with nc.Block() as block:
            @block.sync
            def _(sp):
                def body(t, u, i):
                    sp.wait_ge(y_done, t + 1)
                    sp.dma_start(k.y_rows[bass.ds(t * P, P), :], y[:, u % 2, :]).then_inc(y_out[u % 2], 16)

                trips(sp, body)
                for j in range(2):
                    sp.wait_ge(y_out[j], 16 * X_TILES // 2)

            @block.gpsimd
            def _(pool):
                def body(t, u, i):
                    pool.wait_ge(idx_done, t + 1)
                    pool.sem_inc(held, 1)
                    pool.indirect_dma_start(out=xrow[:, u, :], out_offset=None, in_=k.ffn_rows,
                                            in_offset=bass.IndirectOffsetOnAxis(idx[:, u:u + 1], 0),
                                            bounds_check=NODES - 1, oob_is_err=False).then_inc(got[u], 16)

                def before_back():
                    for j in range(2):
                        pool.wait_ge(y_out[j], 16 * STORED)

                def gather_back(c, j):
                    pool.wait_ge(back_idx_done, c + 1)
                    pool.sem_inc(held, 1)
                    pool.indirect_dma_start(out=back[:, j, :], out_offset=None, in_=k.y_rows[0:HALF_TILES * P, :],
                                            in_offset=bass.IndirectOffsetOnAxis(back_idx[:, j:j + 1], 0),
                                            bounds_check=HALF_TILES * P - 1, oob_is_err=False).then_inc(back_in[j], 16)

                for u in range(X_UNROLL):
                    body(u, u, 0)
                with pool.Fori(1, BACK_FROM) as i:
                    for u in range(X_UNROLL):
                        body(X_UNROLL * i + u, u, i)
                before_back()
                for u in range(X_UNROLL):
                    body(X_UNROLL * BACK_FROM + u, u, BACK_FROM)
                    if u >= TOP:
                        gather_back(u - TOP, u % TOP)
                with pool.Fori(BACK_FROM + 1, X_TRIPS) as i:
                    for u in range(X_UNROLL):
                        body(X_UNROLL * i + u, u, i)
                        gather_back(X_UNROLL * (i - BACK_FROM) + u - TOP, u % TOP)

            @block.scalar
            def _(act):
                def transposed(t, slot):
                    act.wait_ge(x_done, t + 1)
                    start_after(act, hid_done, t - 1)
                    for c in range(DC):
                        act.activation(xT[:, slot, c * P:(c + 1) * P], ps_x[slot][:, c * P:(c + 1) * P], ACT.Identity,
                                       scale=k.gb[:, 0, c:c + 1], bias=k.gb[:, 1, c:c + 1]).then_inc(xT_copied, 1)

                transposed(0, 0)

                def body(t, u, i):
                    slot = u % 2
                    if not (isinstance(t, int) and t + 1 == X_TILES):
                        transposed(t + 1, 1 - slot)
                    act.wait_ge(hid_done, t + 1)
                    start_after(act, down_done, t - 1)
                    for c in range(HC):
                        act.activation(hT[:, slot, c * P:(c + 1) * P], ps_h[slot][:, c * P:(c + 1) * P], ACT.Gelu,
                                       bias=parts[slot][1][:, c:c + 1]).then_inc(gelu_done, 1)

                trips(act, body)

            @block.vector
            def _(dve):
                for u in range(X_UNROLL):
                    dve.tensor_copy(idx[:, u:u + 1], ids[:, u:u + 1]).then_inc(idx_done, 1)
                dve.wait_ge(k.weights_in, 16 * N_WEIGHTS)

                def finish(t, slot, uses):
                    dve.wait_ge(down_done, t + 1)
                    start_after(dve, y_out[slot], 16 * uses)
                    dve.tensor_tensor(y[:, slot, :], ps_y[slot][:, 0:D], parts[slot][3], ALU.add).then_inc(y_done, 1)

                expert = [dve.snap(dve.value_load(k.expert_words[0:1, 0:1]) & (N_EXPERTS - 1))]
                dve.tensor_copy(up_now[:, 0:1, :], k.up_all[:, bass.ds(expert[0], 1), :]).then_inc(up_copied, 1)

                def body(t, u, i):
                    slot = u % 2
                    if u == 0:
                        k.word = dve.value_load(k.expert_words[0:1, bass.ds(i, 1)])
                    e = [dve.snap((k.word >> (GROUP_BITS * v)) & (N_EXPERTS - 1)) for v in (u, u + 1)]
                    start_after(dve, y_done, t - 1)
                    start_after(dve, down_done, t - 1)
                    dve.tensor_copy(down_now[:, slot:slot + 1, :], k.down_all[:, bass.ds(e[0], 1), :]).then_inc(down_copied, 1)
                    start_after(dve, gelu_done, HC * t)
                    dve.tensor_copy(up_now[:, 1 - slot:2 - slot, :], k.up_all[:, bass.ds(e[1], 1), :]).then_inc(up_copied, 1)
                    dve.wait_ge(x_done, t + 1)
                    dve.tensor_copy(idx[:, u:u + 1], ids[:, bass.ds(t + X_UNROLL, 1)]).then_inc(idx_done, 1)
                    if not (isinstance(t, int) and t == 0):
                        finish(t - 1, 1 - slot, 2 * i + (u - 1) // 2 if u > 0 else 2 * i - 1)

                def back_indices(j, block):
                    dve.tensor_copy(back_idx[:, j:j + 1], k.pos[:, 0, j, bass.ds(block, 1)]).then_inc(back_idx_done, 1)

                BACK_CREDIT = 1

                def before_back():
                    dve.sem_inc(back_added, BACK_CREDIT)
                    for j in range(TOP):
                        back_indices(j, 0)

                def add_back(c, j, block, tail):
                    dve.wait_ge(back_in[j], 16 * (block + 1))
                    dve.wait_ge(back_added, c + BACK_CREDIT)
                    here = k.acc[:, bass.ds(block, 1), :]
                    dve.scalar_tensor_tensor(out=here, in0=back[:, j:j + 1, :], scalar=k.gate_w[:, j, bass.ds(block, 1)],
                                             in1=here, op0=ALU.mult, op1=ALU.add).then_inc(back_added, 1)
                    if not tail:
                        back_indices(j, block + 1)

                trips(dve, body, add_back, before_back)
                finish(X_TILES - 1, (X_TILES - 1) % 2, X_TILES // 2 - 1)

            @block.tensor
            def _(pe):
                def turn(t, u, i):
                    pe.wait_ge(got[u], 16 * (i + 1))
                    start_after(pe, xT_copied, DC * (t - 1))
                    for c in range(DC):
                        last = pe.transpose(ps_x[u % 2][:, c * P:(c + 1) * P], xrow[:, u, c * P:(c + 1) * P], k.ident[:, :])
                    last.then_inc(x_done, 1)

                def down(t, slot):
                    pe.wait_ge(gelu_done, HC * t + HC)
                    pe.wait_ge(down_copied, t + 1)
                    start_after(pe, y_done, t - 1)
                    for c in range(HC):
                        last = pe.matmul(ps_y[slot][:, 0:D], hT[:, slot, c * P:(c + 1) * P], parts[slot][2][:, c, :],
                                         start=(c == 0), stop=(c == HC - 1))
                    last.then_inc(down_done, 1)

                turn(0, 0, 0)

                def body(t, u, i):
                    slot = u % 2
                    if not (isinstance(t, int) and t + 1 == X_TILES):
                        turn(t + 1, (u + 1) % X_UNROLL, i + (u + 1) // X_UNROLL)
                    pe.wait_ge(xT_copied, DC * t + DC)
                    pe.wait_ge(up_copied, t + 1)
                    start_after(pe, gelu_done, HC * (t - 1))
                    for c in range(HC):
                        for d in range(DC):
                            last = pe.matmul(ps_h[slot][:, c * P:(c + 1) * P], parts[slot][0][:, d, c * P:(c + 1) * P],
                                             xT[:, slot, d * P:(d + 1) * P], start=(d == 0), stop=(d == DC - 1))
                    last.then_inc(hid_done, 1)
                    if not (isinstance(t, int) and t == 0):
                        down(t - 1, 1 - slot)

                trips(pe, body)
                down(X_TILES - 1, (X_TILES - 1) % 2)


def combine(k):
    nc = k.nc
    with ExitStack() as ctx:
        sb = lambda name, shape, dt=F32: k.sb(name, shape, dt, ctx)
        idx = sb("idx6", [P, 2, TOP, CHUNK], I32)
        rows = sb("rows6", [P, 2, TOP, CHUNK, D])
        got = [k.sem(f"y_in{h}") for h in range(2)]
        idx_done, added, out_done, held = (k.sem("combine_" + n) for n in "idx_done added out_done held".split())
        out_v = k.out.rearrange("(t p) d -> p t d", p=P)
        OPS = TOP * CHUNK

        def chunks(eng, body):
            with eng.Fori(0, HALF_CHUNKS // 2) as turn:
                for h in range(2):
                    body(2 * turn + h, h, turn)
            body(HALF_CHUNKS - 1, 0, HALF_CHUNKS // 2)

        with nc.Block() as block:
            @block.sync
            def _(sp):
                sp.dma_start(out_v[:, 0:HALF, :], k.acc[:, 0:HALF, :]).then_inc(out_done, 16)

                def body(c, h, turn):
                    sp.wait_ge(added, OPS * (c + 1))
                    cut = bass.ds(HALF + c * CHUNK, CHUNK)
                    sp.dma_start(out_v[:, cut, :], k.acc[:, cut, :]).then_inc(out_done, 16)

                chunks(sp, body)
                sp.wait_ge(out_done, 16 * (1 + HALF_CHUNKS))

            @block.gpsimd
            def _(pool):
                def body(c, h, turn):
                    pool.wait_ge(idx_done, c + 1)
                    pool.sem_inc(held, 1)
                    for j in range(TOP):
                        for b in range(CHUNK):
                            pool.indirect_dma_start(
                                out=rows[:, h, j, b, :], out_offset=None, in_=k.y_rows,
                                in_offset=bass.IndirectOffsetOnAxis(idx[:, h, j, b:b + 1], 0),
                                bounds_check=P * X_TILES - 1, oob_is_err=False).then_inc(got[h], 16)

                chunks(pool, body)

            @block.vector
            def _(dve):
                def indices(h, c):
                    dve.tensor_copy(idx[:, h, :, :], k.pos[:, 1, :, bass.ds(c * CHUNK, CHUNK)]).then_inc(idx_done, 1)

                def add(c, h, turn):
                    dve.wait_ge(got[h], 16 * OPS * (turn + 1))
                    for j in range(TOP):
                        if j > 0:
                            dve.wait_ge(added, OPS * c + CHUNK * j)
                        for b in range(CHUNK):
                            n = HALF + c * CHUNK + b
                            here = k.acc[:, bass.ds(n, 1), :]
                            dve.scalar_tensor_tensor(out=here, in0=rows[:, h, j, b:b + 1, :],
                                                     scalar=k.gate_w[:, j, bass.ds(n, 1)], in1=here, op0=ALU.mult,
                                                     op1=ALU.add).then_inc(added, 1)

                def add_and_go_on(c, h, turn):
                    add(c, h, turn)
                    dve.wait_ge(added, OPS * (c + 1))
                    indices(h, c + 2)

                for h in range(2):
                    indices(h, h)
                with dve.Fori(0, HALF_CHUNKS // 2 - 1) as turn:
                    for h in range(2):
                        add_and_go_on(2 * turn + h, h, turn)
                add_and_go_on(HALF_CHUNKS - 3, 0, HALF_CHUNKS // 2 - 1)
                add(HALF_CHUNKS - 2, 1, HALF_CHUNKS // 2 - 1)
                add(HALF_CHUNKS - 1, 0, HALF_CHUNKS // 2)


_NAMES = {
    "gnn_W": "L0_gnn_W", "gnn_b": "L0_gnn_b", "gnn_W1": "L0_gnn_W1", "gnn_b1": "L0_gnn_b1", "gnn_W2": "L0_gnn_W2",
    "gnn_b2": "L0_gnn_b2", "w_qkv": "L0_mix_w_qkv", "b_qkv": "L0_mix_b_qkv", "kln_g": "L0_mix_kln_g",
    "kln_b": "L0_mix_kln_b", "vln_g": "L0_mix_vln_g", "vln_b": "L0_mix_vln_b", "mix_w1": "L0_mix_w1",
    "mix_b1": "L0_mix_b1", "mix_w2": "L0_mix_w2", "mix_b2": "L0_mix_b2", "gamma": "L0_ffn_gamma",
    "beta": "L0_ffn_beta", "Wr": "L0_ffn_Wr", "br": "L0_ffn_br", "W1": "L0_ffn_W1", "b1": "L0_ffn_b1",
    "W2": "L0_ffn_W2", "b2": "L0_ffn_b2",
}


def kernel(**inputs):
    import numpy as np
    import concourse.bacc as bacc
    from concourse.bass_utils import run_bass_kernel_spmd

    def padded(a, n, fill):
        a = np.asarray(a)
        return np.concatenate([a, np.full((n - a.shape[0],) + a.shape[1:], fill, a.dtype)])

    edges = P * EDGE_COLS
    arrays = {
        "x": padded(inputs["x"], NODES + AHEAD * P, 0),
        "src": padded(inputs["src"], edges, NODES).reshape(P, EDGE_COLS),
        "dst": padded(inputs["dst"], edges, 0).reshape(P, EDGE_COLS),
        "ew": padded(inputs["edge_weight"], edges, 0).reshape(P, EDGE_COLS),
    }
    for short, name in _NAMES.items():
        arrays[short] = np.ascontiguousarray(inputs[name])
    nc = bacc.Bacc("TRN2", target_bir_lowering=False, num_devices=1)
    aps = {n: nc.dram_tensor(f"in_{n}", a.shape, mybir.dt.from_np(a.dtype), kind="ExternalInput").ap()
           for n, a in arrays.items()}
    out = nc.dram_tensor("out", [NODES, D], F32, kind="ExternalOutput").ap()
    gps_layer(nc, aps, out)
    r = run_bass_kernel_spmd(nc, [{f"in_{n}": a for n, a in arrays.items()}], core_ids=[0])
    return r.results[0]["out"][:N_NODES]
```
